# Optimizing a Trainium2 kernel written in Bass

```python
import numpy as np
import jax
import jax.numpy as jnp

def _softmax(x, axis=-1):
    return jax.nn.softmax(x, axis=axis)

def _gelu(x):
    return jax.nn.gelu(x, approximate=True)

def _silu(x):
    return jax.nn.silu(x)

def _sigmoid(x):
    return jax.nn.sigmoid(x)

def _layernorm(x, axis=-1, eps=1e-05):
    m = jnp.mean(x, axis=axis, keepdims=True)
    v = jnp.var(x, axis=axis, keepdims=True)
    return (x - m) / jnp.sqrt(v + eps)

def _scatter_add(tgt, idx, src, axis=0):
    return tgt.at[idx].add(src)

def _segment_sum(src, seg, n):
    return jax.ops.segment_sum(src, seg, n)
kernel_name = 'mk_xattn_seq_d4_seqx_r4_f4b385'

def setup_inputs(seed: int=0):
    np.random.seed(seed)
    _w = jnp.asarray

    def _rec_inputs():
        import jax
        import jax.numpy as jnp
        _rk = jax.random.key(seed)
        x = 7.22e-05 + 1 * jax.random.normal(jax.random.fold_in(_rk, 1), (8, 112, 256), jnp.float32)
        _lenS = 112 - jax.random.randint(jax.random.fold_in(_rk, 7), (8,), 0, max(1, 112 // 4) + 1, jnp.int32)
        _lenS2 = 375 - jax.random.randint(jax.random.fold_in(_rk, 8), (8,), 0, max(1, 375 // 4) + 1, jnp.int32)
        _ctx_768P = jax.random.normal(jax.random.fold_in(_rk, 11), (8, 16, 192), jnp.float32)
        _ctx_768c = jax.random.dirichlet(jax.random.fold_in(_rk, 511), 0.3 * jnp.ones((16,), jnp.float32), (8, 375))
        _ctx_768t = jnp.einsum('bsk,bkd->bsd', _ctx_768c, _ctx_768P)
        _ctx_768t = _ctx_768t * jax.lax.rsqrt(jnp.mean(jnp.square(_ctx_768t)) + 1e-12) * 0.953939
        ctx_768 = 0.000651243 + 0.998673 * (_ctx_768t + 0.3 * jax.random.normal(jax.random.fold_in(_rk, 611), (8, 375, 192), jnp.float32))
        _validS = jnp.arange(112)[None, :] < _lenS[:, None]
        _validS2 = jnp.arange(375)[None, :] < _lenS2[:, None]
        _causal = jnp.tril(jnp.ones((112, 112), dtype=bool))
        mask_BxS_bf0 = jnp.logical_not(jnp.ones((8, 112), dtype=bool))
        mask_BxS2_bf0 = jnp.logical_not(jnp.ones((8, 375), dtype=bool))
        return (x, ctx_768, mask_BxS_bf0, mask_BxS2_bf0)
    x, ctx_768, mask_BxS_bf0, mask_BxS2_bf0 = _rec_inputs()

    def _L0_xattn_setup():
        import jax, jax.numpy as jnp
        import numpy as np
        HEADS = 16
        D_HEAD = 64
        EPS = 1e-05

        def _ln(x, g, b):
            m = jnp.mean(x, axis=-1, keepdims=True)
            v = jnp.var(x, axis=-1, keepdims=True)
            return (x - m) * jax.lax.rsqrt(v + EPS) * g + b

        def _attn(xq, xc, Wq, Wk, Wv, Wo, bo):
            B, N, _ = xq.shape
            S = xc.shape[1]
            q = (xq @ Wq).reshape(B, N, HEADS, D_HEAD)
            k = (xc @ Wk).reshape(B, S, HEADS, D_HEAD)
            v = (xc @ Wv).reshape(B, S, HEADS, D_HEAD)
            scale = D_HEAD ** (-0.5)
            scores = jnp.einsum('bnhd,bshd->bhns', q, k) * scale
            attn = jax.nn.softmax(scores, axis=-1)
            out = jnp.einsum('bhns,bshd->bnhd', attn, v).reshape(B, N, HEADS * D_HEAD)
            return out @ Wo + bo

        def _geglu_ff(x, Wp, bp, Wf, bf):
            h = x @ Wp + bp
            a, gate = jnp.split(h, 2, axis=-1)
            return a * jax.nn.gelu(gate, approximate=False) @ Wf + bf
        key = jax.random.key(seed)
        ks = jax.random.split(key, 16)
        dim, ctx, inner, ffin = (256, 192, HEADS * D_HEAD, 4 * 256)

        def w(k, i, o):
            return jax.random.normal(k, (i, o), jnp.float32) * i ** (-0.5)
        inp = {'x': jax.random.normal(ks[0], (4, 512, dim), jnp.float32), 'context': jax.random.normal(ks[1], (4, 77, ctx), jnp.float32), 'Wq1': w(ks[2], dim, inner), 'Wk1': w(ks[3], dim, inner), 'Wv1': w(ks[4], dim, inner), 'Wo1': w(ks[5], inner, dim), 'bo1': jnp.zeros((dim,), jnp.float32), 'Wq2': w(ks[6], dim, inner), 'Wk2': w(ks[7], ctx, inner), 'Wv2': w(ks[8], ctx, inner), 'Wo2': w(ks[9], inner, dim), 'bo2': jnp.zeros((dim,), jnp.float32), 'Wp': w(ks[10], dim, 2 * ffin), 'bp': jnp.zeros((2 * ffin,), jnp.float32), 'Wf': w(ks[11], ffin, dim), 'bf': jnp.zeros((dim,), jnp.float32), 'g1': jnp.ones((dim,), jnp.float32), 'b1': jnp.zeros((dim,), jnp.float32), 'g2': jnp.ones((dim,), jnp.float32), 'b2': jnp.zeros((dim,), jnp.float32), 'g3': jnp.ones((dim,), jnp.float32), 'b3': jnp.zeros((dim,), jnp.float32)}
        return inp
    _L0_xattn_all = _L0_xattn_setup()
    _L0_xattn_in = {k: v for k, v in _L0_xattn_all.items() if k in ('Wq1', 'Wk1', 'Wv1', 'Wo1', 'bo1', 'Wq2', 'Wk2', 'Wv2', 'Wo2', 'bo2', 'Wp', 'bp', 'Wf', 'bf', 'g1', 'b1', 'g2', 'b2', 'g3', 'b3')}
    del _L0_xattn_all

    def _L1_xattn_setup():
        import jax, jax.numpy as jnp
        import numpy as np
        DIM = 256
        HEADS = 16
        D_HEAD = 64
        INNER = HEADS * D_HEAD
        CTX_DIM = 192
        FF_INNER = 4 * DIM
        EPS = 1e-05
        SCALE = D_HEAD ** (-0.5)

        def _layer_norm(x, g, b):
            m = jnp.mean(x, axis=-1, keepdims=True)
            v = jnp.mean(jnp.square(x - m), axis=-1, keepdims=True)
            return (x - m) * jax.lax.rsqrt(v + EPS) * g + b

        def _attention(x, ctx, wq, wk, wv, wo, bo):
            B, S, _ = x.shape
            T = ctx.shape[1]
            q = (x @ wq).reshape(B, S, HEADS, D_HEAD).transpose(0, 2, 1, 3)
            k = (ctx @ wk).reshape(B, T, HEADS, D_HEAD).transpose(0, 2, 1, 3)
            v = (ctx @ wv).reshape(B, T, HEADS, D_HEAD).transpose(0, 2, 1, 3)
            attn = jnp.einsum('bhid,bhjd->bhij', q, k) * SCALE
            attn = jax.nn.softmax(attn, axis=-1)
            out = jnp.einsum('bhij,bhjd->bhid', attn, v)
            out = out.transpose(0, 2, 1, 3).reshape(B, S, INNER)
            return out @ wo + bo
        key = jax.random.key(seed)
        ks = jax.random.split(key, 20)
        rn = lambda k, shape, s=0.02: jax.random.normal(k, shape, dtype=jnp.float32) * s
        inp = {'hidden_states': jax.random.normal(ks[0], (4, 512, DIM), dtype=jnp.float32), 'context': jax.random.normal(ks[1], (4, 77, CTX_DIM), dtype=jnp.float32), 'wq1': rn(ks[2], (DIM, INNER)), 'wk1': rn(ks[3], (DIM, INNER)), 'wv1': rn(ks[4], (DIM, INNER)), 'wo1': rn(ks[5], (INNER, DIM)), 'bo1': jnp.zeros((DIM,), jnp.float32), 'wq2': rn(ks[6], (DIM, INNER)), 'wk2': rn(ks[7], (CTX_DIM, INNER)), 'wv2': rn(ks[8], (CTX_DIM, INNER)), 'wo2': rn(ks[9], (INNER, DIM)), 'bo2': jnp.zeros((DIM,), jnp.float32), 'w_ff1': rn(ks[10], (DIM, 2 * FF_INNER)), 'b_ff1': jnp.zeros((2 * FF_INNER,), jnp.float32), 'w_ff2': rn(ks[11], (FF_INNER, DIM)), 'b_ff2': jnp.zeros((DIM,), jnp.float32), 'ln1_g': jnp.ones((DIM,), jnp.float32), 'ln1_b': jnp.zeros((DIM,), jnp.float32), 'ln2_g': jnp.ones((DIM,), jnp.float32), 'ln2_b': jnp.zeros((DIM,), jnp.float32), 'ln3_g': jnp.ones((DIM,), jnp.float32), 'ln3_b': jnp.zeros((DIM,), jnp.float32)}
        return inp
    _L1_xattn_all = _L1_xattn_setup()
    _L1_xattn_in = {k: v for k, v in _L1_xattn_all.items() if k in ('wq1', 'wk1', 'wv1', 'wo1', 'bo1', 'wq2', 'wk2', 'wv2', 'wo2', 'bo2', 'w_ff1', 'b_ff1', 'w_ff2', 'b_ff2', 'ln1_g', 'ln1_b', 'ln2_g', 'ln2_b', 'ln3_g', 'ln3_b')}
    del _L1_xattn_all

    def _L2_xattn_setup():
        import jax, jax.numpy as jnp
        import numpy as np
        D_Q, D_CTX, N_HEADS, HEAD_DIM = (256, 192, 16, 64)
        INNER = N_HEADS * HEAD_DIM
        EPS = 1e-05

        def _layernorm(x, gamma, beta):
            mu = jnp.mean(x, axis=-1, keepdims=True)
            var = jnp.var(x, axis=-1, keepdims=True)
            return (x - mu) * jax.lax.rsqrt(var + EPS) * gamma + beta
        key = jax.random.key(seed)
        ks = jax.random.split(key, 8)
        B, NQ, NC = (4, 256, 256)
        s_q = 1.0 / np.sqrt(D_Q)
        s_c = 1.0 / np.sqrt(D_CTX)
        s_i = 1.0 / np.sqrt(INNER)
        return {'x': jax.random.normal(ks[0], (B, NQ, D_Q), jnp.float32), 'context': jax.random.normal(ks[1], (B, NC, D_CTX), jnp.float32), 'Wq': jax.random.normal(ks[2], (D_Q, INNER), jnp.float32) * s_q, 'Wk': jax.random.normal(ks[3], (D_CTX, INNER), jnp.float32) * s_c, 'Wv': jax.random.normal(ks[4], (D_CTX, INNER), jnp.float32) * s_c, 'Wo': jax.random.normal(ks[5], (INNER, D_Q), jnp.float32) * s_i, 'bo': jnp.zeros((D_Q,), jnp.float32), 'gamma': jnp.ones((D_Q,), jnp.float32), 'beta': jnp.zeros((D_Q,), jnp.float32)}
    _L2_xattn_all = _L2_xattn_setup()
    _L2_xattn_in = {k: v for k, v in _L2_xattn_all.items() if k in ('Wq', 'Wk', 'Wv', 'Wo', 'bo', 'gamma', 'beta')}
    del _L2_xattn_all

    def _L3_xattn_setup():
        import jax, jax.numpy as jnp
        import numpy as np
        D_DEC, D_ENC, H, D_MLP = (256, 192, 16, 1024)
        HD = D_DEC // H

        def _layernorm(x, w, b, eps=1e-05):
            m = x.mean(-1, keepdims=True)
            v = ((x - m) ** 2).mean(-1, keepdims=True)
            return (x - m) / jnp.sqrt(v + eps) * w + b

        def _decoder_block(x, enc, tgt_mask, enc_mask, ln1_w, ln1_b, qkv_w, qkv_b, proj_w, proj_b, ln2_w, ln2_b, q_w, q_b, k_w, k_b, v_w, v_b, out_w, out_b, ln3_w, ln3_b, mlp1_w, mlp1_b, mlp2_w, mlp2_b):
            B, T, C = x.shape
            S = enc.shape[1]
            scale = HD ** (-0.5)
            neg = jnp.asarray(-jnp.inf, x.dtype)
            h = _layernorm(x, ln1_w, ln1_b)
            qkv = (h @ qkv_w + qkv_b).reshape(B, T, 3, H, HD)
            q, k, v = [qkv[:, :, i].transpose(0, 2, 1, 3) for i in range(3)]
            attn = jnp.einsum('bhtd,bhsd->bhts', q, k) * scale
            causal = jnp.triu(jnp.ones((T, T), bool), 1)
            attn = jnp.where(causal[None, None], neg, attn)
            attn = jnp.where(tgt_mask[:, None, None, :], neg, attn)
            attn = jax.nn.softmax(attn, axis=-1)
            sa = jnp.einsum('bhts,bhsd->bhtd', attn, v).transpose(0, 2, 1, 3).reshape(B, T, C)
            x = x + sa @ proj_w + proj_b
            h = _layernorm(x, ln2_w, ln2_b)
            q = (h @ q_w + q_b).reshape(B, T, H, HD).transpose(0, 2, 1, 3)
            k = (enc @ k_w + k_b).reshape(B, S, H, HD).transpose(0, 2, 1, 3)
            v = (enc @ v_w + v_b).reshape(B, S, H, HD).transpose(0, 2, 1, 3)
            attn = jnp.einsum('bhtd,bhsd->bhts', q, k) * scale
            attn = jnp.where(enc_mask[:, None, None, :], neg, attn)
            attn = jax.nn.softmax(attn, axis=-1)
            ca = jnp.einsum('bhts,bhsd->bhtd', attn, v).transpose(0, 2, 1, 3).reshape(B, T, C)
            x = x + ca @ out_w + out_b
            h = _layernorm(x, ln3_w, ln3_b)
            h = jax.nn.gelu(h @ mlp1_w + mlp1_b, approximate=False)
            x = x + h @ mlp2_w + mlp2_b
            return x
        key = jax.random.key(seed)
        ks = jax.random.split(key, 16)
        B, T, S = (4, 256, 144)

        def lin(k, din, dout):
            kw, kb = jax.random.split(k)
            bound = 1.0 / np.sqrt(din)
            W = jax.random.uniform(kw, (din, dout), jnp.float32, -bound, bound)
            b = jax.random.uniform(kb, (dout,), jnp.float32, -bound, bound)
            return (W, b)
        qkv_w, qkv_b = lin(ks[0], D_DEC, 3 * D_DEC)
        proj_w, proj_b = lin(ks[1], D_DEC, D_DEC)
        q_w, q_b = lin(ks[2], D_DEC, D_DEC)
        k_w, k_b = lin(ks[3], D_ENC, D_DEC)
        v_w, v_b = lin(ks[4], D_ENC, D_DEC)
        out_w, out_b = lin(ks[5], D_DEC, D_DEC)
        mlp1_w, mlp1_b = lin(ks[6], D_DEC, D_MLP)
        mlp2_w, mlp2_b = lin(ks[7], D_MLP, D_DEC)
        return {'x': jax.random.normal(ks[8], (B, T, D_DEC), jnp.float32), 'enc': jax.random.normal(ks[9], (B, S, D_ENC), jnp.float32), 'tgt_key_padding_mask': jnp.zeros((B, T), bool), 'enc_padding_mask': jnp.zeros((B, S), bool), 'ln1_w': jnp.ones((D_DEC,)), 'ln1_b': jnp.zeros((D_DEC,)), 'qkv_w': qkv_w, 'qkv_b': qkv_b, 'proj_w': proj_w, 'proj_b': proj_b, 'ln2_w': jnp.ones((D_DEC,)), 'ln2_b': jnp.zeros((D_DEC,)), 'q_w': q_w, 'q_b': q_b, 'k_w': k_w, 'k_b': k_b, 'v_w': v_w, 'v_b': v_b, 'out_w': out_w, 'out_b': out_b, 'ln3_w': jnp.ones((D_DEC,)), 'ln3_b': jnp.zeros((D_DEC,)), 'mlp1_w': mlp1_w, 'mlp1_b': mlp1_b, 'mlp2_w': mlp2_w, 'mlp2_b': mlp2_b}
    _L3_xattn_all = _L3_xattn_setup()
    _L3_xattn_in = {k: v for k, v in _L3_xattn_all.items() if k in ('ln1_w', 'ln1_b', 'qkv_w', 'qkv_b', 'proj_w', 'proj_b', 'ln2_w', 'ln2_b', 'q_w', 'q_b', 'k_w', 'k_b', 'v_w', 'v_b', 'out_w', 'out_b', 'ln3_w', 'ln3_b', 'mlp1_w', 'mlp1_b', 'mlp2_w', 'mlp2_b')}
    del _L3_xattn_all
    return {'x': x, 'ctx_768': ctx_768, 'mask_BxS_bf0': mask_BxS_bf0, 'mask_BxS2_bf0': mask_BxS2_bf0, 'L0_xattn_Wq1': _L0_xattn_in['Wq1'], 'L0_xattn_Wk1': _L0_xattn_in['Wk1'], 'L0_xattn_Wv1': _L0_xattn_in['Wv1'], 'L0_xattn_Wo1': _L0_xattn_in['Wo1'], 'L0_xattn_bo1': _L0_xattn_in['bo1'], 'L0_xattn_Wq2': _L0_xattn_in['Wq2'], 'L0_xattn_Wk2': _L0_xattn_in['Wk2'], 'L0_xattn_Wv2': _L0_xattn_in['Wv2'], 'L0_xattn_Wo2': _L0_xattn_in['Wo2'], 'L0_xattn_bo2': _L0_xattn_in['bo2'], 'L0_xattn_Wp': _L0_xattn_in['Wp'], 'L0_xattn_bp': _L0_xattn_in['bp'], 'L0_xattn_Wf': _L0_xattn_in['Wf'], 'L0_xattn_bf': _L0_xattn_in['bf'], 'L0_xattn_g1': _L0_xattn_in['g1'], 'L0_xattn_b1': _L0_xattn_in['b1'], 'L0_xattn_g2': _L0_xattn_in['g2'], 'L0_xattn_b2': _L0_xattn_in['b2'], 'L0_xattn_g3': _L0_xattn_in['g3'], 'L0_xattn_b3': _L0_xattn_in['b3'], 'L1_xattn_wq1': _L1_xattn_in['wq1'], 'L1_xattn_wk1': _L1_xattn_in['wk1'], 'L1_xattn_wv1': _L1_xattn_in['wv1'], 'L1_xattn_wo1': _L1_xattn_in['wo1'], 'L1_xattn_bo1': _L1_xattn_in['bo1'], 'L1_xattn_wq2': _L1_xattn_in['wq2'], 'L1_xattn_wk2': _L1_xattn_in['wk2'], 'L1_xattn_wv2': _L1_xattn_in['wv2'], 'L1_xattn_wo2': _L1_xattn_in['wo2'], 'L1_xattn_bo2': _L1_xattn_in['bo2'], 'L1_xattn_w_ff1': _L1_xattn_in['w_ff1'], 'L1_xattn_b_ff1': _L1_xattn_in['b_ff1'], 'L1_xattn_w_ff2': _L1_xattn_in['w_ff2'], 'L1_xattn_b_ff2': _L1_xattn_in['b_ff2'], 'L1_xattn_ln1_g': _L1_xattn_in['ln1_g'], 'L1_xattn_ln1_b': _L1_xattn_in['ln1_b'], 'L1_xattn_ln2_g': _L1_xattn_in['ln2_g'], 'L1_xattn_ln2_b': _L1_xattn_in['ln2_b'], 'L1_xattn_ln3_g': _L1_xattn_in['ln3_g'], 'L1_xattn_ln3_b': _L1_xattn_in['ln3_b'], 'L2_xattn_Wq': _L2_xattn_in['Wq'], 'L2_xattn_Wk': _L2_xattn_in['Wk'], 'L2_xattn_Wv': _L2_xattn_in['Wv'], 'L2_xattn_Wo': _L2_xattn_in['Wo'], 'L2_xattn_bo': _L2_xattn_in['bo'], 'L2_xattn_gamma': _L2_xattn_in['gamma'], 'L2_xattn_beta': _L2_xattn_in['beta'], 'L3_xattn_ln1_w': _L3_xattn_in['ln1_w'], 'L3_xattn_ln1_b': _L3_xattn_in['ln1_b'], 'L3_xattn_qkv_w': _L3_xattn_in['qkv_w'], 'L3_xattn_qkv_b': _L3_xattn_in['qkv_b'], 'L3_xattn_proj_w': _L3_xattn_in['proj_w'], 'L3_xattn_proj_b': _L3_xattn_in['proj_b'], 'L3_xattn_ln2_w': _L3_xattn_in['ln2_w'], 'L3_xattn_ln2_b': _L3_xattn_in['ln2_b'], 'L3_xattn_q_w': _L3_xattn_in['q_w'], 'L3_xattn_q_b': _L3_xattn_in['q_b'], 'L3_xattn_k_w': _L3_xattn_in['k_w'], 'L3_xattn_k_b': _L3_xattn_in['k_b'], 'L3_xattn_v_w': _L3_xattn_in['v_w'], 'L3_xattn_v_b': _L3_xattn_in['v_b'], 'L3_xattn_out_w': _L3_xattn_in['out_w'], 'L3_xattn_out_b': _L3_xattn_in['out_b'], 'L3_xattn_ln3_w': _L3_xattn_in['ln3_w'], 'L3_xattn_ln3_b': _L3_xattn_in['ln3_b'], 'L3_xattn_mlp1_w': _L3_xattn_in['mlp1_w'], 'L3_xattn_mlp1_b': _L3_xattn_in['mlp1_b'], 'L3_xattn_mlp2_w': _L3_xattn_in['mlp2_w'], 'L3_xattn_mlp2_b': _L3_xattn_in['mlp2_b']}

def reference(x, ctx_768, mask_BxS_bf0, mask_BxS2_bf0, L0_xattn_Wq1, L0_xattn_Wk1, L0_xattn_Wv1, L0_xattn_Wo1, L0_xattn_bo1, L0_xattn_Wq2, L0_xattn_Wk2, L0_xattn_Wv2, L0_xattn_Wo2, L0_xattn_bo2, L0_xattn_Wp, L0_xattn_bp, L0_xattn_Wf, L0_xattn_bf, L0_xattn_g1, L0_xattn_b1, L0_xattn_g2, L0_xattn_b2, L0_xattn_g3, L0_xattn_b3, L1_xattn_wq1, L1_xattn_wk1, L1_xattn_wv1, L1_xattn_wo1, L1_xattn_bo1, L1_xattn_wq2, L1_xattn_wk2, L1_xattn_wv2, L1_xattn_wo2, L1_xattn_bo2, L1_xattn_w_ff1, L1_xattn_b_ff1, L1_xattn_w_ff2, L1_xattn_b_ff2, L1_xattn_ln1_g, L1_xattn_ln1_b, L1_xattn_ln2_g, L1_xattn_ln2_b, L1_xattn_ln3_g, L1_xattn_ln3_b, L2_xattn_Wq, L2_xattn_Wk, L2_xattn_Wv, L2_xattn_Wo, L2_xattn_bo, L2_xattn_gamma, L2_xattn_beta, L3_xattn_ln1_w, L3_xattn_ln1_b, L3_xattn_qkv_w, L3_xattn_qkv_b, L3_xattn_proj_w, L3_xattn_proj_b, L3_xattn_ln2_w, L3_xattn_ln2_b, L3_xattn_q_w, L3_xattn_q_b, L3_xattn_k_w, L3_xattn_k_b, L3_xattn_v_w, L3_xattn_v_b, L3_xattn_out_w, L3_xattn_out_b, L3_xattn_ln3_w, L3_xattn_ln3_b, L3_xattn_mlp1_w, L3_xattn_mlp1_b, L3_xattn_mlp2_w, L3_xattn_mlp2_b):
    import jax
    import jax.numpy as jnp

    def _L0_xattn_ref(x, context, Wq1, Wk1, Wv1, Wo1, bo1, Wq2, Wk2, Wv2, Wo2, bo2, Wp, bp, Wf, bf, g1, b1, g2, b2, g3, b3):
        import jax, jax.numpy as jnp
        import numpy as np
        HEADS = 16
        D_HEAD = 64
        EPS = 1e-05

        def _ln(x, g, b):
            m = jnp.mean(x, axis=-1, keepdims=True)
            v = jnp.var(x, axis=-1, keepdims=True)
            return (x - m) * jax.lax.rsqrt(v + EPS) * g + b

        def _attn(xq, xc, Wq, Wk, Wv, Wo, bo):
            B, N, _ = xq.shape
            S = xc.shape[1]
            q = (xq @ Wq).reshape(B, N, HEADS, D_HEAD)
            k = (xc @ Wk).reshape(B, S, HEADS, D_HEAD)
            v = (xc @ Wv).reshape(B, S, HEADS, D_HEAD)
            scale = D_HEAD ** (-0.5)
            scores = jnp.einsum('bnhd,bshd->bhns', q, k) * scale
            attn = jax.nn.softmax(scores, axis=-1)
            out = jnp.einsum('bhns,bshd->bnhd', attn, v).reshape(B, N, HEADS * D_HEAD)
            return out @ Wo + bo

        def _geglu_ff(x, Wp, bp, Wf, bf):
            h = x @ Wp + bp
            a, gate = jnp.split(h, 2, axis=-1)
            return a * jax.nn.gelu(gate, approximate=False) @ Wf + bf
        x = _attn(_ln(x, g1, b1), _ln(x, g1, b1), Wq1, Wk1, Wv1, Wo1, bo1) + x
        x = _attn(_ln(x, g2, b2), context, Wq2, Wk2, Wv2, Wo2, bo2) + x
        x = _geglu_ff(_ln(x, g3, b3), Wp, bp, Wf, bf) + x
        return x

    def _L1_xattn_ref(hidden_states, context, wq1, wk1, wv1, wo1, bo1, wq2, wk2, wv2, wo2, bo2, w_ff1, b_ff1, w_ff2, b_ff2, ln1_g, ln1_b, ln2_g, ln2_b, ln3_g, ln3_b):
        import jax, jax.numpy as jnp
        import numpy as np
        DIM = 256
        HEADS = 16
        D_HEAD = 64
        INNER = HEADS * D_HEAD
        CTX_DIM = 192
        FF_INNER = 4 * DIM
        EPS = 1e-05
        SCALE = D_HEAD ** (-0.5)

        def _layer_norm(x, g, b):
            m = jnp.mean(x, axis=-1, keepdims=True)
            v = jnp.mean(jnp.square(x - m), axis=-1, keepdims=True)
            return (x - m) * jax.lax.rsqrt(v + EPS) * g + b

        def _attention(x, ctx, wq, wk, wv, wo, bo):
            B, S, _ = x.shape
            T = ctx.shape[1]
            q = (x @ wq).reshape(B, S, HEADS, D_HEAD).transpose(0, 2, 1, 3)
            k = (ctx @ wk).reshape(B, T, HEADS, D_HEAD).transpose(0, 2, 1, 3)
            v = (ctx @ wv).reshape(B, T, HEADS, D_HEAD).transpose(0, 2, 1, 3)
            attn = jnp.einsum('bhid,bhjd->bhij', q, k) * SCALE
            attn = jax.nn.softmax(attn, axis=-1)
            out = jnp.einsum('bhij,bhjd->bhid', attn, v)
            out = out.transpose(0, 2, 1, 3).reshape(B, S, INNER)
            return out @ wo + bo
        h = hidden_states
        h = h + _attention(_layer_norm(h, ln1_g, ln1_b), _layer_norm(h, ln1_g, ln1_b), wq1, wk1, wv1, wo1, bo1)
        h = h + _attention(_layer_norm(h, ln2_g, ln2_b), context, wq2, wk2, wv2, wo2, bo2)
        x = _layer_norm(h, ln3_g, ln3_b) @ w_ff1 + b_ff1
        lin, gate = jnp.split(x, 2, axis=2)
        h = h + lin * jax.nn.gelu(gate) @ w_ff2 + b_ff2
        return h

    def _L2_xattn_ref(x, context, Wq, Wk, Wv, Wo, bo, gamma, beta):
        import jax, jax.numpy as jnp
        import numpy as np
        D_Q, D_CTX, N_HEADS, HEAD_DIM = (256, 192, 16, 64)
        INNER = N_HEADS * HEAD_DIM
        EPS = 1e-05

        def _layernorm(x, gamma, beta):
            mu = jnp.mean(x, axis=-1, keepdims=True)
            var = jnp.var(x, axis=-1, keepdims=True)
            return (x - mu) * jax.lax.rsqrt(var + EPS) * gamma + beta
        scale = HEAD_DIM ** (-0.5)
        h = _layernorm(x, gamma, beta)
        B, NQ, _ = x.shape
        NC = context.shape[1]
        Q = (h @ Wq).reshape(B, NQ, N_HEADS, HEAD_DIM)
        K = (context @ Wk).reshape(B, NC, N_HEADS, HEAD_DIM)
        V = (context @ Wv).reshape(B, NC, N_HEADS, HEAD_DIM)
        attn = jnp.einsum('bihd,bjhd->bhij', Q, K)
        attn = jax.nn.softmax(attn, axis=-1) * scale
        vals = jnp.einsum('bhij,bjhd->bihd', attn, V).reshape(B, NQ, INNER)
        out = vals @ Wo + bo
        return x + out

    def _L3_xattn_ref(x, enc, tgt_key_padding_mask, enc_padding_mask, ln1_w, ln1_b, qkv_w, qkv_b, proj_w, proj_b, ln2_w, ln2_b, q_w, q_b, k_w, k_b, v_w, v_b, out_w, out_b, ln3_w, ln3_b, mlp1_w, mlp1_b, mlp2_w, mlp2_b):
        import jax, jax.numpy as jnp
        import numpy as np
        D_DEC, D_ENC, H, D_MLP = (256, 192, 16, 1024)
        HD = D_DEC // H

        def _layernorm(x, w, b, eps=1e-05):
            m = x.mean(-1, keepdims=True)
            v = ((x - m) ** 2).mean(-1, keepdims=True)
            return (x - m) / jnp.sqrt(v + eps) * w + b

        def _decoder_block(x, enc, tgt_mask, enc_mask, ln1_w, ln1_b, qkv_w, qkv_b, proj_w, proj_b, ln2_w, ln2_b, q_w, q_b, k_w, k_b, v_w, v_b, out_w, out_b, ln3_w, ln3_b, mlp1_w, mlp1_b, mlp2_w, mlp2_b):
            B, T, C = x.shape
            S = enc.shape[1]
            scale = HD ** (-0.5)
            neg = jnp.asarray(-jnp.inf, x.dtype)
            h = _layernorm(x, ln1_w, ln1_b)
            qkv = (h @ qkv_w + qkv_b).reshape(B, T, 3, H, HD)
            q, k, v = [qkv[:, :, i].transpose(0, 2, 1, 3) for i in range(3)]
            attn = jnp.einsum('bhtd,bhsd->bhts', q, k) * scale
            causal = jnp.triu(jnp.ones((T, T), bool), 1)
            attn = jnp.where(causal[None, None], neg, attn)
            attn = jnp.where(tgt_mask[:, None, None, :], neg, attn)
            attn = jax.nn.softmax(attn, axis=-1)
            sa = jnp.einsum('bhts,bhsd->bhtd', attn, v).transpose(0, 2, 1, 3).reshape(B, T, C)
            x = x + sa @ proj_w + proj_b
            h = _layernorm(x, ln2_w, ln2_b)
            q = (h @ q_w + q_b).reshape(B, T, H, HD).transpose(0, 2, 1, 3)
            k = (enc @ k_w + k_b).reshape(B, S, H, HD).transpose(0, 2, 1, 3)
            v = (enc @ v_w + v_b).reshape(B, S, H, HD).transpose(0, 2, 1, 3)
            attn = jnp.einsum('bhtd,bhsd->bhts', q, k) * scale
            attn = jnp.where(enc_mask[:, None, None, :], neg, attn)
            attn = jax.nn.softmax(attn, axis=-1)
            ca = jnp.einsum('bhts,bhsd->bhtd', attn, v).transpose(0, 2, 1, 3).reshape(B, T, C)
            x = x + ca @ out_w + out_b
            h = _layernorm(x, ln3_w, ln3_b)
            h = jax.nn.gelu(h @ mlp1_w + mlp1_b, approximate=False)
            x = x + h @ mlp2_w + mlp2_b
            return x
        return _decoder_block(x, enc, tgt_key_padding_mask, enc_padding_mask, ln1_w, ln1_b, qkv_w, qkv_b, proj_w, proj_b, ln2_w, ln2_b, q_w, q_b, k_w, k_b, v_w, v_b, out_w, out_b, ln3_w, ln3_b, mlp1_w, mlp1_b, mlp2_w, mlp2_b)
    x = _L0_xattn_ref(x, ctx_768, L0_xattn_Wq1, L0_xattn_Wk1, L0_xattn_Wv1, L0_xattn_Wo1, L0_xattn_bo1, L0_xattn_Wq2, L0_xattn_Wk2, L0_xattn_Wv2, L0_xattn_Wo2, L0_xattn_bo2, L0_xattn_Wp, L0_xattn_bp, L0_xattn_Wf, L0_xattn_bf, L0_xattn_g1, L0_xattn_b1, L0_xattn_g2, L0_xattn_b2, L0_xattn_g3, L0_xattn_b3)
    x = _L1_xattn_ref(x, ctx_768, L1_xattn_wq1, L1_xattn_wk1, L1_xattn_wv1, L1_xattn_wo1, L1_xattn_bo1, L1_xattn_wq2, L1_xattn_wk2, L1_xattn_wv2, L1_xattn_wo2, L1_xattn_bo2, L1_xattn_w_ff1, L1_xattn_b_ff1, L1_xattn_w_ff2, L1_xattn_b_ff2, L1_xattn_ln1_g, L1_xattn_ln1_b, L1_xattn_ln2_g, L1_xattn_ln2_b, L1_xattn_ln3_g, L1_xattn_ln3_b)
    x = _L2_xattn_ref(x, ctx_768, L2_xattn_Wq, L2_xattn_Wk, L2_xattn_Wv, L2_xattn_Wo, L2_xattn_bo, L2_xattn_gamma, L2_xattn_beta)
    x = _L3_xattn_ref(x, ctx_768, mask_BxS_bf0, mask_BxS2_bf0, L3_xattn_ln1_w, L3_xattn_ln1_b, L3_xattn_qkv_w, L3_xattn_qkv_b, L3_xattn_proj_w, L3_xattn_proj_b, L3_xattn_ln2_w, L3_xattn_ln2_b, L3_xattn_q_w, L3_xattn_q_b, L3_xattn_k_w, L3_xattn_k_b, L3_xattn_v_w, L3_xattn_v_b, L3_xattn_out_w, L3_xattn_out_b, L3_xattn_ln3_w, L3_xattn_ln3_b, L3_xattn_mlp1_w, L3_xattn_mlp1_b, L3_xattn_mlp2_w, L3_xattn_mlp2_b)
    return x

_drawn_inputs = setup_inputs


def setup_inputs(seed=0):
    import zlib

    import numpy as np

    out = dict(_drawn_inputs(seed))
    spreads = {'L0_xattn_bo1': (0.0, 0.1),
     'L0_xattn_bo2': (0.0, 0.1),
     'L0_xattn_bp': (0.0, 0.1),
     'L0_xattn_bf': (0.0, 0.1),
     'L0_xattn_g1': (1.0, 0.2),
     'L0_xattn_b1': (0.0, 0.1),
     'L0_xattn_g2': (1.0, 0.2),
     'L0_xattn_b2': (0.0, 0.424),
     'L0_xattn_g3': (1.0, 0.2),
     'L0_xattn_b3': (0.0, 0.1),
     'L1_xattn_bo1': (0.0, 0.1),
     'L1_xattn_bo2': (0.0, 0.1),
     'L1_xattn_b_ff1': (0.0, 0.724),
     'L1_xattn_b_ff2': (0.0, 0.1),
     'L1_xattn_ln1_g': (1.0, 0.6),
     'L1_xattn_ln1_b': (0.0, 0.538),
     'L1_xattn_ln2_g': (1.0, 0.6),
     'L1_xattn_ln2_b': (0.0, 0.8),
     'L1_xattn_ln3_g': (1.0, 0.6),
     'L1_xattn_ln3_b': (0.0, 0.8),
     'L2_xattn_bo': (0.0, 0.1),
     'L2_xattn_gamma': (1.0, 0.2),
     'L2_xattn_beta': (0.0, 0.46),
     'L3_xattn_ln1_w': (1.0, 0.6),
     'L3_xattn_ln1_b': (0.0, 0.39),
     'L3_xattn_ln2_w': (1.0, 0.6),
     'L3_xattn_ln2_b': (0.0, 0.8),
     'L3_xattn_ln3_w': (1.0, 0.593),
     'L3_xattn_ln3_b': (0.0, 0.522)}
    factors = {'L1_xattn_wq1': 8.0,
     'L1_xattn_wk1': 8.0,
     'L1_xattn_wq2': 8.0,
     'L1_xattn_wk2': 8.0,
     'L3_xattn_qkv_b': 4.446,
     'L3_xattn_q_w': 3.806,
     'L3_xattn_q_b': 8.0,
     'L3_xattn_k_w': 3.829,
     'L3_xattn_k_b': 64.0,
     'L3_xattn_v_b': 3.355,
     'L3_xattn_mlp1_b': 6.104,
     'L3_xattn_mlp2_b': 4.551,
     'L3_xattn_out_b': 2.714}
    for name, (base, spread) in spreads.items():
        noise = np.random.default_rng([zlib.crc32(name.encode()), seed]).standard_normal(out[name].shape)
        drawn = base * np.exp(spread * noise) if base else spread * noise
        out[name] = jnp.asarray(drawn.astype(out[name].dtype))
    for name, factor in factors.items():
        out[name] = (out[name] * factor).astype(out[name].dtype)
    return out
```

```python
from collections import namedtuple
from contextlib import ExitStack

import numpy as np

import concourse.bass as bass
from concourse import mybir

B, T, C = 8, 112, 256
S2, E = 375, 192
SP = S2 + 1
KM = S2 // 3
H = 16
PAIR = 2 * T
NPAIR = B // 2
CHUNK = 4 * T
EPS = 1e-5
MASKED = -1e38
LAG_T, LAG_A = 2, 3
NP_, WQ = 4, 512

Stage = namedtuple("Stage", "i self_ small ln res q k v o items loop_items end_items qscale escale nscale")


def make_stages():
    W = 1024
    L0s = dict(i=0, self_=True, small=False, ln=0, res=0, q=(0, 0, W), k=(1, 0, W), v=(2, 0, W), o=(3, 0, C),
               loop_items=((5, 4), (6, 5)), end_items=((4, 0), (7, 1)), qscale=0.125, escale=1.0, nscale=1.0)
    L0c = dict(i=1, self_=False, small=False, ln=1, res=1, q=(0, 0, W), k=(4, 0, W), v=(5, 0, W), o=(1, 0, C),
               loop_items=((8, 2), (9, 3)), end_items=((10, 0),), qscale=0.125, escale=1.0, nscale=1.0)
    L1s = dict(i=2, self_=True, small=False, ln=3, res=3, q=(4, 0, W), k=(5, 0, W), v=(1, 0, W), o=(2, 0, C),
               loop_items=((16, 0), (17, 3)), end_items=((15, 4), (18, 5)), qscale=0.125, escale=1.0, nscale=1.0)
    L1c = dict(i=3, self_=False, small=False, ln=4, res=4, q=(4, 0, W), k=(0, 0, W), v=(3, 0, W), o=(5, 0, C),
               loop_items=((19, 1), (20, 2)), end_items=((21, 4),), qscale=0.125, escale=1.0, nscale=1.0)
    L2c = dict(i=4, self_=False, small=False, ln=6, res=6, q=(0, 0, W), k=(3, 0, W), v=(5, 0, W), o=(1, 0, C),
               loop_items=((26, 2), (27, 4)), end_items=(), qscale=1.0, escale=1.0, nscale=0.125)
    L3s = dict(i=5, self_=True, small=True, ln=7, res=7, q=(2, 0, W), k=(2, 512, W), v=(4, 0, 512), o=(4, 1024, C),
               loop_items=((29, 3), (28, 0)), end_items=(), qscale=1.0, escale=0.25, nscale=1.0)
    L3c = dict(i=6, self_=False, small=True, ln=8, res=8, q=(0, 0, 512), k=(3, 0, 512), v=(3, 1024, 512),
               o=(0, 1024, C), loop_items=((30, 5), (31, 1)), end_items=(), qscale=1.0, escale=0.25, nscale=1.0)
    return [Stage(items=None, **s) for s in (L0s, L0c, L1s, L1c, L2c, L3s, L3c)]


FF = namedtuple("FF", "value gate out ln res bias act early late")
FFS = {
    1: FF(2, 3, 0, 2, 2, 0, "erf", ((11, 4), (12, 5), (13, 1)), (14, 2)),
    3: FF(1, 2, 4, 5, 5, 16, "tanh", ((22, 0), (23, 3), (24, 5)), (25, 1)),
    6: FF(None, 5, 1, 9, 9, 32, "erf", (), None),
}
FIRST_ITEMS = ((0, 0), (1, 1), (2, 2), (3, 3))
N_LN = 10

Ev = namedtuple("Ev", "kind st a b par batch n seg prev", defaults=(None,) * 7)


def affine(c0, c1=0):
    return (c0, c1)


def at(c, p, plus=0):
    return c[0] + plus + c[1] * p if c[1] else c[0] + plus


DONE_KINDS = {"q": "q_lo", "k": "k_lo", "v": "v_ready", "wo": "x_ready", "ff2": "x_ready", "lnt": "hT_ready",
              "ffg": "gelu_ready", "ffa": "hid_ready"}


class Shape:

    def __init__(self, st):
        self.G = 4 if st.self_ else 1
        self.NU = H // self.G
        self.HPT = 4 if st.small else 2
        self.NT = H // self.HPT
        self.M = 32 if st.small else 64
        self.keys = T if st.self_ else S2
        self.KT = 1 if st.self_ else 3
        self.krows = T if st.self_ else KM
        self.VH = H * self.M // 512
        self.NV = self.VH * self.KT
        self.NO = 1 if st.small else 2


def build_schedule():
    stages = make_stages()
    shapes = [Shape(s) for s in stages]
    base = {"u": [0], "k": [0], "q": [0], "v": [0], "a": [0], "m": [0]}
    for s, sh in zip(stages, shapes):
        base["u"].append(base["u"][-1] + B * sh.NU)
        base["k"].append(base["k"][-1] + sh.NT * (NPAIR if s.self_ else B))
        base["q"].append(base["q"][-1] + sh.NT * NPAIR)
        base["v"].append(base["v"][-1] + sh.NV * B)
        base["a"].append(base["a"][-1] + sh.NO * B)
        base["m"].append(base["m"][-1] + (B if s.small else 0))

    def kv_pieces(st, tb, tp, with_k, with_q):
        sh = shapes[st.i]
        qs = [Ev("q", st, a=t, batch=tp) for t in range(sh.NT)] if with_q else []
        ks = [Ev("k", st, a=t, batch=tp if st.self_ else tb) for t in range(sh.NT)] if with_k else []
        vs = [Ev("v", st, a=hf, b=m, batch=tb) for hf in range(sh.VH) for m in range(sh.KT)]
        return qs, ks, vs

    def batch_events(st, par, nxt, first_of_loop=False, last=False):
        sh = shapes[st.i]
        me = affine(par, 2)
        steps = sh.NU + LAG_A
        fill = [[] for _ in range(steps)]
        tail = []
        head = []
        if nxt == "same":
            tb = affine(par + 1, 2)
            tp = affine(1, 1)
            new_pair = par == 1
            qs, ks, vs = kv_pieces(st, tb, tp, (not st.self_) or new_pair, new_pair)
            head.append(Ev("src", st, batch=tb))
            if st.self_:
                if new_pair:
                    for t in range(sh.NT):
                        u = t * sh.HPT // sh.G
                        s = min(u + 1 + (t % (sh.NT // 4)) // 2, steps - 1)
                        fill[s] += [qs[t], ks[t]]
                fill[2] += vs
            else:
                span = sh.NU // sh.NT
                for t in range(sh.NT):
                    fill[span * t + span].append(ks[t])
                    if new_pair:
                        fill[span * t + span + 1].append(qs[t])
                half = vs if sh.VH == 1 else vs[:sh.KT]
                if sh.VH == 1:
                    tail += vs
                else:
                    for m, e in enumerate(half):
                        fill[11 + 2 * m].append(e)
                    tail += vs[sh.KT:]
        elif nxt:
            head.append(Ev("src", nxt[0].st, batch=affine(0)))
            tail += nxt
        ev = head + ([Ev("mask", st)] if st.small else [])
        for j in range(steps):
            if j < sh.NU:
                ev.append(Ev("scores", st, a=j))
            if 1 <= j <= sh.NU:
                ev.append(Ev("norm", st, a=j - 1))
            if j == 1 and par == 0:
                ev += [Ev("w", st, a=i, b=s, batch=affine(0, 1)) for i, s in st.loop_items]
            if j == 3 and last and par == 0:
                ev += [Ev("w", st, a=i, b=s, batch=affine(c)) for i, s in st.end_items for c in range(4)]
            ev += fill[j]
            if 0 <= j - LAG_T < sh.NU:
                ev.append(Ev("trans", st, a=j - LAG_T))
            if 0 <= j - LAG_A < sh.NU:
                u = j - LAG_A
                ev.append(Ev("av", st, a=u))
                per = sh.NU // sh.NO
                if u % per == per - 1:
                    ev.append(Ev("ao", st, a=u // per))
        t1, t2 = (2, 1) if nxt == "same" else (4, 4)
        ev += tail[:t1]
        ev.append(Ev("wo", st, a=st.res, b=st.res < N_LN - 1))
        ev += tail[t1:t1 + t2]
        if st.res < N_LN - 1:
            ev.append(Ev("lnt", st, a=st.res + 1))
        ev += tail[t1 + t2:]
        if st.i == 0:
            ev.append(Ev("ctx", st))
        return [e._replace(par=par, batch=e.batch if e.batch is not None else me) for e in ev]

    segments = []

    def prologue(st):
        qs, ks, vs = kv_pieces(st, affine(0), affine(0), True, True)
        zero = [Ev("zero", st, batch=affine(0))] if st.small and st.self_ else []
        return zero + [e for pair in zip(qs, ks) for e in pair] + vs

    segs = []
    first = [Ev("w", stages[0], a=i, b=s, batch=affine(c)) for i, s in FIRST_ITEMS[:2] for c in range(4)]
    for b in range(B):
        first.append(Ev("ln0", stages[0], a=0, par=b % 2, batch=affine(b)))
        first.append(Ev("lnt", stages[0], a=0, par=b % 2, batch=affine(b)))
        if b == 1:
            first += [Ev("w", stages[0], a=i, b=s, batch=affine(c)) for i, s in FIRST_ITEMS[2:] for c in range(4)]
    first.append(Ev("src", stages[0], batch=affine(0)))
    first += prologue(stages[0])
    segs.append((0, 1, first))
    for st in stages:
        body = batch_events(st, 0, "same") + batch_events(st, 1, "same")
        if st.i == 0:
            segs.append((0, 1, body))
            segs.append((1, 3, body))
        else:
            segs.append((0, 3, body))
        direct = st.i not in FFS and st.i + 1 < len(stages)
        follow = prologue(stages[st.i + 1]) if direct and st.self_ else []
        bo_next = [Ev("bo", st, a=st.res + 2, par=0, batch=affine(0))] if st.res + 2 < N_LN else []
        segs.append((3, 4, batch_events(st, 0, "same", last=True) + batch_events(st, 1, follow, last=True) + bo_next))
        ev = []
        if st.i in FFS:
            ff = FFS[st.i]
            for c in range(2):
                for t in range(8):
                    ev.append(Ev("ffg", st, a=t, b=c))
                    if ff.value is not None:
                        ev.append(Ev("ffa", st, a=t, b=c))
                    if c == 0 and ff.early and t < 6:
                        ev += [Ev("w", st, a=i, b=s, batch=affine(q))
                               for i, s in ff.early[t // 2:t // 2 + 1] for q in (2 * (t % 2), 2 * (t % 2) + 1)]
                for j in range(4):
                    b = 4 * c + j
                    ev.append(Ev("ff2", st, a=ff.res, b=j, par=b % 2, batch=affine(b)))
                    if ff.res < N_LN - 1 and j:
                        ev.append(Ev("lnt", st, a=ff.res + 1, par=(b - 1) % 2, batch=affine(b - 1)))
                if ff.res < N_LN - 1:
                    ev.append(Ev("lnt", st, a=ff.res + 1, par=1, batch=affine(4 * c + 3)))
            if ff.res + 2 < N_LN:
                ev.append(Ev("bo", st, a=ff.res + 2, par=0, batch=affine(0)))
            if ff.late:
                ev += [Ev("w", st, a=ff.late[0], b=ff.late[1], batch=affine(q), par="late") for q in range(4)]
        if st.i + 1 < len(stages) and not follow:
            ev.append(Ev("src", stages[st.i + 1], batch=affine(0)))
            ev += prologue(stages[st.i + 1])
        if ev:
            segs.append((3, 4, ev))

    n0 = w0 = 0
    item_done = {}
    made = dict.fromkeys(DONE_KINDS.values(), 0)
    for p0, p1, events in segs:
        looped = p1 - p0 > 1
        n = sum(e.kind in DONE_KINDS for e in events)
        w = sum(e.kind == "w" for e in events)
        made_here = {k: sum(DONE_KINDS.get(e.kind) == k for e in events) for k in made}
        assert not looped or (n % 2 == 0 and w % 2 == 0)
        ns, ws = (n, w) if looped else (0, 0)
        before = {k: affine(made[k] - made_here[k] * p0 * looped, made_here[k] * looped) for k in made}
        at_n = at_w = 0
        in_bank = [None, None]
        out = []
        for e in events:
            num = prev = None
            if e.kind in DONE_KINDS:
                num = affine(n0 + at_n - ns * p0, ns)
                prev = in_bank[num[0] % 2] or (before if at_n == 0 else None)
                in_bank[num[0] % 2] = e
                at_n += 1
            if e.kind == "w":
                num = affine(w0 + at_w - ws * p0, ws)
                at_w += 1
                item_done[e.a] = max(item_done.get(e.a, 0), w0 + at_w + ws * (p1 - 1 - p0))
            free = affine(n0 + at_n) if e.par == "late" else affine(n0 - ns * p0, ns)
            out.append(e._replace(n=num, seg=free, prev=prev))
        segments.append((p0, p1, out))
        n0 += n * (p1 - p0)
        w0 += w * (p1 - p0)
        for k in made:
            made[k] += made_here[k] * (p1 - p0)
    return stages, shapes, base, segments, item_done


ITEM_OF = {
    0: dict(q=0, k=1, v=2, o=3), 1: dict(q=4, k=5, v=6, o=7), 2: dict(q=11, k=12, v=13, o=14),
    3: dict(q=15, k=16, v=17, o=18), 4: dict(q=22, k=23, v=24, o=25), 5: dict(q=26, k=26, v=27, o=27),
    6: dict(q=28, k=29, v=29, o=28),
}
FF_ITEMS = {1: (8, 9, 10), 3: (19, 20, 21), 6: (None, 30, 31)}


def program(nc, x_in, ctxT, wts, lnp, bo, bff, bsm, mask_s, mask_x, out):
    F32, F32R, I32, U8 = mybir.dt.float32, mybir.dt.float32r, mybir.dt.int32, mybir.dt.uint8
    ACT, ALU, AX = mybir.ActivationFunctionType, mybir.AluOpType, mybir.AxisListType
    stages, shapes, base, segments, item_done = build_schedule()

    with ExitStack() as ctx:
        def sb(name, shape, dt=F32):
            return ctx.enter_context(nc.sbuf_tensor(name, shape, dt))

        def sem(name):
            return ctx.enter_context(nc.semaphore(name))

        x = sb("x", [T, B, C])
        hT_hi, hT_lo = sb("hT_hi", [128, 2, B * T], F32R), sb("hT_lo", [128, 2, B * T], F32R)
        W = sb("W", [128, 6, 2, 2048], F32R)
        wraw = sb("wraw", [128, 2, WQ])
        KS = sb("KS", [128, H, SP], F32R)
        V = sb("V", [128, 3, 1024])
        QH, QL = sb("QH", [128, H, PAIR], F32R), sb("QL", [128, H, PAIR], F32R)
        AOT_hi, AOT_lo = sb("AOT_hi", [128, 8, T], F32R), sb("AOT_lo", [128, 8, T], F32R)
        P = sb("P", [128, NP_, CHUNK])
        PT = sb("PT", [128, 2, CHUNK])
        src = sb("src", [128, 3 * SP], F32R)
        craw = V[:, 2, 0:2 * SP].rearrange("p (k n) -> p k n", k=2)
        cst = sb("cst", [128, 3, SP])
        hn = sb("hn", [T, 2, C])
        tmp, full = sb("tmp", [T, C]), sb("full", [128, 2, T])
        bo_b = sb("bo_b", [T, 2, C])
        mask_words = sb("mask_words", [T, 2, SP // 4], I32)
        maskf = cst[0:T, 0:2, :]
        causal = sb("causal", [T, T])
        ident = sb("ident", [128, 128])
        lnp_sb, bff_sb, bsm_sb = sb("lnp_sb", [128, N_LN, 2, 2]), sb("bff_sb", [128, 40]), sb("bsm_sb", [128, 6, 4])
        nmax, rawmax = sb("nmax", [T, NP_, 4]), sb("rawmax", [T, 4])
        rsum, rinv = sb("rsum", [T, NP_, 4]), sb("rinv", [T, NP_, 4])
        bn6, mv = sb("bn6", [T, 6]), sb("mv", [T, 2, 2])
        ve, rstd, mhalf = sb("ve", [T, 2]), sb("rstd", [T, 2]), sb("mhalf", [T, 1])
        ctx_split = nc.dram_tensor("ctx_split", [B, 128, 3 * SP], F32).ap()

        def bank(name):
            return ctx.enter_context(nc.psum_tensor(name, [128, 512], F32))
        pS = [bank("pS0"), bank("pS1")]
        pT = [bank("pT0"), bank("pT1")]
        pO = [bank("pO0"), bank("pO1")]
        pG = [bank("pG0"), bank("pG1")]

        consts_in = sem("consts_in")
        x_in_sem = sem("x_in_sem")
        bo_in = sem("bo_in")
        craw_in = sem("craw_in")
        ctx_out = sem("ctx_out")
        src_in = sem("src_in")
        mask_in = [sem("mask_in0"), sem("mask_in1")]
        wraw_in = [sem("wraw_in0"), sem("wraw_in1")]
        out_done = sem("out_done")
        const_ready = sem("const_ready")
        ident0 = sem("ident0")
        w_hi, w_lo = sem("w_hi"), sem("w_lo")
        ctx_hi, ctx_lo = sem("ctx_hi"), sem("ctx_lo")
        ctx_lo2 = sem("ctx_lo2")
        pieces = sem("pieces")
        scored = sem("scored")
        maxed = sem("maxed")
        masked, rawmaxed = sem("masked"), sem("rawmaxed")
        exped = sem("exped")
        recip = sem("recip")
        normed = sem("normed")
        transposed = sem("transposed")
        pt_ready = sem("pt_ready")
        attended = sem("attended")
        ao_hi, ao_lo = sem("ao_hi"), sem("ao_lo")
        q_zero = sem("q_zero")
        q_hi, q_lo, q_dup = sem("q_hi"), sem("q_lo"), sem("q_dup")
        k_hi, k_lo = sem("k_hi"), sem("k_lo")
        v_ready = sem("v_ready")
        gelu_ready, hid_ready = sem("gelu_ready"), sem("hid_ready")
        hid_hi, hid_lo = sem("hid_hi"), sem("hid_lo")
        res_tmp, x_ready = sem("res_tmp"), sem("x_ready")
        ln_stats, ln_mv = sem("ln_stats"), sem("ln_mv")
        ln_ve, ln_rstd = sem("ln_ve"), sem("ln_rstd")
        ln_h = sem("ln_h")
        hT_hi_ready, ln_full, hT_ready = sem("hT_hi_ready"), sem("ln_full"), sem("hT_ready")
        mask_f, mask_ready = sem("mask_f"), sem("mask_ready")

        block = ctx.enter_context(nc.Block())

        def unit(e, p, u=None):
            sh = shapes[e.st.i]
            u = e.a if u is None else u
            return at(affine(base["u"][e.st.i] + e.par * sh.NU + u, 2 * sh.NU), p)

        def unit_ring(e, u=None):
            return (e.a if u is None else u) % 4

        def of_batch(e, p, per):
            return at(affine(per * e.batch[0], per * e.batch[1]), p)

        def k_tiles_before(e, p):
            sh = shapes[e.st.i]
            step = sh.NT if e.st.self_ else 2 * sh.NT
            off = 0 if e.st.self_ else e.par * sh.NT
            return at(affine(base["k"][e.st.i] + off, step), p)

        def wait(eng, s, n):
            if type(n) is int and n <= 0:
                return
            eng.wait_ge(s, n)

        def wait_apart(eng, s, n):
            if type(n) is not int:
                n = eng.to_reg(n)
            elif n <= 0:
                return
            eng.wait_ge(const_ready, 1)
            eng.wait_ge(s, n)

        def made_by(e):
            sh = shapes[e.st.i]
            kind = DONE_KINDS[e.kind]
            b0, b1 = e.batch or (0, 0)
            if e.kind in ("q", "k"):
                n = affine(base[e.kind][e.st.i] + sh.NT * b0 + e.a + 1, sh.NT * b1)
            elif e.kind == "v":
                n = affine(base["v"][e.st.i] + sh.NV * b0 + e.a * sh.KT + e.b + 1, sh.NV * b1)
            elif e.kind in ("wo", "ff2", "lnt"):
                n = affine(8 * e.a + b0 + 1, b1)
            else:
                n = affine(16 * sorted(FFS).index(e.st.i) + 8 * e.b + e.a + 1)
            return kind, n

        def bank_of(e):
            return e.n[0] % 2

        def walk(eng, emit):
            for p0, p1, events in segments:
                if p1 - p0 > 1:
                    with eng.Fori(p0, p1) as p:
                        for e in events:
                            emit(e, p)
                else:
                    for e in events:
                        emit(e, p0)

        def w_view(slot, hl, col, n):
            return W[:, slot, hl, col:col + n]

        def hidden(buf):
            return buf[:, :, :].rearrange("p h n -> p (h n)")[:, 0:8 * CHUNK].rearrange("p (t n) -> p t n", t=8)

        def k_rewritable(e, p):
            st = e.st
            sh = shapes[st.i]
            if e.batch[1] == 0:
                return base["u"][st.i]
            last_unit = (e.a * sh.HPT + sh.HPT - 1) // sh.G
            if e.kind == "q" or st.self_:
                return at(affine(base["u"][st.i] + (2 * e.batch[0] - 1) * sh.NU + last_unit + 1, 2 * sh.NU), p)
            return at(affine(base["u"][st.i] + (e.batch[0] - 1) * sh.NU + last_unit + 1, 2 * sh.NU), p)

        def ff_before(st):
            done = [FFS[i].res for i in FFS if i < st.i]
            return 8 * (max(done) + 1) if done else 0

        def gelu_buf(i):
            return P[:, :, :].rearrange("p a n -> p (a n)")[:, i * CHUNK:(i + 1) * CHUNK]

        @block.sync
        def _(sp):
            sp.dma_start(lnp_sb[:, :, :, :], lnp).then_inc(consts_in, 16)
            sp.dma_start(bff_sb[:, :], bff).then_inc(consts_in, 16)
            sp.dma_start(bsm_sb[:, :, :], bsm).then_inc(consts_in, 16)
            sp.dma_start(x[:, :, :], x_in).then_inc(x_in_sem, 16)
            for i in range(2):
                sp.dma_start(bo_b[:, i, :], bo[i:i + 1, :].broadcast_to([T, C])).then_inc(bo_in, 16)

            def emit(e, p):
                st = e.st
                if e.kind == "w":
                    buf = e.n[0] % 2
                    if e.n[1] or e.n[0] > 1:
                        wait_apart(sp, w_lo, at(e.n, p, -1))
                    col = at(affine(e.batch[0] * WQ, e.batch[1] * WQ), p)
                    sp.dma_start(wraw[:, buf, :], wts[e.a, :, bass.ds(col, WQ)]).then_inc(wraw_in[buf], 16)
                elif e.kind == "src":
                    wait_apart(sp, v_ready, base["v"][st.i] + of_batch(e, p, shapes[st.i].NV))
                    sh = shapes[st.i]
                    if st.self_:
                        wait_apart(sp, hT_ready, 8 * st.ln + of_batch(e, p, 1) + 1)
                        sv = src[:, 0:4 * T].bitcast(F32).rearrange("p (a k t) -> p a k t", a=2, k=2)
                        tok = of_batch(e, p, T)
                        sp.dma_start(sv[:, 0, :, :], hT_hi[:, :, bass.ds(tok, T)].bitcast(F32)).then_inc(src_in, 16)
                        sp.dma_start(sv[:, 1, :, :], hT_lo[:, :, bass.ds(tok, T)].bitcast(F32)).then_inc(src_in, 16)
                    else:
                        wait_apart(sp, k_lo, base["k"][st.i] + of_batch(e, p, sh.NT))
                        sp.wait_ge(ctx_out, 16 * (B - 1) if st.i == 1 and e.batch == affine(0) else 16 * B)
                        n = 3 * SP // 2
                        for h in range(2):
                            sp.dma_start(src[:, h * n:(h + 1) * n].bitcast(F32),
                                         ctx_split[bass.ds(of_batch(e, p, 1), 1), :, h * n:(h + 1) * n]
                                         .rearrange("a p n -> (a p) n")).then_inc(src_in, 16)
                elif e.kind == "mask":
                    words = shapes[st.i].keys // 4 if st.self_ else SP // 4
                    wait_apart(sp, maxed, unit(e, p, -shapes[st.i].NU))
                    msrc = mask_s if st.self_ else mask_x
                    sp.dma_start(mask_words[:, e.par, 0:words],
                                 msrc[bass.ds(of_batch(e, p, 1), 1), :].broadcast_to([T, words])).then_inc(mask_in[e.par], 16)
                elif e.kind == "ctx":
                    b = of_batch(e, p, 1)
                    wait_apart(sp, ctx_lo, b)
                    wait_apart(sp, ctx_lo2, b)
                    sp.dma_start(craw[:, :, :], ctxT[:, bass.ds(b, 1), :, :].rearrange("p b k t -> p (b k) t")).then_inc(craw_in, 16)
                    wait_apart(sp, ctx_lo, b + 1)
                    wait_apart(sp, ctx_lo2, b + 1)
                    sp.dma_start(ctx_split[bass.ds(b, 1), :, :].rearrange("a p n -> (a p) n"),
                                 cst[:, :, :].rearrange("p a n -> p (a n)")).then_inc(ctx_out, 16)
                if e.kind == "ff2" and st.i == 6:
                    sp.wait_ge(x_ready, 8 * e.a + e.batch[0] + 1)
                    b = e.batch[0]
                    sp.dma_start(out[:, b, :], x[:, b, :]).then_inc(out_done, 16)
                if e.kind == "bo":
                    sp.wait_ge(x_ready, 8 * (e.a - 1))
                    sp.dma_start(bo_b[:, e.a % 2, :], bo[e.a:e.a + 1, :].broadcast_to([T, C])).then_inc(bo_in, 16)
            walk(sp, emit)
            sp.wait_ge(out_done, 16 * B)

        @block.tensor
        def _(pe):
            def mm(o, l, r, first, last):
                return nc.tensor.matmul(o, l, r, start=first, stop=last)

            def accumulate(o, passes):
                for i, (l, r) in enumerate(passes):
                    ins = mm(o, l, r, i == 0, i == len(passes) - 1)
                return ins

            done = {"q_lo": q_lo, "k_lo": k_lo, "v_ready": v_ready, "x_ready": x_ready, "hT_ready": hT_ready,
                    "gelu_ready": gelu_ready, "hid_ready": hid_ready}

            def piece_start(e, p):
                if e.prev is None:
                    return
                if type(e.prev) is dict:
                    for name, n in e.prev.items():
                        if n != affine(0):
                            wait(pe, done[name], at(n, p))
                    return
                name, n = made_by(e.prev)
                wait(pe, done[name], at(n, p))

            seen = set()

            def weights_ready(item):
                if item not in seen:
                    seen.add(item)
                    pe.wait_ge(w_lo, item_done[item])

            pe.wait_ge(const_ready, 1)

            def emit(e, p):
                st = e.st
                sh = shapes[st.i]
                if e.kind in ("q", "k") and (e.kind == "q" or st.self_):
                    role = st.q if e.kind == "q" else st.k
                    weights_ready(ITEM_OF[st.i][e.kind])
                    tok = of_batch(e, p, PAIR)
                    wait(pe, hT_ready, 8 * st.ln + of_batch(e, p, 2) + 2)
                    piece_start(e, p)
                    slot, col, ks = role
                    passes = []
                    for k in range(2):
                        hi = w_view(slot, 0, col + k * ks + e.a * 128, 128)
                        lo = w_view(slot, 1, col + k * ks + e.a * 128, 128)
                        ah, al = hT_hi[:, k, bass.ds(tok, PAIR)], hT_lo[:, k, bass.ds(tok, PAIR)]
                        passes += [(hi, ah), (hi, al), (lo, ah)]
                    accumulate(pG[bank_of(e)][:, 0:PAIR], passes).then_inc(pieces, 1)
                elif e.kind == "k":
                    weights_ready(ITEM_OF[st.i]["k"])
                    pe.wait_ge(src_in, 32 * 8 * st.i + of_batch(e, p, 32) + 32)
                    piece_start(e, p)
                    slot, col, ks = st.k
                    wv = [[w_view(slot, hl, col + k * ks + e.a * 128, 128) for hl in range(2)] for k in range(2)]
                    s = [src[:, i * SP:(i + 1) * SP] for i in range(3)]
                    accumulate(pG[bank_of(e)][:, 0:SP],
                               [(wv[0][0], s[0]), (wv[0][0], s[1]), (wv[0][1], s[0]), (wv[1][0], s[2]), (wv[1][1], s[2])]
                               ).then_inc(pieces, 1)
                elif e.kind == "v":
                    weights_ready(ITEM_OF[st.i]["v"])
                    pe.wait_ge(src_in, 32 * 8 * st.i + of_batch(e, p, 32) + 32)
                    piece_start(e, p)
                    slot, col, ks = st.v
                    wv = [[w_view(slot, hl, col + k * ks + e.a * 512, 512) for hl in range(2)] for k in range(2)]
                    if st.self_:
                        a = [[src[:, (hl * 2 + k) * T:(hl * 2 + k + 1) * T] for hl in range(2)] for k in range(2)]
                        passes = []
                        for k in range(2):
                            passes += [(a[k][0], wv[k][0]), (a[k][0], wv[k][1]), (a[k][1], wv[k][0])]
                    else:
                        s = [src[:, i * SP + e.b * KM:i * SP + (e.b + 1) * KM] for i in range(3)]
                        passes = [(s[0], wv[0][0]), (s[0], wv[0][1]), (s[1], wv[0][0]), (s[2], wv[1][0]), (s[2], wv[1][1])]
                    accumulate(pG[bank_of(e)][0:sh.krows, :], passes).then_inc(pieces, 1)
                elif e.kind == "scores":
                    U = unit(e, p)
                    tile = (e.a * sh.G + sh.G - 1) // sh.HPT
                    if (e.a * sh.G) % sh.HPT == 0:
                        wait(pe, q_lo, at(affine(base["q"][st.i] + tile + 1, sh.NT), p))
                        wait(pe, k_lo, k_tiles_before(e, p) + tile + 1)
                    wait(pe, exped, U - 1)
                    for g in range(sh.G):
                        h = e.a * sh.G + g
                        t = h // sh.HPT
                        qc = slice(e.par * T, (e.par + 1) * T)
                        kc = slice(e.par * T, (e.par + 1) * T) if st.self_ else slice(0, SP)
                        n = T if st.self_ else SP
                        o = pS[e.a % 2][0:T, g * T:g * T + n]
                        if st.small:
                            passes = [(QH[:, h, qc], KS[:, t, kc]), (QH[:, h, qc], KS[:, 4 + t, kc]), (QL[:, h, qc], KS[:, t, kc])]
                        else:
                            passes = [(QH[:, h, qc], KS[:, h, kc]), (QL[:, h, qc], KS[:, h, kc])]
                        ins = accumulate(o, passes)
                    ins.then_inc(scored, 1)
                elif e.kind == "trans":
                    U = unit(e, p)
                    wait(pe, normed, U + 1)
                    wait(pe, pt_ready, U - 1)
                    for i in range(sh.G * sh.KT):
                        lhsT = P[0:T, unit_ring(e), i * sh.krows:(i + 1) * sh.krows]
                        ins = nc.tensor.transpose(pT[e.a % 2][0:sh.krows, i * T:(i + 1) * T], lhsT, ident[0:T, 0:T])
                    ins.then_inc(transposed, 1)
                elif e.kind == "av":
                    U = unit(e, p)
                    pe.wait_ge(pt_ready, U + 1)
                    per = sh.NU // sh.NO
                    o = e.a // per
                    if e.a % per == 0:
                        A = at(affine(base["a"][st.i] + e.par * sh.NO + o, 2 * sh.NO), p)
                        wait(pe, ao_lo, A - 1)
                        pe.wait_ge(v_ready, at(affine(base["v"][st.i] + e.par * sh.NV + (o + 1) * sh.KT * sh.VH // sh.NO, 2 * sh.NV), p))
                    ob = pO[o if sh.NO == 2 else e.par]
                    for g in range(sh.G):
                        h = e.a * sh.G + g
                        t = (h // sh.HPT) % 4
                        row = sh.M * (h % sh.HPT)
                        passes = []
                        for m in range(sh.KT):
                            vs = e.par if st.self_ else m
                            pt = PT[0:sh.krows, e.a % 2, (g + m) * T:(g + m + 1) * T]
                            passes.append((V[0:sh.krows, vs, h * sh.M:(h + 1) * sh.M], pt))
                        ins = accumulate(ob[row:row + sh.M, t * T:(t + 1) * T], passes)
                    ins.then_inc(attended, 1)
                elif e.kind == "wo":
                    weights_ready(ITEM_OF[st.i]["o"])
                    pe.wait_ge(ao_lo, at(affine(base["a"][st.i] + (e.par + 1) * sh.NO, 2 * sh.NO), p))
                    piece_start(e, p)
                    slot, col, ks = st.o
                    passes = []
                    for t in range(sh.NT):
                        hi, lo = w_view(slot, 0, col + t * C, C), w_view(slot, 1, col + t * C, C)
                        passes += [(AOT_hi[:, t, :], hi), (AOT_hi[:, t, :], lo), (AOT_lo[:, t, :], hi)]
                    accumulate(pG[bank_of(e)][0:T, 0:C], passes).then_inc(pieces, 1)
                elif e.kind == "lnt":
                    wait(pe, ln_h, 8 * e.a + of_batch(e, p, 1) + 1)
                    piece_start(e, p)
                    for k in range(2):
                        ins = nc.tensor.transpose(pG[bank_of(e)][:, k * T:(k + 1) * T],
                                                  hn[:, e.par, k * 128:(k + 1) * 128], ident[0:T, 0:T])
                    ins.then_inc(pieces, 1)
                elif e.kind in ("ffg", "ffa"):
                    ff = FFS[st.i]
                    slot = ff.gate if e.kind == "ffg" else ff.value
                    weights_ready(FF_ITEMS[st.i][1 if e.kind == "ffg" else 0])
                    pe.wait_ge(hT_ready, 8 * ff.ln + 4 * (e.b + 1))
                    piece_start(e, p)
                    passes = []
                    for k in range(2):
                        hi, lo = w_view(slot, 0, k * 1024 + e.a * 128, 128), w_view(slot, 1, k * 1024 + e.a * 128, 128)
                        ah, al = hT_hi[:, k, e.b * CHUNK:(e.b + 1) * CHUNK], hT_lo[:, k, e.b * CHUNK:(e.b + 1) * CHUNK]
                        passes += [(hi, ah), (hi, al), (lo, ah)]
                    accumulate(pG[bank_of(e)][:, 0:CHUNK], passes).then_inc(pieces, 1)
                elif e.kind == "ff2":
                    ff = FFS[st.i]
                    weights_ready(FF_ITEMS[st.i][2])
                    k = sorted(FFS).index(st.i)
                    pe.wait_ge(hid_lo, 16 * k + 8 * (e.batch[0] // 4 + 1))
                    piece_start(e, p)
                    gh, gl = hidden(KS), hidden(QH)
                    passes = []
                    for t in range(8):
                        a = slice(e.b * T, (e.b + 1) * T)
                        hi, lo = w_view(ff.out, 0, t * C, C), w_view(ff.out, 1, t * C, C)
                        passes += [(gh[:, t, a], hi), (gh[:, t, a], lo), (gl[:, t, a], hi)]
                    accumulate(pG[bank_of(e)][0:T, 0:C], passes).then_inc(pieces, 1)
            walk(pe, emit)

        @block.scalar
        def _(act):
            act.wait_ge(consts_in, 48)

            def emit(e, p):
                st = e.st
                sh = shapes[st.i]
                g = pG[bank_of(e)] if e.n is not None and e.kind != "w" else None
                if e.kind == "q":
                    act.wait_ge(pieces, at(e.n, p, 1))
                    wait(act, scored, k_rewritable(e, p))
                    if e.batch[1] == 0:
                        wait(act, x_ready, ff_before(st))
                    if st.small:
                        act.wait_ge(q_zero, 3)
                        for i in range(4):
                            r = slice(32 * i, 32 * i + 32)
                            ins = act.activation(QH[r, 4 * e.a + i, :], g[r, 0:PAIR], ACT.Identity,
                                                 bias=bsm_sb[r, 0 if st.self_ else 3, e.a:e.a + 1])
                        ins.then_inc(q_hi, 1)
                    else:
                        act.activation(QH[0:64, 2 * e.a, :], g[0:64, 0:PAIR], ACT.Copy, scale=st.qscale)
                        act.activation(QH[64:128, 2 * e.a + 1, :], g[64:128, 0:PAIR], ACT.Copy, scale=st.qscale).then_inc(q_hi, 1)
                        act.activation(QH[0:64, 2 * e.a + 1, :], g[64:128, 0:PAIR], ACT.Copy, scale=st.qscale).then_inc(q_dup, 1)
                elif e.kind == "k":
                    n = PAIR if st.self_ else SP
                    act.wait_ge(pieces, at(e.n, p, 1))
                    wait(act, scored, k_rewritable(e, p))
                    if e.batch[1] == 0:
                        wait(act, x_ready, ff_before(st))
                    if st.small:
                        act.activation(KS[:, e.a, 0:n], g[:, 0:n], ACT.Identity,
                                       bias=bsm_sb[:, 1 if st.self_ else 4, e.a:e.a + 1]).then_inc(k_hi, 1)
                    else:
                        act.activation(KS[0:64, 2 * e.a, 0:n], g[0:64, 0:n], ACT.Copy)
                        act.activation(KS[64:128, 2 * e.a + 1, 0:n], g[64:128, 0:n], ACT.Copy).then_inc(k_hi, 1)
                elif e.kind == "v":
                    act.wait_ge(pieces, at(e.n, p, 1))
                    if e.batch[1] == 0:
                        wait(act, attended, base["u"][st.i])
                        if st.i == 1:
                            act.wait_ge(ctx_lo2, B)
                            act.wait_ge(ctx_lo, B)
                    else:
                        per = sh.NU // sh.VH
                        back = 2 if st.self_ else 1
                        c = affine(base["u"][st.i] + (e.batch[0] - back) * sh.NU + (e.a + 1) * per, 2 * sh.NU)
                        wait(act, attended, at(c, p))
                    slot = (e.batch[0] % 2) if st.self_ else e.b
                    act.activation(V[0:sh.krows, slot, e.a * 512:(e.a + 1) * 512], g[0:sh.krows, :], ACT.Copy).then_inc(v_ready, 1)
                elif e.kind == "scores":
                    U = unit(e, p)
                    act.wait_ge(maxed, U + 1)
                    if not st.small:
                        wait(act, transposed, U - NP_ + 1)
                    for i in range(sh.G):
                        n = sh.keys
                        o = P[0:T, unit_ring(e), i * n:(i + 1) * n]
                        s = o if st.small else pS[e.a % 2][0:T, i * n:(i + 1) * n]
                        ins = act.activation(o, s, ACT.Exp, bias=nmax[:, unit_ring(e), i:i + 1], scale=st.escale,
                                             accum_out=rsum[:, unit_ring(e), i:i + 1])
                    ins.then_inc(exped, 1)
                elif e.kind == "trans":
                    U = unit(e, p)
                    act.wait_ge(transposed, U + 1)
                    wait(act, attended, U - 1)
                    n = sh.G * sh.KT * T
                    act.activation(PT[0:sh.krows, e.a % 2, 0:n], pT[e.a % 2][0:sh.krows, 0:n], ACT.Copy).then_inc(pt_ready, 1)
                elif e.kind == "ao":
                    per = sh.NU // sh.NO
                    act.wait_ge(attended, unit(e, p, (e.a + 1) * per - 1) + 1)
                    wait(act, x_ready, 8 * st.res + of_batch(e, p, 1))
                    ob = pO[e.a if sh.NO == 2 else e.par]
                    if st.small:
                        for t in range(4):
                            ins = act.activation(AOT_hi[:, t, :], ob[:, t * T:(t + 1) * T], ACT.Identity,
                                                 bias=bsm_sb[:, 2 if st.self_ else 5, t:t + 1])
                    else:
                        ins = act.activation(AOT_hi[:, 4 * e.a:4 * e.a + 4, :],
                                             ob[:, 0:4 * T].rearrange("p (t n) -> p t n", t=4), ACT.Copy)
                    ins.then_inc(ao_hi, 1)
                elif e.kind == "lnt":
                    act.wait_ge(pieces, at(e.n, p, 1))
                    for k in range(2):
                        ins = act.activation(hT_hi[:, k, bass.ds(of_batch(e, p, T), T)], g[:, k * T:(k + 1) * T], ACT.Identity,
                                             bias=lnp_sb[:, e.a, 1, k:k + 1], scale=lnp_sb[:, e.a, 0, k:k + 1])
                    ins.then_inc(hT_hi_ready, 1)
                elif e.kind == "ffg":
                    ff = FFS[st.i]
                    N = 16 * sorted(FFS).index(st.i) + 8 * e.b + e.a
                    act.wait_ge(pieces, at(e.n, p, 1))
                    col = ff.bias + e.a + (8 if ff.value is not None else 0)
                    if ff.value is not None:
                        wait(act, hid_ready, N - 1 if N % 16 > 1 else N - N % 16)
                        o = gelu_buf(N % 2)
                        if N % 16 < 2:
                            act.wait_ge(transposed, base["u"][st.i + 1])
                    else:
                        wait(act, hid_lo, N - 1)
                        o = PT[:, N % 2, :]
                        if N % 16 < 2:
                            act.wait_ge(attended, base["u"][st.i + 1])
                    fn = ACT.Gelu if ff.act == "erf" else ACT.Gelu_apprx_tanh
                    act.activation(o, g[:, 0:CHUNK], fn, bias=bff_sb[:, col:col + 1]).then_inc(gelu_ready, 1)
            walk(act, emit)

        @block.vector
        def _(dve):
            dve.wait_ge(consts_in, 48)
            dve.wait_ge(const_ready, 1)

            def split_w(e, p):
                buf = e.n[0] % 2
                dve.wait_ge(wraw_in[buf], at(affine(16 * (e.n[0] // 2 + 1), 16 * (e.n[1] // 2)), p))
                wait(dve, pieces, at(e.seg, p))
                col = at(affine(e.batch[0] * WQ, e.batch[1] * WQ), p)
                dve.tensor_copy(W[:, e.b, 0, bass.ds(col, WQ)], wraw[:, buf, :]).then_inc(w_hi, 1)

            def layer_norm(e, p, group):
                n = 8 * group + of_batch(e, p, 1)
                xb = x[:, bass.ds(of_batch(e, p, 1), 1), :].rearrange("p a n -> p (a n)")
                if group:
                    wait_apart(dve, x_ready, n - 7)
                dve.bn_stats(bn6[:, :], xb).then_inc(ln_stats, 1)
                wait_apart(dve, ln_stats, n + 1)
                dve.bn_aggr(mv[:, e.par, :], bn6[:, :]).then_inc(ln_mv, 1)

            def residual(e, p, ps):
                r = 8 * e.a + of_batch(e, p, 1)
                xb = x[:, bass.ds(of_batch(e, p, 1), 1), :].rearrange("p a n -> p (a n)")
                dve.wait_ge(bo_in, 16 * (e.a + 1) if e.a else 32)
                wait(dve, x_ready, r)
                dve.tensor_tensor(tmp[0:T, :], ps, bo_b[:, e.a % 2, :], ALU.add).then_inc(res_tmp, 1)
                dve.wait_ge(res_tmp, r + 1)
                dve.tensor_tensor(xb, xb, tmp[0:T, :], ALU.add).then_inc(x_ready, 1)

            def emit(e, p):
                st = e.st
                sh = shapes[st.i]
                isp = e.n is not None and e.kind != "w"
                g = pG[bank_of(e)] if isp else None
                if e.kind == "w":
                    split_w(e, p)
                elif e.kind == "ln0":
                    if e.batch[0] == 0:
                        dve.wait_ge(x_in_sem, 16)
                    layer_norm(e, p, 0)
                elif e.kind == "q":
                    Q = at(affine(base["q"][st.i] + sh.NT * e.batch[0] + e.a, sh.NT * e.batch[1]), p)
                    dve.wait_ge(q_hi, Q + 1)
                    if st.small:
                        for i in range(4):
                            r = slice(32 * i, 32 * i + 32)
                            ins = dve.scalar_tensor_tensor(QL[r, 4 * e.a + i, :], g[r, 0:PAIR],
                                                           bsm_sb[r, 0 if st.self_ else 3, e.a:e.a + 1],
                                                           QH[r, 4 * e.a + i, :].bitcast(F32), ALU.add, ALU.subtract)
                        ins.then_inc(q_lo, 1)
                    else:
                        D = at(affine(base["q"][st.i] + sh.NT * e.batch[0] + e.a, sh.NT * e.batch[1]), p)
                        dve.wait_ge(q_dup, D + 1)
                        if st.i == 0 and e.batch[1] == 0:
                            dve.wait_ge(q_zero, 1)
                        dve.scalar_tensor_tensor(QL[0:64, 2 * e.a, :], g[0:64, 0:PAIR], st.qscale,
                                                 QH[0:64, 2 * e.a, :].bitcast(F32), ALU.mult, ALU.subtract)
                        dve.scalar_tensor_tensor(QL[64:128, 2 * e.a + 1, :], g[64:128, 0:PAIR], st.qscale,
                                                 QH[64:128, 2 * e.a + 1, :].bitcast(F32), ALU.mult, ALU.subtract)
                        dve.tensor_copy(QH[64:128, 2 * e.a, :], QH[0:64, 2 * e.a, :].bitcast(F32)).then_inc(q_lo, 1)
                elif e.kind == "k":
                    n = PAIR if st.self_ else SP
                    K = at(affine(base["k"][st.i] + sh.NT * e.batch[0] + e.a, sh.NT * e.batch[1]), p)
                    dve.wait_ge(k_hi, K + 1)
                    if st.small:
                        dve.scalar_tensor_tensor(KS[:, 4 + e.a, 0:n], g[:, 0:n], bsm_sb[:, 1 if st.self_ else 4, e.a:e.a + 1],
                                                 KS[:, e.a, 0:n].bitcast(F32), ALU.add, ALU.subtract).then_inc(k_lo, 1)
                    else:
                        dve.tensor_tensor(KS[64:128, 2 * e.a, 0:n], g[0:64, 0:n], KS[0:64, 2 * e.a, 0:n].bitcast(F32), ALU.subtract)
                        dve.tensor_tensor(KS[0:64, 2 * e.a + 1, 0:n], g[64:128, 0:n], KS[64:128, 2 * e.a + 1, 0:n].bitcast(F32),
                                          ALU.subtract).then_inc(k_lo, 1)
                elif e.kind == "scores":
                    U = unit(e, p)
                    r = unit_ring(e)
                    (wait_apart if st.small else wait)(dve, scored, U + 1)
                    ps = pS[e.a % 2][0:T, 0:sh.G * sh.keys]
                    if not st.small:
                        if sh.G > 1:
                            ps = ps.rearrange("p (g n) -> p g n", g=sh.G)
                        dve.tensor_reduce(nmax[:, r, 0:sh.G], ps, AX.X, ALU.max, negate=True).then_inc(maxed, 1)
                    else:
                        i = U - base["u"][5]
                        if e.a == 0:
                            wait_apart(dve, mask_ready, at(affine(base["m"][st.i] + e.par + 1, 2), p))
                        wait_apart(dve, transposed, U - NP_ + 1)
                        wait_apart(dve, maxed, U)
                        po = P[0:T, r, 0:sh.G * sh.keys]
                        if st.self_:
                            po = po.rearrange("p (g n) -> p g n", g=4)
                            mk = maskf[:, e.par:e.par + 1, 0:T].broadcast_to([T, 4, T])
                            dve.tensor_tensor(po, ps.rearrange("p (g n) -> p g n", g=4), mk, ALU.add).then_inc(masked, 1)
                            dve.wait_ge(masked, i + 1)
                            dve.tensor_reduce(rawmax[:, 0:4], po, AX.X, ALU.max).then_inc(rawmaxed, 1)
                        else:
                            dve.tensor_tensor_reduce(out=po, in0=ps, in1=maskf[:, e.par, 0:S2], scale=1.0, scalar=-3e38,
                                                     op0=ALU.add, op1=ALU.max, accum_out=rawmax[:, 0:1]).then_inc(rawmaxed, 1)
                        dve.wait_ge(rawmaxed, i + 1)
                        dve.tensor_scalar(nmax[:, r, 0:sh.G], rawmax[:, 0:sh.G], -st.escale, None, ALU.mult).then_inc(maxed, 1)
                elif e.kind == "norm":
                    U = unit(e, p)
                    dve.wait_ge(exped, U + 1)
                    r = unit_ring(e)
                    dve.reciprocal(rinv[:, r, 0:sh.G], rsum[:, r, 0:sh.G]).then_inc(recip, 1)
                elif e.kind == "ao":
                    A = at(affine(base["a"][st.i] + e.par * sh.NO + e.a, 2 * sh.NO), p)
                    dve.wait_ge(ao_hi, A + 1)
                    ob = pO[e.a if sh.NO == 2 else e.par]
                    if st.small:
                        for t in range(4):
                            ins = dve.scalar_tensor_tensor(AOT_lo[:, t, :], ob[:, t * T:(t + 1) * T], bsm_sb[:, 2 if st.self_ else 5, t:t + 1],
                                                           AOT_hi[:, t, :].bitcast(F32), ALU.add, ALU.subtract)
                    else:
                        ins = dve.tensor_tensor(AOT_lo[:, 4 * e.a:4 * e.a + 4, :], ob[:, 0:4 * T].rearrange("p (t n) -> p t n", t=4),
                                                AOT_hi[:, 4 * e.a:4 * e.a + 4, :].bitcast(F32), ALU.subtract)
                    ins.then_inc(ao_lo, 1)
                elif e.kind in ("wo", "ff2"):
                    dve.wait_ge(pieces, at(e.n, p, 1))
                    residual(e, p, g[0:T, 0:C])
                    if e.a < N_LN - 1:
                        layer_norm(e, p, e.a + 1)
                elif e.kind == "ctx":
                    b = of_batch(e, p, 1)
                    dve.wait_ge(ctx_hi, b + 1)
                    dve.tensor_tensor(cst[64:128, 2, :].bitcast(F32R), craw[64:128, 1, :], cst[64:128, 2, :],
                                      ALU.subtract).then_inc(ctx_lo2, 1)
                elif e.kind == "lnt":
                    n = 8 * e.a + of_batch(e, p, 1)
                    xb = x[:, bass.ds(of_batch(e, p, 1), 1), :].rearrange("p a n -> p (a n)")
                    dve.wait_ge(ln_rstd, n + 1)
                    dve.tensor_scalar(hn[:, e.par, :], xb, mv[:, e.par, 0:1], rstd[:, e.par:e.par + 1],
                                      ALU.subtract, ALU.mult).then_inc(ln_h, 1)
                    dve.wait_ge(hT_hi_ready, n + 1)
                    for k in range(2):
                        ins = dve.tensor_scalar(full[:, k, :], g[:, k * T:(k + 1) * T], lnp_sb[:, e.a, 0, k:k + 1],
                                                lnp_sb[:, e.a, 1, k:k + 1], ALU.mult, ALU.add)
                    ins.then_inc(ln_full, 1)
                    dve.wait_ge(ln_full, n + 1)
                    tok = of_batch(e, p, T)
                    dve.tensor_tensor(hT_lo[:, :, bass.ds(tok, T)], full[:, :, :], hT_hi[:, :, bass.ds(tok, T)].bitcast(F32),
                                      ALU.subtract).then_inc(hT_ready, 1)
                elif e.kind in ("ffg", "ffa"):
                    ff = FFS[st.i]
                    if e.kind == "ffg" and ff.value is not None:
                        return
                    k = sorted(FFS).index(st.i)
                    N = 16 * k + 8 * e.b + e.a
                    dve.wait_ge(gelu_ready, N + 1)
                    if ff.value is not None:
                        dve.wait_ge(pieces, at(e.n, p, 1))
                        if e.b == 0 and e.a == 0:
                            dve.wait_ge(attended, base["u"][st.i + 1])
                        col = ff.bias + e.a
                        dve.scalar_tensor_tensor(PT[:, N % 2, :], g[:, 0:CHUNK], bff_sb[:, col:col + 1], gelu_buf(N % 2),
                                                 ALU.add, ALU.mult).then_inc(hid_ready, 1)
                        dve.wait_ge(hid_ready, N + 1)
                    if e.b == 0 and e.a == 0:
                        dve.wait_ge(scored, base["u"][st.i + 1])
                    if e.b == 1 and e.a == 0:
                        dve.wait_ge(x_ready, 8 * ff.res + 4)
                    hid = PT[:, N % 2, :]
                    dve.tensor_copy(hidden(KS)[:, e.a, :], hid).then_inc(hid_hi, 1)
                    dve.wait_ge(hid_hi, N + 1)
                    dve.tensor_tensor(hidden(QH)[:, e.a, :], hid, hidden(KS)[:, e.a, :].bitcast(F32), ALU.subtract).then_inc(hid_lo, 1)
            walk(dve, emit)

        @block.gpsimd
        def _(pool):
            pool.memset(ident[:, :], 0.0).then_inc(ident0, 1)
            pool.memset(causal[:, :], 0.0).then_inc(ident0, 1)
            pool.memset(mhalf[:, :], -0.5).then_inc(ident0, 1)
            pool.wait_ge(ident0, 3)
            pool.affine_select(out=causal[:, :], in_=causal[:, :], compare_op=ALU.is_ge, fill=MASKED,
                               base=0, pattern=[[-1, T]], channel_multiplier=1).then_inc(ident0, 1)
            pool.affine_select(out=ident[:, :], in_=ident[:, :], compare_op=ALU.not_equal, fill=1.0,
                               base=0, pattern=[[-1, 128]], channel_multiplier=1).then_inc(const_ready, 1)
            pool.wait_ge(ident0, 4)
            pool.memset(QL[:, :, :].bitcast(F32), 0.0).then_inc(q_zero, 1)

            def rstd_of(e, p, group):
                n = 8 * group + of_batch(e, p, 1)
                wait_apart(pool, ln_mv, n + 1)
                pool.tensor_scalar(ve[:, e.par:e.par + 1], mv[:, e.par, 1:2], EPS, None, ALU.add).then_inc(ln_ve, 1)
                pool.wait_ge(ln_ve, n + 1)
                pool.tensor_tensor(rstd[:, e.par:e.par + 1], ve[:, e.par:e.par + 1], mhalf[:, :], ALU.pow).then_inc(ln_rstd, 1)

            def emit(e, p):
                st = e.st
                sh = shapes[st.i]
                if e.kind == "zero":
                    pool.wait_ge(scored, base["u"][st.i])
                    pool.memset(QH[:, :, :].bitcast(F32), 0.0).then_inc(q_zero, 1)
                    pool.memset(QL[:, :, :].bitcast(F32), 0.0).then_inc(q_zero, 1)
                elif e.kind == "w":
                    wait_apart(pool, w_hi, at(e.n, p, 1))
                    buf = e.n[0] % 2
                    col = at(affine(e.batch[0] * WQ, e.batch[1] * WQ), p)
                    pool.tensor_tensor(W[:, e.b, 1, bass.ds(col, WQ)], wraw[:, buf, :],
                                       W[:, e.b, 0, bass.ds(col, WQ)].bitcast(F32), ALU.subtract).then_inc(w_lo, 1)
                elif e.kind == "norm":
                    U = unit(e, p)
                    r = unit_ring(e)
                    wait_apart(pool, recip, U + 1)
                    for i in range(sh.G):
                        n = sh.keys
                        o = P[0:T, r, i * n:(i + 1) * n]
                        ins = pool.tensor_scalar(o, o, rinv[:, r, i:i + 1], st.nscale, ALU.mult, ALU.mult)
                    ins.then_inc(normed, 1)
                elif e.kind == "ln0":
                    rstd_of(e, p, 0)
                elif e.kind in ("wo", "ff2") and e.a < N_LN - 1:
                    rstd_of(e, p, e.a + 1)
                elif e.kind == "ctx":
                    b = of_batch(e, p, 1)
                    wait_apart(pool, craw_in, 16 * b + 16)
                    wait_apart(pool, ctx_out, 16 * b)
                    for i in range(2):
                        ins = pool.tensor_scalar(cst[:, 2 * i, :].bitcast(F32R), craw[:, i, :], 1.0, 1.0, ALU.mult, ALU.mult)
                    ins.then_inc(ctx_hi, 1)
                    wait_apart(pool, ctx_hi, b + 1)
                    pool.tensor_tensor(cst[:, 1, :].bitcast(F32R), craw[:, 0, :], cst[:, 0, :], ALU.subtract).then_inc(ctx_lo, 1)
                elif e.kind == "mask":
                    m = at(affine(base["m"][st.i] + e.par, 2), p)
                    keys = sh.keys
                    wait_apart(pool, mask_in[e.par], at(affine(8 * base["m"][st.i] + 16, 16), p))
                    wait_apart(pool, maxed, unit(e, p, -sh.NU))
                    mf = maskf[:, e.par, 0:keys]
                    ins = pool.tensor_scalar(mf, mask_words[:, e.par, :].bitcast(U8)[:, 0:keys], MASKED, 1.0, ALU.mult, ALU.mult).then_inc(mask_f, 1)
                    wait_apart(pool, mask_f, m + 1)
                    if st.self_:
                        pool.tensor_tensor(mf, mf, causal[:, :], ALU.add).then_inc(mask_ready, 1)
                    else:
                        pool.tensor_scalar(mf, mf, 1.0, 1.0, ALU.mult, ALU.mult).then_inc(mask_ready, 1)
            walk(pool, emit)


def pack_weights(g):
    def k256(w):
        return w.reshape(2, 128, 1024).transpose(1, 0, 2).reshape(128, 2048)

    def k192(w):
        return np.concatenate([w[:128], np.concatenate([w[128:], w[128:]], 0)], 1)

    def o1024(w):
        return w.reshape(8, 128, 256).transpose(1, 0, 2).reshape(128, 2048)

    def pad_heads(w):
        k = w.shape[0]
        return np.concatenate([w.reshape(k, 16, 16), np.zeros((k, 16, 16), w.dtype)], 2).reshape(k, 512)

    def pad_rows(w):
        return np.concatenate([w.reshape(16, 16, 256), np.zeros((16, 16, 256), w.dtype)], 1).reshape(4, 128, 256) \
            .transpose(1, 0, 2).reshape(128, 1024)

    def tiles(w):
        return w.reshape(2, 128, w.shape[1]).transpose(1, 0, 2).reshape(128, 2 * w.shape[1])

    L0, L1, L2, L3 = ("L%d_xattn_" % i for i in range(4))
    qkv = g[L3 + "qkv_w"]
    items = [k256(g[L0 + "Wq1"]), k256(g[L0 + "Wk1"]), k256(g[L0 + "Wv1"]), o1024(g[L0 + "Wo1"]),
             k256(g[L0 + "Wq2"]), k192(g[L0 + "Wk2"]), k192(g[L0 + "Wv2"]), o1024(g[L0 + "Wo2"]),
             k256(g[L0 + "Wp"][:, :1024]), k256(g[L0 + "Wp"][:, 1024:]), o1024(g[L0 + "Wf"]),
             k256(g[L1 + "wq1"]), k256(g[L1 + "wk1"]), k256(g[L1 + "wv1"]), o1024(g[L1 + "wo1"]),
             k256(g[L1 + "wq2"]), k192(g[L1 + "wk2"]), k192(g[L1 + "wv2"]), o1024(g[L1 + "wo2"]),
             k256(g[L1 + "w_ff1"][:, :1024]), k256(g[L1 + "w_ff1"][:, 1024:]), o1024(g[L1 + "w_ff2"]),
             k256(g[L2 + "Wq"]), k192(g[L2 + "Wk"]), k192(g[L2 + "Wv"]), o1024(g[L2 + "Wo"]),
             k256(np.concatenate([pad_heads(qkv[:, :256]), pad_heads(qkv[:, 256:512])], 1)),
             np.concatenate([tiles(pad_heads(qkv[:, 512:])), pad_rows(g[L3 + "proj_w"])], 1),
             np.concatenate([tiles(pad_heads(g[L3 + "q_w"])), pad_rows(g[L3 + "out_w"])], 1),
             np.concatenate([k192(pad_heads(g[L3 + "k_w"])), k192(pad_heads(g[L3 + "v_w"]))], 1),
             k256(g[L3 + "mlp1_w"]), o1024(g[L3 + "mlp2_w"])]
    return np.stack(items)


def kernel(**inputs):
    import concourse.bacc as bacc
    from concourse.bass_utils import run_bass_kernel_spmd

    g = {k: np.asarray(v) for k, v in inputs.items()}
    L0, L1, L2, L3 = ("L%d_xattn_" % i for i in range(4))

    def cols(v):
        return v.reshape(-1, 128).T

    def small(v):
        return cols(np.concatenate([v.reshape(16, 16), np.zeros((16, 16), v.dtype)], 1).reshape(512))

    def words(m):
        m = np.ascontiguousarray(m).view(np.uint8)
        return np.concatenate([m, np.zeros((B, -m.shape[1] % 4), np.uint8)], 1).view(np.int32)

    norms = [(L0 + "g1", L0 + "b1"), (L0 + "g2", L0 + "b2"), (L0 + "g3", L0 + "b3"),
             (L1 + "ln1_g", L1 + "ln1_b"), (L1 + "ln2_g", L1 + "ln2_b"), (L1 + "ln3_g", L1 + "ln3_b"),
             (L2 + "gamma", L2 + "beta"), (L3 + "ln1_w", L3 + "ln1_b"), (L3 + "ln2_w", L3 + "ln2_b"), (L3 + "ln3_w", L3 + "ln3_b")]
    lnp = np.stack([np.stack([cols(g[a]), cols(g[b])]) for a, b in norms]).transpose(2, 0, 1, 3)
    bo = np.stack([g[n] for n in (L0 + "bo1", L0 + "bo2", L0 + "bf", L1 + "bo1", L1 + "bo2", L1 + "b_ff2", L2 + "bo",
                                  L3 + "proj_b", L3 + "out_b", L3 + "mlp2_b")])
    bff = np.concatenate([cols(g[L0 + "bp"]), cols(g[L1 + "b_ff1"]), cols(g[L3 + "mlp1_b"])], 1)
    qkv_b = g[L3 + "qkv_b"]
    bsm = np.stack([small(v) for v in (qkv_b[:256], qkv_b[256:512], qkv_b[512:], g[L3 + "q_b"], g[L3 + "k_b"], g[L3 + "v_b"])], 1)
    c = g["ctx_768"]
    c = np.concatenate([c, np.zeros((B, SP - S2, E), c.dtype)], 1).transpose(2, 0, 1)
    ctxT = np.stack([c[:128], np.concatenate([c[128:], c[128:]], 0)], 2)
    arrays = {
        "x_in": g["x"].transpose(1, 0, 2), "ctxT": ctxT, "wts": pack_weights(g), "lnp": lnp, "bo": bo, "bff": bff,
        "bsm": bsm, "mask_s": words(g["mask_BxS_bf0"]), "mask_x": words(g["mask_BxS2_bf0"]),
    }
    arrays = {k: np.ascontiguousarray(v) for k, v in arrays.items()}
    nc = bacc.Bacc("TRN2", target_bir_lowering=False, num_devices=1, dynamic_dma_scratch_size=1024)
    aps = [nc.dram_tensor(k, v.shape, mybir.dt.from_np(v.dtype), kind="ExternalInput").ap() for k, v in arrays.items()]
    out = nc.dram_tensor("out", (T, B, C), mybir.dt.float32, kind="ExternalOutput").ap()
    program(nc, *aps, out)
    r = run_bass_kernel_spmd(nc, [arrays], core_ids=[0])
    return np.ascontiguousarray(r.results[0]["out"].transpose(1, 0, 2))
```

```python
from collections import namedtuple
from contextlib import ExitStack

import numpy as np

import concourse.bass as bass
from concourse import mybir

B, T, C = 8, 112, 256
S2, E = 375, 192
SP = S2 + 1
KM = S2 // 3
H = 16
PAIR = 2 * T
NPAIR = B // 2
CHUNK = 4 * T
EPS = 1e-5
MASKED = -1e38
LAG_T, LAG_A = 3, 4
FOLLOW_STEP = 0.4
WO_AFTER, LNH_AFTER, LNT_AFTER = 1.1, 2.5, 3.1
NP_, WQ = 4, 512

Stage = namedtuple("Stage", "i self_ small ln res q k v o head_items loop_items end_items qscale escale nscale")


def make_stages():
    W = 1024
    L0s = dict(i=0, self_=True, small=False, ln=0, res=0, q=(0, 0, W), k=(1, 0, W), v=(2, 0, W), o=(3, 0, C),
               loop_items=((5, 4), (6, 5)), end_items=((4, 0),), qscale=0.125, escale=1.0, nscale=1.0)
    L0c = dict(i=1, self_=False, small=False, ln=1, res=1, q=(0, 0, W), k=(4, 0, W), v=(5, 0, W), o=(1, 0, C),
               loop_items=((8, 2), (9, 3)), end_items=((10, 0),), qscale=0.125, escale=1.0, nscale=1.0)
    L1s = dict(i=2, self_=True, small=False, ln=3, res=3, q=(4, 0, W), k=(5, 0, W), v=(1, 0, W), o=(2, 0, C),
               loop_items=((16, 0), (17, 3)), end_items=((15, 4),), qscale=0.125, escale=1.0, nscale=1.0)
    L1c = dict(i=3, self_=False, small=False, ln=4, res=4, q=(4, 0, W), k=(0, 0, W), v=(3, 0, W), o=(5, 0, C),
               loop_items=((19, 1), (20, 2)), end_items=((21, 4),), qscale=0.125, escale=1.0, nscale=1.0)
    L2c = dict(i=4, self_=False, small=False, ln=6, res=6, q=(0, 0, W), k=(3, 0, W), v=(5, 0, W), o=(1, 0, C),
               loop_items=((26, 2), (27, 4)), end_items=(), qscale=1.0, escale=1.0, nscale=0.125)
    L3s = dict(i=5, self_=True, small=True, ln=7, res=7, q=(2, 0, W), k=(2, 512, W), v=(4, 0, 512), o=(4, 1024, C),
               loop_items=((29, 3), (28, 0)), end_items=(), qscale=1.0, escale=0.25, nscale=1.0)
    L3c = dict(i=6, self_=False, small=True, ln=8, res=8, q=(0, 0, 512), k=(3, 0, 512), v=(3, 1024, 512),
               o=(0, 1024, C), loop_items=((30, 5), (31, 1)), end_items=(), qscale=1.0, escale=0.25, nscale=1.0)
    head = {1: ((7, 1),), 2: ((14, 2),), 3: ((18, 5),), 4: ((25, 1),)}
    return [Stage(head_items=head.get(s["i"], ()), **s) for s in (L0s, L0c, L1s, L1c, L2c, L3s, L3c)]


FF = namedtuple("FF", "value gate out ln res bias act early")
FFS = {
    1: FF(2, 3, 0, 2, 2, 0, "erf", ((11, 4), (12, 5), (13, 1))),
    3: FF(1, 2, 4, 5, 5, 16, "tanh", ((22, 0), (23, 3), (24, 5))),
    6: FF(None, 5, 1, 9, 9, 32, "erf", ()),
}
FIRST_ITEMS = ((0, 0), (1, 1), (2, 2), (3, 3))
FIRST_CHUNKS = 12
N_LN = 10

Ev = namedtuple("Ev", "kind st a b par batch n seg prev", defaults=(None,) * 7)


def affine(c0, c1=0):
    return (c0, c1)


def at(c, p, plus=0):
    return c[0] + plus + c[1] * p if c[1] else c[0] + plus


DONE_KINDS = {"q": "q_lo", "k": "k_lo", "v": "v_ready", "wo": "x_ready", "ff2": "x_ready", "lnt": "hT_ready",
              "ffg": "gelu_ready", "ffa": "hid_ready"}


class Shape:

    def __init__(self, st):
        self.G = 4 if st.self_ else 1
        self.NU = H // self.G
        self.HPT = 4 if st.small else 2
        self.NT = H // self.HPT
        self.M = 32 if st.small else 64
        self.keys = T if st.self_ else S2
        self.KT = 1 if st.self_ else 3
        self.krows = T if st.self_ else KM
        self.VH = H * self.M // 512
        self.NV = self.VH * self.KT
        self.NO = 1 if st.small else 2


def build_schedule():
    stages = make_stages()
    shapes = [Shape(s) for s in stages]
    base = {"u": [0], "k": [0], "q": [0], "v": [0], "a": [0], "m": [0]}
    for s, sh in zip(stages, shapes):
        base["u"].append(base["u"][-1] + B * sh.NU)
        base["k"].append(base["k"][-1] + sh.NT * (NPAIR if s.self_ else B))
        base["q"].append(base["q"][-1] + sh.NT * NPAIR)
        base["v"].append(base["v"][-1] + sh.NV * B)
        base["a"].append(base["a"][-1] + sh.NO * B)
        base["m"].append(base["m"][-1] + (B if s.small else 0))

    def kv_pieces(st, tb, tp, with_k, with_q):
        sh = shapes[st.i]
        qs = [Ev("q", st, a=t, batch=tp) for t in range(sh.NT)] if with_q else []
        ks = [Ev("k", st, a=t, batch=tp if st.self_ else tb) for t in range(sh.NT)] if with_k else []
        vs = [Ev("v", st, a=hf, b=m, batch=tb) for hf in range(sh.VH) for m in range(sh.KT)]
        return qs, ks, vs

    def pair_events(st, last):
        sh = shapes[st.i]
        out = []

        def put(time, kind, **kw):
            out.append((time, Ev(kind, st, **kw)))
        for par in range(2):
            t0 = par * sh.NU
            me, nxt, nxt_pair = affine(par, 2), affine(par + 1, 2), affine(1, 1)
            for u in range(sh.NU):
                put(t0 + u, "scores", a=u, par=par, batch=me)
                put(t0 + u + 1, "norm", a=u, par=par, batch=me)
                put(t0 + u + LAG_T + 0.4, "trans", a=u, par=par, batch=me)
                put(t0 + u + LAG_A + .8, "av", a=u, par=par, batch=me)
                per = sh.NU // sh.NO
                if u % per == per - 1:
                    put(t0 + u + LAG_A + .85, "ao", a=u // per, par=par, batch=me)
            end = t0 + sh.NU - 1 + LAG_A
            put(end + 1 + WO_AFTER, "wo", a=st.res, b=st.res < N_LN - 1, par=par, batch=me)
            put(end + 1 + LNH_AFTER, "lnh", a=st.res + 1, par=par, batch=me)
            put(end + 1 + LNT_AFTER, "lnt", a=st.res + 1, par=par, batch=me)
            if st.i == 0:
                put(t0 + 1.5, "ctx", par=par, batch=me)
            if not (last and par == 1):
                put(t0 + (LAG_A - 2 if st.self_ else LAG_A + 3), "src", par=par, batch=nxt)
                if st.small:
                    put(t0 + sh.NU / 2, "mask", par=par + 1, batch=nxt)
                if st.self_:
                    for hf in range(sh.VH):
                        put(t0 + LAG_A + 0.2 + .4 * hf, "v", a=hf, b=0, par=par, batch=nxt)
                else:
                    for t in range(sh.NT):
                        ready = (t + 1) * sh.HPT - 1 + 0.2
                        at_ = max(ready, LAG_A + 4.2 + t) if sh.NT == 8 else ready
                        put(t0 + at_, "k", a=t, par=par, batch=nxt)
                    for m in range(sh.KT):
                        if st.small:
                            put(t0 + 8.6 + 2 * m, "v", a=0, b=m, par=par, batch=nxt)
                        else:
                            put(t0 + LAG_A + 9.6 + 1.35 * m, "v", a=0, b=m, par=par, batch=nxt)
                            put(end + .9 + m, "v", a=1, b=m, par=par, batch=nxt)
            if par == 1 and not last:
                for t in range(sh.NT):
                    if not st.self_:
                        put(t0 + (t + 1) * sh.HPT - 1 + 1.2, "q", a=t, par=par, batch=nxt_pair)
                    else:
                        step = 1 if st.small else 0.75
                        put(t0 + 0.7 + step * t, "q", a=t, par=par, batch=nxt_pair)
                        put(t0 + 0.55 + step * t, "k", a=t, par=par, batch=nxt_pair)
        for n, (i, slot) in enumerate(st.loop_items):
            put(sh.NU / 4 + n * sh.NU / 2, "w", a=i, b=slot, par=0, batch=affine(0, 1))
        if last:
            n = len(st.end_items) * 4
            for m, (i, slot) in enumerate((i, c) for i in st.end_items for c in range(4)):
                put(LAG_A + 1 + m * (2 * sh.NU - LAG_A - 2) / n, "w", a=i[0], b=i[1], par=0, batch=affine(slot))
        return out

    segments = []

    def prologue(st):
        qs, ks, vs = kv_pieces(st, affine(0), affine(0), True, True)
        zero = [Ev("zero", st, batch=affine(0))] if st.small and st.self_ else []
        mask = [Ev("mask", st, par=0, batch=affine(0))] if st.small else []
        return zero + mask + [e for pair in zip(qs, ks) for e in pair] + vs

    def in_turn(events, t0=0.0, step=1.0):
        return [(t0 + step * i, e) for i, e in enumerate(events)]

    segs = []
    def load(st, item, slot):
        return [Ev("w", st, a=item, b=slot, batch=affine(c)) for c in range(4)]

    def norm_of(st, group, b):
        return [Ev(kind, st, a=group, par=b % 2, batch=affine(b)) for kind in ("lnh", "lnt")]

    s0 = stages[0]
    qs, ks, vs = kv_pieces(s0, affine(0), affine(0), True, True)
    w_first = [load(s0, i, slot) for i, slot in FIRST_ITEMS]
    ln_first = [Ev("ln0", s0, a=0, par=b, batch=affine(b)) for b in range(2)] + norm_of(s0, 0, 0) + norm_of(s0, 0, 1)
    first = ln_first[:2] + w_first[0][:1] + ln_first[2:4] + w_first[0][1:2] + ln_first[4:] + w_first[0][2:] + w_first[1] + w_first[2]
    first.append(Ev("src", s0, batch=affine(0)))
    first += prologue(s0)
    segs.append((0, 1, in_turn(first)))
    ln_rest = []
    for b in range(2, B):
        t = .25 + (b - 2) * 1.2
        ln_rest.append((t, Ev("ln0", s0, a=0, par=b % 2, batch=affine(b))))
        ln_rest += [(t + .5, norm_of(s0, 0, b)[0]), (t + 1.0, norm_of(s0, 0, b)[1])]
    ln_rest += [(1.2 + c, e) for c, e in enumerate(w_first[3])]
    for st in stages:
        L = 2 * shapes[st.i].NU
        normal = pair_events(st, False)
        now = [(t, e) for t, e in normal if t < L]
        left = [(t - L, e._replace(par=e.par - 2, batch=(e.batch[0] - e.batch[1], e.batch[1]))) for t, e in normal if t >= L]
        head = [(1.2 + c * min(3.5, (L - 2.5) / 4), e) for item, slot in st.head_items for c, e in enumerate(load(st, item, slot))]
        segs.append((0, 1, now + head + (ln_rest if st.i == 0 else [])))
        segs.append((1, 3, now + left))
        final = pair_events(st, True) + left
        after = stages[st.i + 1] if st.i + 1 < len(stages) else None
        follow = prologue(after) if after else []
        qk = [e for e in follow if e.kind in ("q", "k", "zero", "mask")]
        v_first = [e for e in follow if e.kind == "v"]
        src_first = Ev("src", after, batch=affine(0)) if after else None
        bias_next = Ev("bo", st, a=st.res + 2, par=0, batch=affine(0)) if st.res + 2 < N_LN else None
        drain = L + LAG_A + .85
        if bias_next:
            final.append((drain + 5, bias_next))
        if st.i not in FFS:
            final += [(L - .5, src_first)]
            final += in_turn(qk, L + .2, FOLLOW_STEP) + in_turn(v_first, max(drain, L + .2 + FOLLOW_STEP * (len(qk) - 2)), .4)
            segs.append((3, 4, final))
            continue
        ff = FFS[st.i]
        glu = ff.value is not None

        def first_product(c, t0, step):
            out = []
            for t in range(8):
                out.append((t0 + t * step, Ev("ffg", st, a=t, b=c)))
                if glu:
                    out.append((t0 + (t + .5) * step, Ev("ffa", st, a=t, b=c)))
            return out

        def norms(c, t0, step):
            out = []
            if ff.res < N_LN - 1:
                for j in range(4):
                    lnh, lnt = norm_of(st, ff.res + 1, 4 * c + j)
                    out += [(t0 + step * j, lnh), (t0 + step * j + .6 * step, lnt)]
            return out
        final += first_product(0, drain + .02, .8)
        segs.append((3, 4, final))
        ev = []
        for n, (i, slot) in enumerate(ff.early):
            ev += [(n * 3.0 + .6 * c, e) for c, e in enumerate(load(st, i, slot))]
        for c in range(2):
            t0 = 8.0 * c
            ev += [(t0 + .1 + j, Ev("ff2", st, a=ff.res, b=j, par=j % 2, batch=affine(4 * c + j))) for j in range(4)]
            if c == 0:
                ev += first_product(1, t0 + 3.6, .5)
        ev += norms(0, 1.9, 1.0)
        if ff.res + 2 < N_LN:
            ev.append((12.5, Ev("bo", st, a=ff.res + 2, par=0, batch=affine(0))))
        ev += norms(1, 9.9, 1.0)
        if after:
            ev.append((8.3 if after.self_ else 0.0, src_first))
            ev += in_turn(qk, 12.2, .2) + in_turn(v_first, 12.3 + .2 * len(qk), .2)
        segs.append((3, 4, ev))

    def made_by(e):
        sh = shapes[e.st.i]
        b0, b1 = e.batch or (0, 0)
        if e.kind in ("q", "k"):
            n = affine(base[e.kind][e.st.i] + sh.NT * b0 + e.a + 1, sh.NT * b1)
        elif e.kind == "v":
            n = affine(base["v"][e.st.i] + sh.NV * b0 + e.a * sh.KT + e.b + 1, sh.NV * b1)
        elif e.kind in ("wo", "ff2", "lnt"):
            n = affine(8 * e.a + b0 + 1, b1)
        else:
            n = affine(16 * sorted(FFS).index(e.st.i) + 8 * e.b + e.a + 1)
        return DONE_KINDS[e.kind], n

    n0 = w0 = 0
    item_done = {}
    made = dict.fromkeys(DONE_KINDS.values(), 0)
    held = [None, None]
    for p0, p1, timed in segs:
        events = [e for _, e in sorted(timed, key=lambda x: x[0])]
        times = [t for t, _ in sorted(timed, key=lambda x: x[0])]
        looped = p1 - p0 > 1
        n = sum(e.kind in DONE_KINDS for e in events)
        w = sum(e.kind == "w" for e in events)
        made_here = {k: sum(DONE_KINDS.get(e.kind) == k for e in events) for k in made}
        assert not looped or (n % 2 == 0 and w % 2 == 0)
        ns, ws = (n, w) if looped else (0, 0)
        before = {k: affine(made[k] - made_here[k] * p0 * looped, made_here[k] * looped) for k in made}
        own = [e for e in events if e.kind in DONE_KINDS][-2:] if looped else []
        turn_before = [None, None]
        for k, e in enumerate(own):
            kind, c = made_by(e)
            turn_before[(n0 + k) % 2] = kind, affine(c[0] - c[1], c[1])
        exact = not looped or all(a == b[0] and at(b[1], p0) == a_n for (a, a_n), b in zip(held, turn_before))
        in_bank = [None, None]
        at_n = at_w = 0
        out = []
        for e, time in zip(events, times):
            num = prev = None
            if e.kind in DONE_KINDS:
                num = affine(n0 + at_n - ns * p0, ns)
                bank = num[0] % 2
                if in_bank[bank]:
                    prev = (made_by(in_bank[bank]),)
                elif exact:
                    prev = (turn_before[bank],) if looped else held[bank] and ((held[bank][0], affine(held[bank][1])),)
                elif at_n == 0:
                    prev = tuple(before.items())
                in_bank[bank] = e
                at_n += 1
            free = affine(n0 + at_n - ns * p0, ns)
            if e.kind == "w":
                num = affine(w0 + at_w - ws * p0, ws)
                at_w += 1
                item_done[e.a] = max(item_done.get(e.a, 0), w0 + at_w + ws * (p1 - 1 - p0))
            out.append((time, e._replace(n=num, seg=free, prev=prev)))
        segments.append((p0, p1, out))
        for bank in range(2):
            if in_bank[bank]:
                kind, c = made_by(in_bank[bank])
                held[bank] = kind, at(c, p1 - 1)
        n0 += n * (p1 - p0)
        w0 += w * (p1 - p0)
        for k in made:
            made[k] += made_here[k] * (p1 - p0)
    return stages, shapes, base, segments, item_done


ITEM_OF = {
    0: dict(q=0, k=1, v=2, o=3), 1: dict(q=4, k=5, v=6, o=7), 2: dict(q=11, k=12, v=13, o=14),
    3: dict(q=15, k=16, v=17, o=18), 4: dict(q=22, k=23, v=24, o=25), 5: dict(q=26, k=26, v=27, o=27),
    6: dict(q=28, k=29, v=29, o=28),
}
FF_ITEMS = {1: (8, 9, 10), 3: (19, 20, 21), 6: (None, 30, 31)}


def program(nc, x_in, ctxT, wts, lnp, bo, bff, bsm, mask_s, mask_x, out):
    F32, F32R, I32, U8 = mybir.dt.float32, mybir.dt.float32r, mybir.dt.int32, mybir.dt.uint8
    ACT, ALU, AX = mybir.ActivationFunctionType, mybir.AluOpType, mybir.AxisListType
    stages, shapes, base, segments, item_done = build_schedule()

    with ExitStack() as ctx:
        def sb(name, shape, dt=F32):
            return ctx.enter_context(nc.sbuf_tensor(name, shape, dt))

        def sem(name):
            return ctx.enter_context(nc.semaphore(name))

        x = sb("x", [T, B, C])
        hT_hi, hT_lo = sb("hT_hi", [128, 2, B * T], F32R), sb("hT_lo", [128, 2, B * T], F32R)
        W = sb("W", [128, 6, 2, 2048], F32R)
        wraw = sb("wraw", [128, 2, WQ])
        KS = sb("KS", [128, H, SP], F32R)
        V = sb("V", [128, 3, 1024])
        QH, QL = sb("QH", [128, H, PAIR], F32R), sb("QL", [128, H, PAIR], F32R)
        AOT_hi, AOT_lo = sb("AOT_hi", [128, 8, T], F32R), sb("AOT_lo", [128, 8, T], F32R)
        P = sb("P", [128, NP_, CHUNK])
        PT = sb("PT", [128, 2, CHUNK])
        src = sb("src", [128, 3 * SP], F32R)
        craw = V[:, 2, 0:2 * SP].rearrange("p (k n) -> p k n", k=2)
        cst = sb("cst", [128, 3, SP])
        hn = sb("hn", [T, 2, C])
        tmp, full = sb("tmp", [T, C]), sb("full", [128, 2, T])
        bo_b = sb("bo_b", [T, 2, C])
        mask_words = sb("mask_words", [T, 2, SP // 4], I32)
        maskf = cst[0:T, 0:2, :]
        causal = sb("causal", [T, T])
        ident = sb("ident", [128, 128])
        lnp_sb, bff_sb, bsm_sb = sb("lnp_sb", [128, N_LN, 2, 2]), sb("bff_sb", [128, 40]), sb("bsm_sb", [128, 6, 4])
        nmax, rawmax = sb("nmax", [T, NP_, 4]), sb("rawmax", [T, 4])
        rsum, rinv = sb("rsum", [T, NP_, 4]), sb("rinv", [T, NP_, 4])
        bn6, mv = sb("bn6", [T, 6]), sb("mv", [T, 2, 2])
        ve, rstd, mhalf = sb("ve", [T, 2]), sb("rstd", [T, 2]), sb("mhalf", [T, 1])
        ctx_split = nc.dram_tensor("ctx_split", [B, 128, 3 * SP], F32).ap()

        def bank(name):
            return ctx.enter_context(nc.psum_tensor(name, [128, 512], F32))
        pS = [bank("pS0"), bank("pS1")]
        pT = [bank("pT0"), bank("pT1")]
        pO = [bank("pO0"), bank("pO1")]
        pG = [bank("pG0"), bank("pG1")]

        def raw(e):
            n = e.n[0]
            if n < FIRST_CHUNKS and e.n[1] == 0:
                return n % 4, (wraw[:, n % 4, :] if n % 4 < 2 else
                               P[:, :, :].rearrange("p a n -> p (a n)")[:, (n % 4 - 2) * WQ:(n % 4 - 1) * WQ])
            return n % 2, wraw[:, n % 2, :]

        def raw_count(e):
            n, step = e.n
            if n < FIRST_CHUNKS and step == 0:
                return affine(16 * (n // 4 + 1))
            return affine(16 * ((n - FIRST_CHUNKS) // 2 + 1 + FIRST_CHUNKS // 4), 16 * (step // 2))

        consts_in = sem("consts_in")
        x_in_sem = sem("x_in_sem")
        bo_in = sem("bo_in")
        craw_in = sem("craw_in")
        ctx_out = sem("ctx_out")
        src_in = sem("src_in")
        mask_in = [sem("mask_in0"), sem("mask_in1")]
        wraw_in = [sem("wraw_in%d" % i) for i in range(4)]
        out_done = sem("out_done")
        const_ready = sem("const_ready")
        ident0 = sem("ident0")
        w_hi, w_lo = sem("w_hi"), sem("w_lo")
        ctx_hi, ctx_lo = sem("ctx_hi"), sem("ctx_lo")
        ctx_lo2 = sem("ctx_lo2")
        pieces = sem("pieces")
        scored = sem("scored")
        maxed = sem("maxed")
        masked, rawmaxed = sem("masked"), sem("rawmaxed")
        exped = sem("exped")
        recip = sem("recip")
        normed = sem("normed")
        transposed = sem("transposed")
        pt_ready = sem("pt_ready")
        attended = sem("attended")
        ao_hi, ao_lo = sem("ao_hi"), sem("ao_lo")
        q_zero = sem("q_zero")
        q_hi, q_lo, q_dup = sem("q_hi"), sem("q_lo"), sem("q_dup")
        k_hi, k_lo = sem("k_hi"), sem("k_lo")
        v_ready = sem("v_ready")
        gelu_ready, hid_ready = sem("gelu_ready"), sem("hid_ready")
        hid_hi, hid_lo = sem("hid_hi"), sem("hid_lo")
        res_tmp, x_ready = sem("res_tmp"), sem("x_ready")
        ln_stats, ln_mv = sem("ln_stats"), sem("ln_mv")
        ln_ve, ln_rstd = sem("ln_ve"), sem("ln_rstd")
        ln_h = sem("ln_h")
        hT_hi_ready, ln_full, hT_ready = sem("hT_hi_ready"), sem("ln_full"), sem("hT_ready")
        mask_f, mask_ready = sem("mask_f"), sem("mask_ready")

        block = ctx.enter_context(nc.Block())

        def unit(e, p, u=None):
            sh = shapes[e.st.i]
            u = e.a if u is None else u
            return at(affine(base["u"][e.st.i] + e.par * sh.NU + u, 2 * sh.NU), p)

        def unit_ring(e, u=None):
            return (e.a if u is None else u) % 4

        def of_batch(e, p, per):
            return at(affine(per * e.batch[0], per * e.batch[1]), p)

        def k_tiles_before(e, p):
            sh = shapes[e.st.i]
            step = sh.NT if e.st.self_ else 2 * sh.NT
            off = 0 if e.st.self_ else e.par * sh.NT
            return at(affine(base["k"][e.st.i] + off, step), p)

        def wait(eng, s, n):
            if type(n) is int and n <= 0:
                return
            eng.wait_ge(s, n)

        def wait_apart(eng, s, n):
            if type(n) is not int:
                n = eng.to_reg(n)
            elif n <= 0:
                return
            eng.wait_ge(const_ready, 1)
            eng.wait_ge(s, n)

        def side(e):
            return e.par % 2

        def v_column(e, parity):
            return 512 * parity if e.st.small and not e.st.self_ else 0

        def bank_of(e):
            return e.n[0] % 2

        def walk(eng, emit, delays={}):
            for p0, p1, timed in segments:
                events = [e for _, e in sorted(timed, key=lambda x: x[0] + delays.get(x[1].kind, 0))]
                if p1 - p0 > 1:
                    with eng.Fori(p0, p1) as p:
                        for e in events:
                            emit(e, p)
                else:
                    for e in events:
                        emit(e, p0)

        def w_view(slot, hl, col, n):
            return W[:, slot, hl, col:col + n]

        def hidden(buf):
            return buf[:, :, :].rearrange("p h n -> p (h n)")[:, 0:8 * CHUNK].rearrange("p (t n) -> p t n", t=8)

        def k_rewritable(e, p):
            st = e.st
            sh = shapes[st.i]
            if e.batch[1] == 0:
                return base["u"][st.i]
            last_unit = (e.a * sh.HPT + sh.HPT - 1) // sh.G
            if e.kind == "q" or st.self_:
                return at(affine(base["u"][st.i] + (2 * e.batch[0] - 1) * sh.NU + last_unit + 1, 2 * sh.NU), p)
            return at(affine(base["u"][st.i] + (e.batch[0] - 1) * sh.NU + last_unit + 1, 2 * sh.NU), p)

        def ff_before(st):
            done = [FFS[i].res for i in FFS if i < st.i]
            return 8 * (max(done) + 1) if done else 0

        def gelu_buf(i):
            return P[:, :, :].rearrange("p a n -> p (a n)")[:, i * CHUNK:(i + 1) * CHUNK]

        @block.sync
        def _(sp):
            sp.dma_start(lnp_sb[:, :, :, :], lnp).then_inc(consts_in, 16)
            sp.dma_start(bff_sb[:, :], bff).then_inc(consts_in, 16)
            sp.dma_start(bsm_sb[:, :, :], bsm).then_inc(consts_in, 16)
            sp.dma_start(x[:, :, :], x_in).then_inc(x_in_sem, 16)
            for i in range(2):
                sp.dma_start(bo_b[:, i, :], bo[i:i + 1, :].broadcast_to([T, C])).then_inc(bo_in, 16)

            def emit(e, p):
                st = e.st
                if e.kind == "w":
                    buf, view = raw(e)
                    wait_apart(sp, w_lo, at(e.n, p, -3 if e.n[0] < FIRST_CHUNKS and not e.n[1] else -1))
                    col = at(affine(e.batch[0] * WQ, e.batch[1] * WQ), p)
                    sp.dma_start(view, wts[e.a, :, bass.ds(col, WQ)]).then_inc(wraw_in[buf], 16)
                elif e.kind == "src":
                    wait_apart(sp, v_ready, base["v"][st.i] + of_batch(e, p, shapes[st.i].NV))
                    sh = shapes[st.i]
                    if st.self_:
                        wait_apart(sp, hT_ready, 8 * st.ln + of_batch(e, p, 1) + 1)
                        sv = src[:, 0:4 * T].bitcast(F32).rearrange("p (a k t) -> p a k t", a=2, k=2)
                        tok = of_batch(e, p, T)
                        sp.dma_start(sv[:, 0, :, :], hT_hi[:, :, bass.ds(tok, T)].bitcast(F32)).then_inc(src_in, 16)
                        sp.dma_start(sv[:, 1, :, :], hT_lo[:, :, bass.ds(tok, T)].bitcast(F32)).then_inc(src_in, 16)
                    else:
                        wait_apart(sp, k_lo, base["k"][st.i] + of_batch(e, p, sh.NT))
                        sp.wait_ge(ctx_out, 16 * (B - 1) if st.i == 1 and e.batch == affine(0) else 16 * B)
                        n = 3 * SP // 2
                        for h in range(2):
                            sp.dma_start(src[:, h * n:(h + 1) * n].bitcast(F32),
                                         ctx_split[bass.ds(of_batch(e, p, 1), 1), :, h * n:(h + 1) * n]
                                         .rearrange("a p n -> (a p) n")).then_inc(src_in, 16)
                elif e.kind == "mask":
                    words = shapes[st.i].keys // 4 if st.self_ else SP // 4
                    wait_apart(sp, maxed, base["u"][st.i] if e.batch[1] == 0 else unit(e, p, -shapes[st.i].NU))
                    msrc = mask_s if st.self_ else mask_x
                    sp.dma_start(mask_words[:, side(e), 0:words],
                                 msrc[bass.ds(of_batch(e, p, 1), 1), :].broadcast_to([T, words])).then_inc(mask_in[side(e)], 16)
                elif e.kind == "ctx":
                    b = of_batch(e, p, 1)
                    wait_apart(sp, ctx_lo, b)
                    wait_apart(sp, ctx_lo2, b)
                    sp.dma_start(craw[:, :, :], ctxT[:, bass.ds(b, 1), :, :].rearrange("p b k t -> p (b k) t")).then_inc(craw_in, 16)
                    wait_apart(sp, ctx_lo, b + 1)
                    wait_apart(sp, ctx_lo2, b + 1)
                    sp.dma_start(ctx_split[bass.ds(b, 1), :, :].rearrange("a p n -> (a p) n"),
                                 cst[:, :, :].rearrange("p a n -> p (a n)")).then_inc(ctx_out, 16)
                if e.kind == "ff2" and st.i == 6:
                    sp.wait_ge(x_ready, 8 * e.a + e.batch[0] + 1)
                    b = e.batch[0]
                    sp.dma_start(out[:, b, :], x[:, b, :]).then_inc(out_done, 16)
                if e.kind == "bo":
                    sp.wait_ge(x_ready, 8 * (e.a - 1))
                    sp.dma_start(bo_b[:, e.a % 2, :], bo[e.a:e.a + 1, :].broadcast_to([T, C])).then_inc(bo_in, 16)
            walk(sp, emit, dict(w=-1.0))
            sp.wait_ge(out_done, 16 * B)

        @block.tensor
        def _(pe):
            def mm(o, l, r, first, last):
                return nc.tensor.matmul(o, l, r, start=first, stop=last)

            def accumulate(o, passes):
                for i, (l, r) in enumerate(passes):
                    ins = mm(o, l, r, i == 0, i == len(passes) - 1)
                return ins

            done = {"q_lo": q_lo, "k_lo": k_lo, "v_ready": v_ready, "x_ready": x_ready, "hT_ready": hT_ready,
                    "gelu_ready": gelu_ready, "hid_ready": hid_ready}

            def piece_start(e, p):
                for name, n in e.prev or ():
                    if n != affine(0):
                        wait(pe, done[name], at(n, p))

            seen = set()

            def weights_ready(item):
                if item not in seen:
                    seen.add(item)
                    pe.wait_ge(w_lo, item_done[item])

            pe.wait_ge(const_ready, 1)

            def emit(e, p):
                st = e.st
                sh = shapes[st.i]
                if e.kind in ("q", "k") and (e.kind == "q" or st.self_):
                    role = st.q if e.kind == "q" else st.k
                    weights_ready(ITEM_OF[st.i][e.kind])
                    tok = of_batch(e, p, PAIR)
                    wait(pe, hT_ready, 8 * st.ln + of_batch(e, p, 2) + 2)
                    piece_start(e, p)
                    slot, col, ks = role
                    passes = []
                    for k in range(2):
                        hi = w_view(slot, 0, col + k * ks + e.a * 128, 128)
                        lo = w_view(slot, 1, col + k * ks + e.a * 128, 128)
                        ah, al = hT_hi[:, k, bass.ds(tok, PAIR)], hT_lo[:, k, bass.ds(tok, PAIR)]
                        passes += [(hi, ah), (hi, al), (lo, ah)]
                    accumulate(pG[bank_of(e)][:, 0:PAIR], passes).then_inc(pieces, 1)
                elif e.kind == "k":
                    weights_ready(ITEM_OF[st.i]["k"])
                    pe.wait_ge(src_in, 32 * 8 * st.i + of_batch(e, p, 32) + 32)
                    piece_start(e, p)
                    slot, col, ks = st.k
                    wv = [[w_view(slot, hl, col + k * ks + e.a * 128, 128) for hl in range(2)] for k in range(2)]
                    s = [src[:, i * SP:(i + 1) * SP] for i in range(3)]
                    accumulate(pG[bank_of(e)][:, 0:SP],
                               [(wv[0][0], s[0]), (wv[0][0], s[1]), (wv[0][1], s[0]), (wv[1][0], s[2]), (wv[1][1], s[2])]
                               ).then_inc(pieces, 1)
                elif e.kind == "v":
                    weights_ready(ITEM_OF[st.i]["v"])
                    pe.wait_ge(src_in, 32 * 8 * st.i + of_batch(e, p, 32) + 32)
                    piece_start(e, p)
                    slot, col, ks = st.v
                    wv = [[w_view(slot, hl, col + k * ks + e.a * 512, 512) for hl in range(2)] for k in range(2)]
                    if st.self_:
                        a = [[src[:, (hl * 2 + k) * T:(hl * 2 + k + 1) * T] for hl in range(2)] for k in range(2)]
                        passes = []
                        for k in range(2):
                            passes += [(a[k][0], wv[k][0]), (a[k][0], wv[k][1]), (a[k][1], wv[k][0])]
                    else:
                        s = [src[:, i * SP + e.b * KM:i * SP + (e.b + 1) * KM] for i in range(3)]
                        passes = [(s[0], wv[0][0]), (s[0], wv[0][1]), (s[1], wv[0][0]), (s[2], wv[1][0]), (s[2], wv[1][1])]
                    accumulate(pG[bank_of(e)][0:sh.krows, :], passes).then_inc(pieces, 1)
                elif e.kind == "scores":
                    U = unit(e, p)
                    tile = (e.a * sh.G + sh.G - 1) // sh.HPT
                    if (e.a * sh.G) % sh.HPT == 0:
                        wait(pe, q_lo, at(affine(base["q"][st.i] + tile + 1, sh.NT), p))
                        wait(pe, k_lo, k_tiles_before(e, p) + tile + 1)
                    wait(pe, exped, U - 1)
                    for g in range(sh.G):
                        h = e.a * sh.G + g
                        t = h // sh.HPT
                        qc = slice(e.par * T, (e.par + 1) * T)
                        kc = slice(e.par * T, (e.par + 1) * T) if st.self_ else slice(0, SP)
                        n = T if st.self_ else SP
                        o = pS[e.a % 2][0:T, g * T:g * T + n]
                        if st.small:
                            passes = [(QH[:, h, qc], KS[:, t, kc]), (QH[:, h, qc], KS[:, 4 + t, kc]), (QL[:, h, qc], KS[:, t, kc])]
                        else:
                            passes = [(QH[:, h, qc], KS[:, h, kc]), (QL[:, h, qc], KS[:, h, kc])]
                        ins = accumulate(o, passes)
                    ins.then_inc(scored, 1)
                elif e.kind == "trans":
                    U = unit(e, p)
                    wait(pe, normed, U + 1)
                    wait(pe, pt_ready, U - 1)
                    for i in range(sh.G * sh.KT):
                        lhsT = P[0:T, unit_ring(e), i * sh.krows:(i + 1) * sh.krows]
                        ins = nc.tensor.transpose(pT[e.a % 2][0:sh.krows, i * T:(i + 1) * T], lhsT, ident[0:T, 0:T])
                    ins.then_inc(transposed, 1)
                elif e.kind == "av":
                    U = unit(e, p)
                    pe.wait_ge(pt_ready, U + 1)
                    per = sh.NU // sh.NO
                    o = e.a // per
                    if e.a % per == 0:
                        A = at(affine(base["a"][st.i] + e.par * sh.NO + o, 2 * sh.NO), p)
                        wait(pe, ao_lo, A - 1)
                        pe.wait_ge(v_ready, at(affine(base["v"][st.i] + e.par * sh.NV + (o + 1) * sh.KT * sh.VH // sh.NO, 2 * sh.NV), p))
                    ob = pO[o if sh.NO == 2 else side(e)]
                    for g in range(sh.G):
                        h = e.a * sh.G + g
                        t = (h // sh.HPT) % 4
                        row = sh.M * (h % sh.HPT)
                        passes = []
                        vc = v_column(e, side(e))
                        for m in range(sh.KT):
                            vs = side(e) if st.self_ else m
                            pt = PT[0:sh.krows, e.a % 2, (g + m) * T:(g + m + 1) * T]
                            passes.append((V[0:sh.krows, vs, vc + h * sh.M:vc + (h + 1) * sh.M], pt))
                        ins = accumulate(ob[row:row + sh.M, t * T:(t + 1) * T], passes)
                    ins.then_inc(attended, 1)
                elif e.kind == "wo":
                    weights_ready(ITEM_OF[st.i]["o"])
                    pe.wait_ge(ao_lo, at(affine(base["a"][st.i] + (e.par + 1) * sh.NO, 2 * sh.NO), p))
                    piece_start(e, p)
                    slot, col, ks = st.o
                    passes = []
                    for t in range(sh.NT):
                        hi, lo = w_view(slot, 0, col + t * C, C), w_view(slot, 1, col + t * C, C)
                        passes += [(AOT_hi[:, t, :], hi), (AOT_hi[:, t, :], lo), (AOT_lo[:, t, :], hi)]
                    accumulate(pG[bank_of(e)][0:T, 0:C], passes).then_inc(pieces, 1)
                elif e.kind == "lnt":
                    wait(pe, ln_h, 8 * e.a + of_batch(e, p, 1) + 1)
                    piece_start(e, p)
                    for k in range(2):
                        ins = nc.tensor.transpose(pG[bank_of(e)][:, k * T:(k + 1) * T],
                                                  hn[:, side(e), k * 128:(k + 1) * 128], ident[0:T, 0:T])
                    ins.then_inc(pieces, 1)
                elif e.kind in ("ffg", "ffa"):
                    ff = FFS[st.i]
                    slot = ff.gate if e.kind == "ffg" else ff.value
                    weights_ready(FF_ITEMS[st.i][1 if e.kind == "ffg" else 0])
                    pe.wait_ge(hT_ready, 8 * ff.ln + 4 * (e.b + 1))
                    piece_start(e, p)
                    passes = []
                    for k in range(2):
                        hi, lo = w_view(slot, 0, k * 1024 + e.a * 128, 128), w_view(slot, 1, k * 1024 + e.a * 128, 128)
                        ah, al = hT_hi[:, k, e.b * CHUNK:(e.b + 1) * CHUNK], hT_lo[:, k, e.b * CHUNK:(e.b + 1) * CHUNK]
                        passes += [(hi, ah), (hi, al), (lo, ah)]
                    accumulate(pG[bank_of(e)][:, 0:CHUNK], passes).then_inc(pieces, 1)
                elif e.kind == "ff2":
                    ff = FFS[st.i]
                    weights_ready(FF_ITEMS[st.i][2])
                    k = sorted(FFS).index(st.i)
                    pe.wait_ge(hid_lo, 16 * k + 8 * (e.batch[0] // 4 + 1))
                    piece_start(e, p)
                    gh, gl = hidden(KS), hidden(QH)
                    passes = []
                    for t in range(8):
                        a = slice(e.b * T, (e.b + 1) * T)
                        hi, lo = w_view(ff.out, 0, t * C, C), w_view(ff.out, 1, t * C, C)
                        passes += [(gh[:, t, a], hi), (gh[:, t, a], lo), (gl[:, t, a], hi)]
                    accumulate(pG[bank_of(e)][0:T, 0:C], passes).then_inc(pieces, 1)
            walk(pe, emit)

        @block.scalar
        def _(act):
            act.wait_ge(consts_in, 48)

            def emit(e, p):
                st = e.st
                sh = shapes[st.i]
                g = pG[bank_of(e)] if e.n is not None and e.kind != "w" else None
                if e.kind == "q":
                    act.wait_ge(pieces, at(e.n, p, 1))
                    wait(act, scored, k_rewritable(e, p))
                    if e.batch[1] == 0:
                        wait(act, x_ready, ff_before(st))
                    if st.small:
                        act.wait_ge(q_zero, 3)
                        for i in range(4):
                            r = slice(32 * i, 32 * i + 32)
                            ins = act.activation(QH[r, 4 * e.a + i, :], g[r, 0:PAIR], ACT.Identity,
                                                 bias=bsm_sb[r, 0 if st.self_ else 3, e.a:e.a + 1])
                        ins.then_inc(q_hi, 1)
                    else:
                        act.activation(QH[0:64, 2 * e.a, :], g[0:64, 0:PAIR], ACT.Copy, scale=st.qscale)
                        act.activation(QH[64:128, 2 * e.a + 1, :], g[64:128, 0:PAIR], ACT.Copy, scale=st.qscale).then_inc(q_hi, 1)
                        act.activation(QH[0:64, 2 * e.a + 1, :], g[64:128, 0:PAIR], ACT.Copy, scale=st.qscale).then_inc(q_dup, 1)
                elif e.kind == "k":
                    n = PAIR if st.self_ else SP
                    act.wait_ge(pieces, at(e.n, p, 1))
                    wait(act, scored, k_rewritable(e, p))
                    if e.batch[1] == 0:
                        wait(act, x_ready, ff_before(st))
                    if st.small:
                        act.activation(KS[:, e.a, 0:n], g[:, 0:n], ACT.Identity,
                                       bias=bsm_sb[:, 1 if st.self_ else 4, e.a:e.a + 1]).then_inc(k_hi, 1)
                    else:
                        act.activation(KS[0:64, 2 * e.a, 0:n], g[0:64, 0:n], ACT.Copy)
                        act.activation(KS[64:128, 2 * e.a + 1, 0:n], g[64:128, 0:n], ACT.Copy).then_inc(k_hi, 1)
                elif e.kind == "v":
                    act.wait_ge(pieces, at(e.n, p, 1))
                    if e.batch[1] == 0:
                        wait(act, attended, base["u"][st.i])
                        if st.i == 1:
                            act.wait_ge(ctx_lo2, B)
                            act.wait_ge(ctx_lo, B)
                    else:
                        per = sh.NU // sh.VH
                        back = 2 if st.self_ or st.small else 1
                        c = affine(base["u"][st.i] + (e.batch[0] - back) * sh.NU + (e.a + 1) * per, 2 * sh.NU)
                        wait(act, attended, at(c, p))
                    slot = (e.batch[0] % 2) if st.self_ else e.b
                    col = e.a * 512 + v_column(e, e.batch[0] % 2)
                    act.activation(V[0:sh.krows, slot, col:col + 512], g[0:sh.krows, :], ACT.Copy).then_inc(v_ready, 1)
                elif e.kind == "scores":
                    U = unit(e, p)
                    act.wait_ge(maxed, U + 1)
                    if type(U) is int and U == 0:
                        act.wait_ge(w_lo, FIRST_CHUNKS)
                    if not st.small:
                        wait(act, transposed, U - NP_ + 1)
                    for i in range(sh.G):
                        n = sh.keys
                        o = P[0:T, unit_ring(e), i * n:(i + 1) * n]
                        s = o if st.small else pS[e.a % 2][0:T, i * n:(i + 1) * n]
                        ins = act.activation(o, s, ACT.Exp, bias=nmax[:, unit_ring(e), i:i + 1], scale=st.escale,
                                             accum_out=rsum[:, unit_ring(e), i:i + 1])
                    ins.then_inc(exped, 1)
                elif e.kind == "trans":
                    U = unit(e, p)
                    act.wait_ge(transposed, U + 1)
                    wait(act, attended, U - 1)
                    n = sh.G * sh.KT * T
                    act.activation(PT[0:sh.krows, e.a % 2, 0:n], pT[e.a % 2][0:sh.krows, 0:n], ACT.Copy).then_inc(pt_ready, 1)
                elif e.kind == "ao":
                    per = sh.NU // sh.NO
                    act.wait_ge(attended, unit(e, p, (e.a + 1) * per - 1) + 1)
                    wait(act, x_ready, 8 * st.res + of_batch(e, p, 1))
                    ob = pO[e.a if sh.NO == 2 else side(e)]
                    if st.small:
                        for t in range(4):
                            ins = act.activation(AOT_hi[:, t, :], ob[:, t * T:(t + 1) * T], ACT.Identity,
                                                 bias=bsm_sb[:, 2 if st.self_ else 5, t:t + 1])
                    else:
                        ins = act.activation(AOT_hi[:, 4 * e.a:4 * e.a + 4, :],
                                             ob[:, 0:4 * T].rearrange("p (t n) -> p t n", t=4), ACT.Copy)
                    ins.then_inc(ao_hi, 1)
                elif e.kind == "lnt":
                    act.wait_ge(pieces, at(e.n, p, 1))
                    for k in range(2):
                        ins = act.activation(hT_hi[:, k, bass.ds(of_batch(e, p, T), T)], g[:, k * T:(k + 1) * T], ACT.Identity,
                                             bias=lnp_sb[:, e.a, 1, k:k + 1], scale=lnp_sb[:, e.a, 0, k:k + 1])
                    ins.then_inc(hT_hi_ready, 1)
                elif e.kind == "ffg":
                    ff = FFS[st.i]
                    N = 16 * sorted(FFS).index(st.i) + 8 * e.b + e.a
                    act.wait_ge(pieces, at(e.n, p, 1))
                    col = ff.bias + e.a + (8 if ff.value is not None else 0)
                    if ff.value is not None:
                        wait(act, hid_ready, N - 1 if N % 16 > 1 else N - N % 16)
                        o = gelu_buf(N % 2)
                        if N % 16 < 2:
                            act.wait_ge(transposed, base["u"][st.i + 1])
                    else:
                        wait(act, hid_lo, N - 1)
                        o = PT[:, N % 2, :]
                        if N % 16 < 2:
                            act.wait_ge(attended, base["u"][st.i + 1])
                    fn = ACT.Gelu if ff.act == "erf" else ACT.Gelu_apprx_tanh
                    act.activation(o, g[:, 0:CHUNK], fn, bias=bff_sb[:, col:col + 1]).then_inc(gelu_ready, 1)
            walk(act, emit, dict(scores=0.9, trans=0.2, q=0.15, k=0.15, v=0.15, ao=0.1, lnt=0.2, ffg=0.15))

        @block.vector
        def _(dve):
            dve.wait_ge(consts_in, 48)
            dve.wait_ge(const_ready, 1)

            def split_w(e, p):
                buf, view = raw(e)
                dve.wait_ge(wraw_in[buf], at(raw_count(e), p))
                wait(dve, pieces, at(e.seg, p))
                col = at(affine(e.batch[0] * WQ, e.batch[1] * WQ), p)
                dve.tensor_copy(W[:, e.b, 0, bass.ds(col, WQ)], view).then_inc(w_hi, 1)
                if e.n[0] < FIRST_CHUNKS and not e.n[1]:
                    dve.wait_ge(w_hi, e.n[0] + 1)
                    dve.tensor_tensor(W[:, e.b, 1, bass.ds(col, WQ)], view, W[:, e.b, 0, bass.ds(col, WQ)].bitcast(F32),
                                      ALU.subtract).then_inc(w_lo, 1)

            def layer_norm(e, p, group):
                n = 8 * group + of_batch(e, p, 1)
                xb = x[:, bass.ds(of_batch(e, p, 1), 1), :].rearrange("p a n -> p (a n)")
                wait_apart(dve, ln_mv, n)
                if group:
                    wait_apart(dve, x_ready, n - 7)
                dve.bn_stats(bn6[:, :], xb).then_inc(ln_stats, 1)
                wait_apart(dve, ln_stats, n + 1)
                dve.bn_aggr(mv[:, side(e), :], bn6[:, :]).then_inc(ln_mv, 1)

            def residual(e, p, ps):
                r = 8 * e.a + of_batch(e, p, 1)
                xb = x[:, bass.ds(of_batch(e, p, 1), 1), :].rearrange("p a n -> p (a n)")
                dve.wait_ge(bo_in, 16 * (e.a + 1) if e.a else 32)
                wait(dve, x_ready, r)
                dve.tensor_tensor(tmp[0:T, :], ps, bo_b[:, e.a % 2, :], ALU.add).then_inc(res_tmp, 1)
                dve.wait_ge(res_tmp, r + 1)
                dve.tensor_tensor(xb, xb, tmp[0:T, :], ALU.add).then_inc(x_ready, 1)

            def emit(e, p):
                st = e.st
                sh = shapes[st.i]
                isp = e.n is not None and e.kind != "w"
                g = pG[bank_of(e)] if isp else None
                if e.kind == "w":
                    split_w(e, p)
                elif e.kind == "zero":
                    dve.wait_ge(scored, base["u"][st.i])
                    dve.memset(QH[:, :, :].bitcast(F32), 0.0).then_inc(q_zero, 1)
                elif e.kind == "ln0":
                    if e.batch[0] == 0:
                        dve.wait_ge(x_in_sem, 16)
                    layer_norm(e, p, 0)
                elif e.kind == "q":
                    Q = at(affine(base["q"][st.i] + sh.NT * e.batch[0] + e.a, sh.NT * e.batch[1]), p)
                    dve.wait_ge(q_hi, Q + 1)
                    if st.small:
                        for i in range(4):
                            r = slice(32 * i, 32 * i + 32)
                            ins = dve.scalar_tensor_tensor(QL[r, 4 * e.a + i, :], g[r, 0:PAIR],
                                                           bsm_sb[r, 0 if st.self_ else 3, e.a:e.a + 1],
                                                           QH[r, 4 * e.a + i, :].bitcast(F32), ALU.add, ALU.subtract)
                        ins.then_inc(q_lo, 1)
                    else:
                        D = at(affine(base["q"][st.i] + sh.NT * e.batch[0] + e.a, sh.NT * e.batch[1]), p)
                        dve.wait_ge(q_dup, D + 1)
                        if st.i == 0 and e.batch[1] == 0:
                            dve.wait_ge(q_zero, 1)
                        dve.scalar_tensor_tensor(QL[0:64, 2 * e.a, :], g[0:64, 0:PAIR], st.qscale,
                                                 QH[0:64, 2 * e.a, :].bitcast(F32), ALU.mult, ALU.subtract)
                        dve.scalar_tensor_tensor(QL[64:128, 2 * e.a + 1, :], g[64:128, 0:PAIR], st.qscale,
                                                 QH[64:128, 2 * e.a + 1, :].bitcast(F32), ALU.mult, ALU.subtract)
                        dve.tensor_copy(QH[64:128, 2 * e.a, :], QH[0:64, 2 * e.a, :].bitcast(F32)).then_inc(q_lo, 1)
                elif e.kind == "k":
                    n = PAIR if st.self_ else SP
                    K = at(affine(base["k"][st.i] + sh.NT * e.batch[0] + e.a, sh.NT * e.batch[1]), p)
                    dve.wait_ge(k_hi, K + 1)
                    if st.small:
                        dve.scalar_tensor_tensor(KS[:, 4 + e.a, 0:n], g[:, 0:n], bsm_sb[:, 1 if st.self_ else 4, e.a:e.a + 1],
                                                 KS[:, e.a, 0:n].bitcast(F32), ALU.add, ALU.subtract).then_inc(k_lo, 1)
                    else:
                        dve.tensor_tensor(KS[64:128, 2 * e.a, 0:n], g[0:64, 0:n], KS[0:64, 2 * e.a, 0:n].bitcast(F32), ALU.subtract)
                        dve.tensor_tensor(KS[0:64, 2 * e.a + 1, 0:n], g[64:128, 0:n], KS[64:128, 2 * e.a + 1, 0:n].bitcast(F32),
                                          ALU.subtract).then_inc(k_lo, 1)
                elif e.kind == "scores":
                    U = unit(e, p)
                    r = unit_ring(e)
                    (wait_apart if st.small else wait)(dve, scored, U + 1)
                    ps = pS[e.a % 2][0:T, 0:sh.G * sh.keys]
                    if not st.small:
                        if sh.G > 1:
                            ps = ps.rearrange("p (g n) -> p g n", g=sh.G)
                        dve.tensor_reduce(nmax[:, r, 0:sh.G], ps, AX.X, ALU.max, negate=True).then_inc(maxed, 1)
                    else:
                        i = U - base["u"][5]
                        if e.a == 0:
                            wait_apart(dve, mask_ready, at(affine(base["m"][st.i] + e.par + 1, 2), p))
                        wait_apart(dve, transposed, U - NP_ + 1)
                        wait_apart(dve, maxed, U)
                        po = P[0:T, r, 0:sh.G * sh.keys]
                        if st.self_:
                            po = po.rearrange("p (g n) -> p g n", g=4)
                            mk = maskf[:, side(e):side(e) + 1, 0:T].broadcast_to([T, 4, T])
                            dve.tensor_tensor(po, ps.rearrange("p (g n) -> p g n", g=4), mk, ALU.add).then_inc(masked, 1)
                            dve.wait_ge(masked, i + 1)
                            dve.tensor_reduce(rawmax[:, 0:4], po, AX.X, ALU.max).then_inc(rawmaxed, 1)
                        else:
                            dve.tensor_tensor_reduce(out=po, in0=ps, in1=maskf[:, side(e), 0:S2], scale=1.0, scalar=-3e38,
                                                     op0=ALU.add, op1=ALU.max, accum_out=rawmax[:, 0:1]).then_inc(rawmaxed, 1)
                        dve.wait_ge(rawmaxed, i + 1)
                        dve.tensor_scalar(nmax[:, r, 0:sh.G], rawmax[:, 0:sh.G], -st.escale, None, ALU.mult).then_inc(maxed, 1)
                elif e.kind == "norm":
                    U = unit(e, p)
                    dve.wait_ge(exped, U + 1)
                    r = unit_ring(e)
                    dve.reciprocal(rinv[:, r, 0:sh.G], rsum[:, r, 0:sh.G]).then_inc(recip, 1)
                elif e.kind == "ao":
                    A = at(affine(base["a"][st.i] + e.par * sh.NO + e.a, 2 * sh.NO), p)
                    dve.wait_ge(ao_hi, A + 1)
                    ob = pO[e.a if sh.NO == 2 else side(e)]
                    if st.small:
                        for t in range(4):
                            ins = dve.scalar_tensor_tensor(AOT_lo[:, t, :], ob[:, t * T:(t + 1) * T], bsm_sb[:, 2 if st.self_ else 5, t:t + 1],
                                                           AOT_hi[:, t, :].bitcast(F32), ALU.add, ALU.subtract)
                    else:
                        ins = dve.tensor_tensor(AOT_lo[:, 4 * e.a:4 * e.a + 4, :], ob[:, 0:4 * T].rearrange("p (t n) -> p t n", t=4),
                                                AOT_hi[:, 4 * e.a:4 * e.a + 4, :].bitcast(F32), ALU.subtract)
                    ins.then_inc(ao_lo, 1)
                elif e.kind in ("wo", "ff2"):
                    dve.wait_ge(pieces, at(e.n, p, 1))
                    residual(e, p, g[0:T, 0:C])
                    if e.a < N_LN - 1:
                        layer_norm(e, p, e.a + 1)
                elif e.kind == "ctx":
                    b = of_batch(e, p, 1)
                    dve.wait_ge(ctx_hi, b + 1)
                    dve.tensor_tensor(cst[64:128, 2, :].bitcast(F32R), craw[64:128, 1, :], cst[64:128, 2, :],
                                      ALU.subtract).then_inc(ctx_lo2, 1)
                elif e.kind == "lnh":
                    n = 8 * e.a + of_batch(e, p, 1)
                    xb = x[:, bass.ds(of_batch(e, p, 1), 1), :].rearrange("p a n -> p (a n)")
                    dve.wait_ge(ln_rstd, n + 1)
                    dve.tensor_scalar(hn[:, side(e), :], xb, mv[:, side(e), 0:1], rstd[:, side(e):side(e) + 1],
                                      ALU.subtract, ALU.mult).then_inc(ln_h, 1)
                elif e.kind == "lnt":
                    n = 8 * e.a + of_batch(e, p, 1)
                    dve.wait_ge(hT_hi_ready, n + 1)
                    for k in range(2):
                        ins = dve.tensor_scalar(full[:, k, :], g[:, k * T:(k + 1) * T], lnp_sb[:, e.a, 0, k:k + 1],
                                                lnp_sb[:, e.a, 1, k:k + 1], ALU.mult, ALU.add)
                    ins.then_inc(ln_full, 1)
                    dve.wait_ge(ln_full, n + 1)
                    tok = of_batch(e, p, T)
                    dve.tensor_tensor(hT_lo[:, :, bass.ds(tok, T)], full[:, :, :], hT_hi[:, :, bass.ds(tok, T)].bitcast(F32),
                                      ALU.subtract).then_inc(hT_ready, 1)
                elif e.kind in ("ffg", "ffa"):
                    ff = FFS[st.i]
                    if e.kind == "ffg" and ff.value is not None:
                        return
                    k = sorted(FFS).index(st.i)
                    N = 16 * k + 8 * e.b + e.a
                    dve.wait_ge(gelu_ready, N + 1)
                    if ff.value is not None:
                        dve.wait_ge(pieces, at(e.n, p, 1))
                        if e.b == 0 and e.a == 0:
                            dve.wait_ge(attended, base["u"][st.i + 1])
                        col = ff.bias + e.a
                        dve.scalar_tensor_tensor(PT[:, N % 2, :], g[:, 0:CHUNK], bff_sb[:, col:col + 1], gelu_buf(N % 2),
                                                 ALU.add, ALU.mult).then_inc(hid_ready, 1)
                        dve.wait_ge(hid_ready, N + 1)
                    if e.b == 0 and e.a == 0:
                        dve.wait_ge(scored, base["u"][st.i + 1])
                    if e.b == 1 and e.a == 0:
                        dve.wait_ge(x_ready, 8 * ff.res + 4)
                    hid = PT[:, N % 2, :]
                    dve.tensor_copy(hidden(KS)[:, e.a, :], hid).then_inc(hid_hi, 1)
                    dve.wait_ge(hid_hi, N + 1)
                    dve.tensor_tensor(hidden(QH)[:, e.a, :], hid, hidden(KS)[:, e.a, :].bitcast(F32), ALU.subtract).then_inc(hid_lo, 1)
            walk(dve, emit, dict(scores=0.3, norm=0.35, q=0.3, k=0.3, ao=0.45, wo=0.2, lnt=0.3, w=0.3, ffg=0.3, ffa=0.3, ff2=0.2))

        @block.gpsimd
        def _(pool):
            pool.memset(ident[:, :], 0.0).then_inc(ident0, 1)
            pool.memset(causal[:, :], 0.0).then_inc(ident0, 1)
            pool.memset(mhalf[:, :], -0.5).then_inc(ident0, 1)
            pool.wait_ge(ident0, 3)
            pool.affine_select(out=causal[:, :], in_=causal[:, :], compare_op=ALU.is_ge, fill=MASKED,
                               base=0, pattern=[[-1, T]], channel_multiplier=1).then_inc(ident0, 1)
            pool.affine_select(out=ident[:, :], in_=ident[:, :], compare_op=ALU.not_equal, fill=1.0,
                               base=0, pattern=[[-1, 128]], channel_multiplier=1).then_inc(const_ready, 1)
            pool.wait_ge(ident0, 4)
            pool.memset(QL[:, :, :].bitcast(F32), 0.0).then_inc(q_zero, 1)

            def rstd_of(e, p, group):
                n = 8 * group + of_batch(e, p, 1)
                wait_apart(pool, ln_mv, n + 1)
                pool.tensor_scalar(ve[:, side(e):side(e) + 1], mv[:, side(e), 1:2], EPS, None, ALU.add).then_inc(ln_ve, 1)
                pool.wait_ge(ln_ve, n + 1)
                pool.tensor_tensor(rstd[:, side(e):side(e) + 1], ve[:, side(e):side(e) + 1], mhalf[:, :], ALU.pow).then_inc(ln_rstd, 1)

            def emit(e, p):
                st = e.st
                sh = shapes[st.i]
                if e.kind == "zero":
                    pool.wait_ge(scored, base["u"][st.i])
                    pool.memset(QL[:, :, :].bitcast(F32), 0.0).then_inc(q_zero, 1)
                elif e.kind == "w":
                    buf = e.n[0] % 2
                    if e.n[0] < FIRST_CHUNKS and not e.n[1]:
                        return
                    wait_apart(pool, w_hi, at(e.n, p, 1))
                    col = at(affine(e.batch[0] * WQ, e.batch[1] * WQ), p)
                    pool.tensor_tensor(W[:, e.b, 1, bass.ds(col, WQ)], wraw[:, buf, :],
                                       W[:, e.b, 0, bass.ds(col, WQ)].bitcast(F32), ALU.subtract).then_inc(w_lo, 1)
                elif e.kind == "norm":
                    U = unit(e, p)
                    r = unit_ring(e)
                    wait_apart(pool, recip, U + 1)
                    for i in range(sh.G):
                        n = sh.keys
                        o = P[0:T, r, i * n:(i + 1) * n]
                        ins = pool.tensor_scalar(o, o, rinv[:, r, i:i + 1], st.nscale, ALU.mult, ALU.mult)
                    ins.then_inc(normed, 1)
                elif e.kind == "ln0":
                    rstd_of(e, p, 0)
                elif e.kind in ("wo", "ff2") and e.a < N_LN - 1:
                    rstd_of(e, p, e.a + 1)
                elif e.kind == "ctx":
                    b = of_batch(e, p, 1)
                    wait_apart(pool, craw_in, 16 * b + 16)
                    wait_apart(pool, ctx_out, 16 * b)
                    for i in range(2):
                        ins = pool.tensor_scalar(cst[:, 2 * i, :].bitcast(F32R), craw[:, i, :], 1.0, 1.0, ALU.mult, ALU.mult)
                    ins.then_inc(ctx_hi, 1)
                    wait_apart(pool, ctx_hi, b + 1)
                    pool.tensor_tensor(cst[:, 1, :].bitcast(F32R), craw[:, 0, :], cst[:, 0, :], ALU.subtract).then_inc(ctx_lo, 1)
                elif e.kind == "mask":
                    m = at(affine(base["m"][st.i] + e.batch[0], e.batch[1]), p)
                    keys = sh.keys
                    wait_apart(pool, mask_in[side(e)], at(affine(8 * base["m"][st.i] + 16 * (e.par // 2 + 1), 16 * (e.batch[1] // 2)), p))
                    wait_apart(pool, maxed, base["u"][st.i] if e.batch[1] == 0 else unit(e, p, -sh.NU))
                    mf = maskf[:, side(e), 0:keys]
                    ins = pool.tensor_scalar(mf, mask_words[:, side(e), :].bitcast(U8)[:, 0:keys], MASKED, 1.0, ALU.mult, ALU.mult).then_inc(mask_f, 1)
                    wait_apart(pool, mask_f, m + 1)
                    if st.self_:
                        pool.tensor_tensor(mf, mf, causal[:, :], ALU.add).then_inc(mask_ready, 1)
                    else:
                        pool.tensor_scalar(mf, mf, 1.0, 1.0, ALU.mult, ALU.mult).then_inc(mask_ready, 1)
            walk(pool, emit, dict(norm=0.4, wo=0.5, ff2=0.5, w=0.3))


def pack_weights(g):
    def k256(w):
        return w.reshape(2, 128, 1024).transpose(1, 0, 2).reshape(128, 2048)

    def k192(w):
        return np.concatenate([w[:128], np.concatenate([w[128:], w[128:]], 0)], 1)

    def o1024(w):
        return w.reshape(8, 128, 256).transpose(1, 0, 2).reshape(128, 2048)

    def pad_heads(w):
        k = w.shape[0]
        return np.concatenate([w.reshape(k, 16, 16), np.zeros((k, 16, 16), w.dtype)], 2).reshape(k, 512)

    def pad_rows(w):
        return np.concatenate([w.reshape(16, 16, 256), np.zeros((16, 16, 256), w.dtype)], 1).reshape(4, 128, 256) \
            .transpose(1, 0, 2).reshape(128, 1024)

    def tiles(w):
        return w.reshape(2, 128, w.shape[1]).transpose(1, 0, 2).reshape(128, 2 * w.shape[1])

    L0, L1, L2, L3 = ("L%d_xattn_" % i for i in range(4))
    qkv = g[L3 + "qkv_w"]
    items = [k256(g[L0 + "Wq1"]), k256(g[L0 + "Wk1"]), k256(g[L0 + "Wv1"]), o1024(g[L0 + "Wo1"]),
             k256(g[L0 + "Wq2"]), k192(g[L0 + "Wk2"]), k192(g[L0 + "Wv2"]), o1024(g[L0 + "Wo2"]),
             k256(g[L0 + "Wp"][:, :1024]), k256(g[L0 + "Wp"][:, 1024:]), o1024(g[L0 + "Wf"]),
             k256(g[L1 + "wq1"]), k256(g[L1 + "wk1"]), k256(g[L1 + "wv1"]), o1024(g[L1 + "wo1"]),
             k256(g[L1 + "wq2"]), k192(g[L1 + "wk2"]), k192(g[L1 + "wv2"]), o1024(g[L1 + "wo2"]),
             k256(g[L1 + "w_ff1"][:, :1024]), k256(g[L1 + "w_ff1"][:, 1024:]), o1024(g[L1 + "w_ff2"]),
             k256(g[L2 + "Wq"]), k192(g[L2 + "Wk"]), k192(g[L2 + "Wv"]), o1024(g[L2 + "Wo"]),
             k256(np.concatenate([pad_heads(qkv[:, :256]), pad_heads(qkv[:, 256:512])], 1)),
             np.concatenate([tiles(pad_heads(qkv[:, 512:])), pad_rows(g[L3 + "proj_w"])], 1),
             np.concatenate([tiles(pad_heads(g[L3 + "q_w"])), pad_rows(g[L3 + "out_w"])], 1),
             np.concatenate([k192(pad_heads(g[L3 + "k_w"])), k192(pad_heads(g[L3 + "v_w"]))], 1),
             k256(g[L3 + "mlp1_w"]), o1024(g[L3 + "mlp2_w"])]
    return np.stack(items)


def kernel(**inputs):
    import concourse.bacc as bacc
    from concourse.bass_utils import run_bass_kernel_spmd

    g = {k: np.asarray(v) for k, v in inputs.items()}
    L0, L1, L2, L3 = ("L%d_xattn_" % i for i in range(4))

    def cols(v):
        return v.reshape(-1, 128).T

    def small(v):
        return cols(np.concatenate([v.reshape(16, 16), np.zeros((16, 16), v.dtype)], 1).reshape(512))

    def words(m):
        m = np.ascontiguousarray(m).view(np.uint8)
        return np.concatenate([m, np.zeros((B, -m.shape[1] % 4), np.uint8)], 1).view(np.int32)

    norms = [(L0 + "g1", L0 + "b1"), (L0 + "g2", L0 + "b2"), (L0 + "g3", L0 + "b3"),
             (L1 + "ln1_g", L1 + "ln1_b"), (L1 + "ln2_g", L1 + "ln2_b"), (L1 + "ln3_g", L1 + "ln3_b"),
             (L2 + "gamma", L2 + "beta"), (L3 + "ln1_w", L3 + "ln1_b"), (L3 + "ln2_w", L3 + "ln2_b"), (L3 + "ln3_w", L3 + "ln3_b")]
    lnp = np.stack([np.stack([cols(g[a]), cols(g[b])]) for a, b in norms]).transpose(2, 0, 1, 3)
    bo = np.stack([g[n] for n in (L0 + "bo1", L0 + "bo2", L0 + "bf", L1 + "bo1", L1 + "bo2", L1 + "b_ff2", L2 + "bo",
                                  L3 + "proj_b", L3 + "out_b", L3 + "mlp2_b")])
    bff = np.concatenate([cols(g[L0 + "bp"]), cols(g[L1 + "b_ff1"]), cols(g[L3 + "mlp1_b"])], 1)
    qkv_b = g[L3 + "qkv_b"]
    bsm = np.stack([small(v) for v in (qkv_b[:256], qkv_b[256:512], qkv_b[512:], g[L3 + "q_b"], g[L3 + "k_b"], g[L3 + "v_b"])], 1)
    c = g["ctx_768"]
    c = np.concatenate([c, np.zeros((B, SP - S2, E), c.dtype)], 1).transpose(2, 0, 1)
    ctxT = np.stack([c[:128], np.concatenate([c[128:], c[128:]], 0)], 2)
    arrays = {
        "x_in": g["x"].transpose(1, 0, 2), "ctxT": ctxT, "wts": pack_weights(g), "lnp": lnp, "bo": bo, "bff": bff,
        "bsm": bsm, "mask_s": words(g["mask_BxS_bf0"]), "mask_x": words(g["mask_BxS2_bf0"]),
    }
    arrays = {k: np.ascontiguousarray(v) for k, v in arrays.items()}
    nc = bacc.Bacc("TRN2", target_bir_lowering=False, num_devices=1, dynamic_dma_scratch_size=1024)
    aps = [nc.dram_tensor(k, v.shape, mybir.dt.from_np(v.dtype), kind="ExternalInput").ap() for k, v in arrays.items()]
    out = nc.dram_tensor("out", (T, B, C), mybir.dt.float32, kind="ExternalOutput").ap()
    program(nc, *aps, out)
    r = run_bass_kernel_spmd(nc, [arrays], core_ids=[0])
    return np.ascontiguousarray(r.results[0]["out"].transpose(1, 0, 2))
```

```python
from collections import namedtuple
from contextlib import ExitStack

import numpy as np

import concourse.bass as bass
from concourse import mybir

B, T, C = 8, 112, 256
S2, E = 375, 192
SP = S2 + 1
KM = S2 // 3
H = 16
PAIR = 2 * T
NPAIR = B // 2
CHUNK = 4 * T
EPS = 1e-5
MASKED = -1e38
NP_, WQ = 4, 512

TIMES = {
    (True, False): dict(
        LT=3, LA=4, trans=0.4, wo=1.1, lnh=2.5, lnt=3.1, q=0.7, k=-0.1, step=0.65, v=-0.1, v_step=1.4,
        follow=0.5, v_first=0.4, ahead=7.9, ahead_direct=8, before=0.9, open_step=0.2, v_head=1.9,
        v_head_step=0.3,
        act=dict(scores=0.9, trans=0.2, q=0.45, k=0.85, qk=0.15, v=0.15, ao=0.1, lnt=0.2, w=0.15, ffg=0.65),
        dve=dict(scores=0.3, norm=0.1, q=-0.4, k=0.2, qk=0.3, ao=0.45, wo=0.2, lnt=0.2, w=0.3, ffg=0.3, ffa=0.5, ff2=0.2),
        pool=dict(norm=-0.1, wo=0.5, ff2=1.5, k=0.25, qk=0.25),
        sp=dict(w=-1),
        pe=dict(),),
    (False, False): dict(
        LT=3, LA=4, trans=0.4, wo=1.1, lnh=2.5, lnt=3.1, q=1.2, k=-0.8, step=0.45, v=9.6, v_step=1.35,
        follow=0.4, v_first=0.8, ahead=2, ahead_direct=8.5, before=99, open_step=0.7, v_head=3.3,
        v_head_step=0.4,
        act=dict(scores=0.9, trans=0.2, q=0.15, k=0.15, qk=0.15, v=0.15, ao=0.1, lnt=0.2, w=0.15, ffg=0.15),
        dve=dict(scores=0.3, norm=0.35, q=0.3, k=0.3, qk=0.1, ao=0.45, wo=0.35, lnt=0.3, w=0.3, ffg=1, ffa=0.3, ff2=0.5),
        pool=dict(norm=0.3, wo=0.5, ff2=1.5, k=1.25, qk=0.25),
        sp=dict(w=-1),
        pe=dict(),),
    (True, True): dict(
        LT=2, LA=3, trans=0.1, wo=1.6, lnh=2.5, lnt=3.1, q=0.7, k=-0.6, step=1, v=1.2, v_step=0.5,
        follow=0.4, v_first=0.4, ahead=7, ahead_direct=8.3, before=0.9, open_step=0.3, v_head=1.4,
        v_head_step=1.3,
        act=dict(scores=0.9, trans=0.2, q=-0.35, k=1.25, qk=-0.15, v=0.15, ao=0.1, lnt=0.2, w=0.15, ffg=0.25),
        dve=dict(scores=0.3, norm=0.25, q=0.3, k=1.3, qk=0.3, ao=0.45, wo=0.2, lnt=0.3, w=0.3, ffg=0.3, ffa=0.3, ff2=0.2),
        pool=dict(norm=0.4, wo=0.5, ff2=0.5, k=-0.05, qk=0.25),
        sp=dict(w=-1),
        pe=dict(),),
    (False, True): dict(
        LT=3, LA=4, trans=0.4, wo=1.1, lnh=2.3, lnt=3.1, q=1.2, k=0.2, step=1.05, v=8.6, v_step=2,
        follow=0.4, v_first=0.4, ahead=2, ahead_direct=8, before=99, open_step=0.7, v_head=3.3,
        v_head_step=-0.4,
        act=dict(scores=1.05, trans=0, q=-0.05, k=0.2, qk=0.15, v=-0.15, ao=0.1, lnt=0.2, w=0.15, ffg=0.15),
        dve=dict(scores=0.1, norm=0.35, q=0.6, k=0.3, qk=0, ao=0.45, wo=0.1, lnt=0.3, w=0.3, ffg=1, ffa=-0.2, ff2=0.1),
        pool=dict(norm=0.4, wo=-0.1, ff2=0.5, k=0.25, qk=-0.75),
        sp=dict(w=-1),
        pe=dict(),),
}
FF_TIMES = dict(first_step=0.8, second_start=3.3, second_step=0.5, norm=1.9, norm_t=0.6, qk=12.4, qk_step=0.2)

Stage = namedtuple("Stage", "i self_ small ln res q k v o head_items loop_items end_items qscale escale nscale")


def make_stages():
    W = 1024
    L0s = dict(i=0, self_=True, small=False, ln=0, res=0, q=(0, 0, W), k=(1, 0, W), v=(2, 0, W), o=(3, 0, C),
               loop_items=((5, 4), (6, 5)), end_items=((4, 0),), qscale=0.125, escale=1.0, nscale=1.0)
    L0c = dict(i=1, self_=False, small=False, ln=1, res=1, q=(0, 0, W), k=(4, 0, W), v=(5, 0, W), o=(1, 0, C),
               loop_items=((8, 2), (9, 3)), end_items=((10, 0),), qscale=0.125, escale=1.0, nscale=1.0)
    L1s = dict(i=2, self_=True, small=False, ln=3, res=3, q=(4, 0, W), k=(5, 0, W), v=(1, 0, W), o=(2, 0, C),
               loop_items=((16, 0), (17, 3)), end_items=((15, 4),), qscale=0.125, escale=1.0, nscale=1.0)
    L1c = dict(i=3, self_=False, small=False, ln=4, res=4, q=(4, 0, W), k=(0, 0, W), v=(3, 0, W), o=(5, 0, C),
               loop_items=((19, 1), (20, 2)), end_items=((21, 4),), qscale=0.125, escale=1.0, nscale=1.0)
    L2c = dict(i=4, self_=False, small=False, ln=6, res=6, q=(0, 0, W), k=(3, 0, W), v=(5, 0, W), o=(1, 0, C),
               loop_items=((26, 2), (27, 4)), end_items=(), qscale=1.0, escale=1.0, nscale=0.125)
    L3s = dict(i=5, self_=True, small=True, ln=7, res=7, q=(2, 0, W), k=(2, 512, W), v=(4, 0, 512), o=(4, 1024, C),
               loop_items=((29, 3), (28, 0)), end_items=(), qscale=1.0, escale=0.25, nscale=1.0)
    L3c = dict(i=6, self_=False, small=True, ln=8, res=8, q=(0, 0, 512), k=(3, 0, 512), v=(3, 1024, 512),
               o=(0, 1024, C), loop_items=((30, 5), (31, 1)), end_items=(), qscale=1.0, escale=0.25, nscale=1.0)
    head = {1: ((7, 1),), 2: ((14, 2),), 3: ((18, 5),), 4: ((25, 1),)}
    return [Stage(head_items=head.get(s["i"], ()), **s) for s in (L0s, L0c, L1s, L1c, L2c, L3s, L3c)]


FF = namedtuple("FF", "value gate out ln res bias act early")
FFS = {
    1: FF(2, 3, 0, 2, 2, 0, "erf", ((11, 4), (12, 5), (13, 1))),
    3: FF(1, 2, 4, 5, 5, 16, "tanh", ((22, 0), (23, 3), (24, 5))),
    6: FF(None, 5, 1, 9, 9, 32, "erf", ()),
}
FIRST_ITEMS = ((0, 0), (1, 1), (2, 2), (3, 3))
FIRST_CHUNKS = 12
N_LN = 10

Ev = namedtuple("Ev", "kind st a b par batch n seg prev", defaults=(None,) * 7)


def affine(c0, c1=0):
    return (c0, c1)


def at(c, p, plus=0):
    return c[0] + plus + c[1] * p if c[1] else c[0] + plus


DONE_KINDS = {"q": "q_lo", "qk": "k_lo", "k": "k_lo", "v": "v_ready", "wo": "x_ready", "ff2": "x_ready", "lnt": "hT_ready",
              "ffg": "gelu_ready", "ffa": "hid_ready"}


class Shape:

    def __init__(self, st):
        self.G = 4 if st.self_ else 1
        self.NU = H // self.G
        self.HPT = 4 if st.small else 2
        self.NT = H // self.HPT
        self.M = 32 if st.small else 64
        self.keys = T if st.self_ else S2
        self.KT = 1 if st.self_ else 3
        self.krows = T if st.self_ else KM
        self.VH = H * self.M // 512
        self.NV = self.VH * self.KT
        self.NO = 1 if st.small else 2


def build_schedule():
    stages = make_stages()
    shapes = [Shape(s) for s in stages]
    base = {"u": [0], "k": [0], "q": [0], "v": [0], "a": [0], "m": [0]}
    for s, sh in zip(stages, shapes):
        base["u"].append(base["u"][-1] + B * sh.NU)
        base["k"].append(base["k"][-1] + sh.NT * (NPAIR if s.self_ else B))
        base["q"].append(base["q"][-1] + sh.NT * NPAIR)
        base["v"].append(base["v"][-1] + sh.NV * B)
        base["a"].append(base["a"][-1] + sh.NO * B)
        base["m"].append(base["m"][-1] + (B if s.small else 0))

    def first_pieces(st):
        sh = shapes[st.i]
        b0 = affine(0)
        qs = [Ev("qk" if st.self_ else "q", st, a=t, batch=b0) for t in range(sh.NT)]
        ks = [] if st.self_ else [Ev("k", st, a=t, batch=b0) for t in range(sh.NT)]
        vs = [Ev("v", st, a=hf, b=m, batch=b0) for hf in range(sh.VH) for m in range(sh.KT)]
        return qs, ks, vs

    def time_of(st):
        return TIMES[st.self_, st.small]

    def pair_events(st, last):
        sh = shapes[st.i]
        tm = time_of(st)
        out = []

        def put(time, kind, **kw):
            out.append((time, Ev(kind, st, **kw)))
        for par in range(2):
            t0 = par * sh.NU
            me, nxt, nxt_pair = affine(par, 2), affine(par + 1, 2), affine(1, 1)
            for u in range(sh.NU):
                put(t0 + u, "scores", a=u, par=par, batch=me)
                put(t0 + u + 1, "norm", a=u, par=par, batch=me)
                put(t0 + u + tm["LT"] + tm["trans"], "trans", a=u, par=par, batch=me)
                put(t0 + u + tm["LA"] + .8, "av", a=u, par=par, batch=me)
                per = sh.NU // sh.NO
                if u % per == per - 1:
                    put(t0 + u + tm["LA"] + .85, "ao", a=u // per, par=par, batch=me)
            end = t0 + sh.NU - 1 + tm["LA"]
            put(end + 1 + tm["wo"], "wo", a=st.res, b=st.res < N_LN - 1, par=par, batch=me)
            put(end + 1 + tm["lnh"], "lnh", a=st.res + 1, par=par, batch=me)
            put(end + 1 + tm["lnt"], "lnt", a=st.res + 1, par=par, batch=me)
            if st.i == 0:
                put(t0 + 1.5, "ctx", par=par, batch=me)
            if not (last and par == 1):
                put(t0 + (tm["LA"] - 2 if st.self_ else tm["LA"] + 3), "src", par=par, batch=nxt)
                if st.small:
                    put(t0 + sh.NU / 2, "mask", par=par + 1, batch=nxt)
                if st.self_:
                    for hf in range(sh.VH):
                        put(t0 + tm["LA"] + tm["v"] + tm["v_step"] * hf, "v", a=hf, b=0, par=par, batch=nxt)
                else:
                    for t in range(sh.NT):
                        ready = (t + 1) * sh.HPT - 1 + tm["k"]
                        at_ = max(ready, tm["LA"] + 4.2 + t) if sh.NT == 8 else ready
                        put(t0 + at_, "k", a=t, par=par, batch=nxt)
                    for m in range(sh.KT):
                        if st.small:
                            put(t0 + tm["v"] + tm["v_step"] * m, "v", a=0, b=m, par=par, batch=nxt)
                        else:
                            put(t0 + tm["LA"] + tm["v"] + tm["v_step"] * m, "v", a=0, b=m, par=par, batch=nxt)
                            put(end + .9 + m, "v", a=1, b=m, par=par, batch=nxt)
            if par == 1 and not last:
                for t in range(sh.NT):
                    if not st.self_:
                        put(t0 + (t + 1) * sh.HPT - 1 + tm["q"], "q", a=t, par=par, batch=nxt_pair)
                    else:
                        put(t0 + tm["q"] + tm["step"] * t, "qk", a=t, par=par, batch=nxt_pair)
        for n, (i, slot) in enumerate(st.loop_items):
            put(sh.NU / 4 + n * sh.NU / 2, "w", a=i, b=slot, par=0, batch=affine(0, 1))
        if last:
            n = len(st.end_items) * 4
            for m, (i, slot) in enumerate((i, c) for i in st.end_items for c in range(4)):
                put(tm["LA"] + 1 + m * (2 * sh.NU - tm["LA"] - 2) / n, "w", a=i[0], b=i[1], par=0, batch=affine(slot))
        return out

    segments = []

    def opening(st, direct):
        sh, tm = shapes[st.i], time_of(st)
        qs, ks, vs = first_pieces(st)
        early, late = [], []
        for t in range(sh.NT):
            tile = [e for e in qs + ks if e.a == t]
            if t < (tm["ahead_direct"] if direct else tm["ahead"]):
                early += tile
            else:
                due = t * sh.HPT // sh.G
                late += [(max(due - tm["before"], .05 + tm["open_step"] * t) + .15 * n, e) for n, e in enumerate(tile)]
        if direct:
            early += vs
        else:
            late += [(tm["v_head"] + tm["v_head_step"] * n, e) for n, e in enumerate(vs)]
        return early, late

    def preparations(st):
        zero = [Ev("zero", st, batch=affine(0))] if st.small and st.self_ else []
        mask = [Ev("mask", st, par=0, batch=affine(0))] if st.small else []
        return zero + mask

    def in_turn(events, t0=0.0, step=1.0):
        return [(t0 + step * i, e) for i, e in enumerate(events)]

    segs = []
    def load(st, item, slot):
        return [Ev("w", st, a=item, b=slot, batch=affine(c)) for c in range(4)]

    def norm_of(st, group, b):
        return [Ev(kind, st, a=group, par=b % 2, batch=affine(b)) for kind in ("lnh", "lnt")]

    s0 = stages[0]
    w_first = [load(s0, i, slot) for i, slot in FIRST_ITEMS]
    (lnh0, lnt0), (lnh1, lnt1) = norm_of(s0, 0, 0), norm_of(s0, 0, 1)
    w012 = w_first[0] + w_first[1] + w_first[2]
    first = [Ev("ln0", s0, a=0, par=b, batch=affine(b)) for b in range(2)] + [w012[0], lnh0, lnh1, w012[1], lnt0, *w012[2:5], lnt1, *w012[5:]]
    first.append(Ev("src", s0, batch=affine(0)))
    early, opening_late = opening(s0, False)
    first += early
    segs.append((0, 1, in_turn(first)))
    ln_rest = []
    for b in range(2, B):
        t = .25 + (b - 2) * 1.2
        ln_rest.append((t, Ev("ln0", s0, a=0, par=b % 2, batch=affine(b))))
        ln_rest += [(t + .5, norm_of(s0, 0, b)[0]), (t + 1.0, norm_of(s0, 0, b)[1])]
    ln_rest += [(1.2 + c, e) for c, e in enumerate(w_first[3])]
    for st in stages:
        L = 2 * shapes[st.i].NU
        normal = pair_events(st, False)
        now = [(t, e) for t, e in normal if t < L]
        left = [(t - L, e._replace(par=e.par - 2, batch=(e.batch[0] - e.batch[1], e.batch[1]))) for t, e in normal if t >= L]
        head = [(1.2 + c * min(3.5, (L - 2.5) / 4), e) for item, slot in st.head_items for c, e in enumerate(load(st, item, slot))]
        segs.append((0, 1, now + head + opening_late + (ln_rest if st.i == 0 else [])))
        segs.append((1, 3, now + left))
        final = pair_events(st, True) + left
        after = stages[st.i + 1] if st.i + 1 < len(stages) else None
        direct = st.i not in FFS
        follow, opening_late = opening(after, direct) if after else ([], [])
        follow = (preparations(after) if after else []) + follow
        qk = [e for e in follow if e.kind in ("qk", "q", "k", "zero", "mask")]
        v_first = [e for e in follow if e.kind == "v"]
        src_first = Ev("src", after, batch=affine(0)) if after else None
        bias_next = Ev("bo", st, a=st.res + 2, par=0, batch=affine(0)) if st.res + 2 < N_LN else None
        drain = L + time_of(st)["LA"] + .85
        if bias_next:
            final.append((drain + 5, bias_next))
        if direct:
            final += [(L - .5, src_first)]
            step = time_of(st)["follow"]
            final += in_turn(qk, L + .2, step) + in_turn(v_first, max(drain, L + .2 + step * (len(qk) - 2)), time_of(st)["v_first"])
            segs.append((3, 4, final))
            continue
        ff = FFS[st.i]
        glu = ff.value is not None

        def first_product(c, t0, step):
            out = []
            for t in range(8):
                out.append((t0 + t * step, Ev("ffg", st, a=t, b=c)))
                if glu:
                    out.append((t0 + (t + .5) * step, Ev("ffa", st, a=t, b=c)))
            return out

        def norms(c, t0, step):
            out = []
            if ff.res < N_LN - 1:
                for j in range(4):
                    lnh, lnt = norm_of(st, ff.res + 1, 4 * c + j)
                    out += [(t0 + step * j, lnh), (t0 + step * j + FF_TIMES["norm_t"], lnt)]
            return out
        final += first_product(0, drain + .02, FF_TIMES["first_step"])
        segs.append((3, 4, final))
        ev = []
        for n, (i, slot) in enumerate(ff.early):
            ev += [(n * 3.0 + .6 * c, e) for c, e in enumerate(load(st, i, slot))]
        for c in range(2):
            t0 = 8.0 * c
            ev += [(t0 + .1 + j, Ev("ff2", st, a=ff.res, b=j, par=j % 2, batch=affine(4 * c + j))) for j in range(4)]
            if c == 0:
                ev += first_product(1, t0 + FF_TIMES["second_start"], FF_TIMES["second_step"])
        ev += norms(0, FF_TIMES["norm"], 1.0)
        if ff.res + 2 < N_LN:
            ev.append((12.5, Ev("bo", st, a=ff.res + 2, par=0, batch=affine(0))))
        ev += norms(1, 8 + FF_TIMES["norm"], 1.0)
        if after:
            ev.append((8.3 if after.self_ else 0.0, src_first))
            ev += in_turn(qk, FF_TIMES["qk"], FF_TIMES["qk_step"]) + in_turn(v_first, FF_TIMES["qk"] + .1 + FF_TIMES["qk_step"] * len(qk), .2)
        segs.append((3, 4, ev))

    def made_by(e):
        sh = shapes[e.st.i]
        b0, b1 = e.batch or (0, 0)
        if e.kind in ("q", "k", "qk"):
            n = affine(base[e.kind[-1]][e.st.i] + sh.NT * b0 + e.a + 1, sh.NT * b1)
        elif e.kind == "v":
            n = affine(base["v"][e.st.i] + sh.NV * b0 + e.a * sh.KT + e.b + 1, sh.NV * b1)
        elif e.kind in ("wo", "ff2", "lnt"):
            n = affine(8 * e.a + b0 + 1, b1)
        else:
            n = affine(16 * sorted(FFS).index(e.st.i) + 8 * e.b + e.a + 1)
        return DONE_KINDS[e.kind], n

    n0 = w0 = 0
    item_done = {}
    made = dict.fromkeys(DONE_KINDS.values(), 0)
    held = [None, None]
    for p0, p1, timed in segs:
        events = [e for _, e in sorted(timed, key=lambda x: x[0])]
        times = [t for t, _ in sorted(timed, key=lambda x: x[0])]
        looped = p1 - p0 > 1
        n = sum(e.kind in DONE_KINDS for e in events)
        w = sum(e.kind == "w" for e in events)
        made_here = {k: sum(DONE_KINDS.get(e.kind) == k for e in events) for k in made}
        assert not looped or (n % 2 == 0 and w % 2 == 0)
        ns, ws = (n, w) if looped else (0, 0)
        before = {k: affine(made[k] - made_here[k] * p0 * looped, made_here[k] * looped) for k in made}
        own = [e for e in events if e.kind in DONE_KINDS][-2:] if looped else []
        turn_before = [None, None]
        for k, e in enumerate(own):
            kind, c = made_by(e)
            turn_before[(n0 + k) % 2] = kind, affine(c[0] - c[1], c[1])
        exact = not looped or all(a == b[0] and at(b[1], p0) == a_n for (a, a_n), b in zip(held, turn_before))
        in_bank = [None, None]
        at_n = at_w = 0
        out = []
        for e, time in zip(events, times):
            num = prev = None
            if e.kind in DONE_KINDS:
                num = affine(n0 + at_n - ns * p0, ns)
                bank = num[0] % 2
                if in_bank[bank]:
                    prev = (made_by(in_bank[bank]),)
                elif exact:
                    prev = (turn_before[bank],) if looped else held[bank] and ((held[bank][0], affine(held[bank][1])),)
                elif at_n == 0:
                    prev = tuple(before.items())
                in_bank[bank] = e
                at_n += 1
            free = affine(n0 + at_n - ns * p0, ns)
            if e.kind == "w":
                num = affine(w0 + at_w - ws * p0, ws)
                at_w += 1
                item_done[e.a] = max(item_done.get(e.a, 0), w0 + at_w + ws * (p1 - 1 - p0))
            out.append((time, e._replace(n=num, seg=free, prev=prev)))
        segments.append((p0, p1, out))
        for bank in range(2):
            if in_bank[bank]:
                kind, c = made_by(in_bank[bank])
                held[bank] = kind, at(c, p1 - 1)
        n0 += n * (p1 - p0)
        w0 += w * (p1 - p0)
        for k in made:
            made[k] += made_here[k] * (p1 - p0)
    return stages, shapes, base, segments, item_done


ITEM_OF = {
    0: dict(q=0, k=1, v=2, o=3), 1: dict(q=4, k=5, v=6, o=7), 2: dict(q=11, k=12, v=13, o=14),
    3: dict(q=15, k=16, v=17, o=18), 4: dict(q=22, k=23, v=24, o=25), 5: dict(q=26, k=26, v=27, o=27),
    6: dict(q=28, k=29, v=29, o=28),
}
FF_ITEMS = {1: (8, 9, 10), 3: (19, 20, 21), 6: (None, 30, 31)}


def program(nc, x_in, ctxT, wts, lnp, bo, bff, bsm, lo_rows, mask_s, mask_x, out):
    F32, F32R, I32, U8 = mybir.dt.float32, mybir.dt.float32r, mybir.dt.int32, mybir.dt.uint8
    ACT, ALU, AX = mybir.ActivationFunctionType, mybir.AluOpType, mybir.AxisListType
    stages, shapes, base, segments, item_done = build_schedule()

    with ExitStack() as ctx:
        def sb(name, shape, dt=F32):
            return ctx.enter_context(nc.sbuf_tensor(name, shape, dt))

        def sem(name):
            return ctx.enter_context(nc.semaphore(name))

        x = sb("x", [T, B, C])
        hT_hi, hT_lo = sb("hT_hi", [128, 2, B * T], F32R), sb("hT_lo", [128, 2, B * T], F32R)
        W = sb("W", [128, 6, 2, 2048], F32R)
        wraw = sb("wraw", [128, 2, WQ])
        KS = sb("KS", [128, H, SP], F32R)
        V = sb("V", [128, 3, 1024])
        QH, QL = sb("QH", [128, H, PAIR], F32R), sb("QL", [128, H, PAIR], F32R)
        AOT_hi, AOT_lo = sb("AOT_hi", [128, 8, T], F32R), sb("AOT_lo", [128, 8, T], F32R)
        P = sb("P", [128, NP_, CHUNK])
        PT = sb("PT", [128, 2, CHUNK])
        src = sb("src", [128, 3 * SP], F32R)
        craw = V[:, 2, 0:2 * SP].rearrange("p (k n) -> p k n", k=2)
        cst = sb("cst", [128, 3, SP])
        hn = sb("hn", [T, 2, C])
        tmp, full = sb("tmp", [T, C]), sb("full", [128, 2, T])
        bo_b = sb("bo_b", [T, 2, C])
        mask_words = sb("mask_words", [T, 2, SP // 4], I32)
        maskf = cst[0:T, 0:2, :]
        causal = sb("causal", [T, T])
        ident = sb("ident", [128, 128])
        lnp_sb, bff_sb, bsm_sb = sb("lnp_sb", [128, N_LN, 2, 2]), sb("bff_sb", [128, 40]), sb("bsm_sb", [128, 6, 4])
        lo_rows_sb = sb("lo_rows_sb", [128, 1])
        nmax, rawmax = sb("nmax", [T, NP_, 4]), sb("rawmax", [T, 4])
        rsum, rinv = sb("rsum", [T, NP_, 4]), sb("rinv", [T, NP_, 4])
        bn6, mv = sb("bn6", [T, 6]), sb("mv", [T, 2, 2])
        ve, rstd, mhalf = sb("ve", [T, 2]), sb("rstd", [T, 2]), sb("mhalf", [T, 1])
        ctx_split = nc.dram_tensor("ctx_split", [B, 128, 3 * SP], F32).ap()

        def bank(name):
            return ctx.enter_context(nc.psum_tensor(name, [128, 512], F32))
        pS = [bank("pS0"), bank("pS1")]
        pT = [bank("pT0"), bank("pT1")]
        pO = [bank("pO0"), bank("pO1")]
        pG = [bank("pG0"), bank("pG1")]

        def raw(e):
            n = e.n[0]
            if n < FIRST_CHUNKS and e.n[1] == 0:
                return n % 4, (wraw[:, n % 4, :] if n % 4 < 2 else
                               P[:, :, :].rearrange("p a n -> p (a n)")[:, (n % 4 - 2) * WQ:(n % 4 - 1) * WQ])
            return n % 2, wraw[:, n % 2, :]

        def raw_count(e):
            n, step = e.n
            if n < FIRST_CHUNKS and step == 0:
                return affine(16 * (n // 4 + 1))
            return affine(16 * ((n - FIRST_CHUNKS) // 2 + 1 + FIRST_CHUNKS // 4), 16 * (step // 2))

        consts_in = sem("consts_in")
        x_in_sem = sem("x_in_sem")
        bo_in = sem("bo_in")
        craw_in = sem("craw_in")
        ctx_out = sem("ctx_out")
        src_in = sem("src_in")
        mask_in = [sem("mask_in0"), sem("mask_in1")]
        wraw_in = [sem("wraw_in%d" % i) for i in range(4)]
        out_done = sem("out_done")
        const_ready = sem("const_ready")
        ident0 = sem("ident0")
        w_hi, w_lo = sem("w_hi"), sem("w_lo")
        ctx_hi, ctx_lo = sem("ctx_hi"), sem("ctx_lo")
        ctx_lo2 = sem("ctx_lo2")
        pieces = sem("pieces")
        scored = sem("scored")
        maxed = sem("maxed")
        masked, rawmaxed = sem("masked"), sem("rawmaxed")
        exped = sem("exped")
        recip = sem("recip")
        normed = sem("normed")
        transposed = sem("transposed")
        pt_ready = sem("pt_ready")
        attended = sem("attended")
        ao_hi, ao_lo = sem("ao_hi"), sem("ao_lo")
        q_zero = sem("q_zero")
        q_hi, q_lo, q_dup = sem("q_hi"), sem("q_lo"), sem("q_dup")
        k_hi, k_lo = sem("k_hi"), sem("k_lo")
        k_all = sem("k_all")
        v_ready = sem("v_ready")
        gelu_ready, hid_ready = sem("gelu_ready"), sem("hid_ready")
        hid_hi, hid_lo = sem("hid_hi"), sem("hid_lo")
        res_tmp, x_ready = sem("res_tmp"), sem("x_ready")
        ln_stats, ln_mv = sem("ln_stats"), sem("ln_mv")
        ln_ve, ln_rstd = sem("ln_ve"), sem("ln_rstd")
        ln_h = sem("ln_h")
        hT_hi_ready, ln_full, hT_ready = sem("hT_hi_ready"), sem("ln_full"), sem("hT_ready")
        mask_f, mask_ready = sem("mask_f"), sem("mask_ready")

        block = ctx.enter_context(nc.Block())

        def unit(e, p, u=None):
            sh = shapes[e.st.i]
            u = e.a if u is None else u
            return at(affine(base["u"][e.st.i] + e.par * sh.NU + u, 2 * sh.NU), p)

        def unit_ring(e, u=None):
            return (e.a if u is None else u) % 4

        def of_batch(e, p, per):
            return at(affine(per * e.batch[0], per * e.batch[1]), p)

        def k_tiles_before(e, p):
            sh = shapes[e.st.i]
            step = sh.NT if e.st.self_ else 2 * sh.NT
            off = 0 if e.st.self_ else e.par * sh.NT
            return at(affine(base["k"][e.st.i] + off, step), p)

        def wait(eng, s, n):
            if type(n) is int and n <= 0:
                return
            eng.wait_ge(s, n)

        def wait_apart(eng, s, n):
            if type(n) is not int:
                n = eng.to_reg(n)
            elif n <= 0:
                return
            eng.wait_ge(const_ready, 1)
            eng.wait_ge(s, n)

        def side(e):
            return e.par % 2

        def v_column(e, parity):
            return 512 * parity if e.st.small and not e.st.self_ else 0

        def bank_of(e):
            return e.n[0] % 2

        def walk(eng, emit, name):
            for p0, p1, timed in segments:
                events = [e for _, e in sorted(timed, key=lambda x: x[0] + TIMES[x[1].st.self_, x[1].st.small][name].get(x[1].kind, 0))]
                if p1 - p0 > 1:
                    with eng.Fori(p0, p1) as p:
                        for e in events:
                            emit(e, p)
                else:
                    for e in events:
                        emit(e, p0)

        def w_view(slot, hl, col, n):
            return W[:, slot, hl, col:col + n]

        def hidden(buf):
            return buf[:, :, :].rearrange("p h n -> p (h n)")[:, 0:8 * CHUNK].rearrange("p (t n) -> p t n", t=8)

        def k_rewritable(e, p):
            st = e.st
            sh = shapes[st.i]
            if e.batch[1] == 0:
                return base["u"][st.i]
            last_unit = (e.a * sh.HPT + sh.HPT - 1) // sh.G
            if e.kind == "q" or st.self_:
                return at(affine(base["u"][st.i] + (2 * e.batch[0] - 1) * sh.NU + last_unit + 1, 2 * sh.NU), p)
            return at(affine(base["u"][st.i] + (e.batch[0] - 1) * sh.NU + last_unit + 1, 2 * sh.NU), p)

        def ff_before(st):
            done = [FFS[i].res for i in FFS if i < st.i]
            return 8 * (max(done) + 1) if done else 0

        def gelu_buf(i):
            return P[:, :, :].rearrange("p a n -> p (a n)")[:, i * CHUNK:(i + 1) * CHUNK]

        @block.sync
        def _(sp):
            sp.dma_start(lnp_sb[:, :, :, :], lnp).then_inc(consts_in, 16)
            sp.dma_start(bff_sb[:, :], bff).then_inc(consts_in, 16)
            sp.dma_start(bsm_sb[:, :, :], bsm).then_inc(consts_in, 16)
            sp.dma_start(lo_rows_sb[:, :], lo_rows).then_inc(consts_in, 16)
            sp.dma_start(x[:, :, :], x_in).then_inc(x_in_sem, 16)
            for i in range(2):
                sp.dma_start(bo_b[:, i, :], bo[i:i + 1, :].broadcast_to([T, C])).then_inc(bo_in, 16)

            def emit(e, p):
                st = e.st
                if e.kind == "w":
                    buf, view = raw(e)
                    wait_apart(sp, w_lo, at(e.n, p, -3 if e.n[0] < FIRST_CHUNKS and not e.n[1] else -1))
                    col = at(affine(e.batch[0] * WQ, e.batch[1] * WQ), p)
                    sp.dma_start(view, wts[e.a, :, bass.ds(col, WQ)]).then_inc(wraw_in[buf], 16)
                elif e.kind == "src":
                    wait_apart(sp, v_ready, base["v"][st.i] + of_batch(e, p, shapes[st.i].NV))
                    sh = shapes[st.i]
                    if st.self_:
                        wait_apart(sp, hT_ready, 8 * st.ln + of_batch(e, p, 1) + 1)
                        sv = src[:, 0:4 * T].bitcast(F32).rearrange("p (a k t) -> p a k t", a=2, k=2)
                        tok = of_batch(e, p, T)
                        sp.dma_start(sv[:, 0, :, :], hT_hi[:, :, bass.ds(tok, T)].bitcast(F32)).then_inc(src_in, 16)
                        sp.dma_start(sv[:, 1, :, :], hT_lo[:, :, bass.ds(tok, T)].bitcast(F32)).then_inc(src_in, 16)
                    else:
                        wait_apart(sp, k_lo, base["k"][st.i] + of_batch(e, p, sh.NT))
                        sp.wait_ge(ctx_out, 16 * (B - 1) if st.i == 1 and e.batch == affine(0) else 16 * B)
                        n = 3 * SP // 2
                        for h in range(2):
                            sp.dma_start(src[:, h * n:(h + 1) * n].bitcast(F32),
                                         ctx_split[bass.ds(of_batch(e, p, 1), 1), :, h * n:(h + 1) * n]
                                         .rearrange("a p n -> (a p) n")).then_inc(src_in, 16)
                elif e.kind == "mask":
                    words = shapes[st.i].keys // 4 if st.self_ else SP // 4
                    wait_apart(sp, maxed, base["u"][st.i] if e.batch[1] == 0 else unit(e, p, -shapes[st.i].NU))
                    msrc = mask_s if st.self_ else mask_x
                    sp.dma_start(mask_words[:, side(e), 0:words],
                                 msrc[bass.ds(of_batch(e, p, 1), 1), :].broadcast_to([T, words])).then_inc(mask_in[side(e)], 16)
                elif e.kind == "ctx":
                    b = of_batch(e, p, 1)
                    wait_apart(sp, ctx_lo, b)
                    wait_apart(sp, ctx_lo2, b)
                    sp.dma_start(craw[:, :, :], ctxT[:, bass.ds(b, 1), :, :].rearrange("p b k t -> p (b k) t")).then_inc(craw_in, 16)
                    wait_apart(sp, ctx_lo, b + 1)
                    wait_apart(sp, ctx_lo2, b + 1)
                    sp.dma_start(ctx_split[bass.ds(b, 1), :, :].rearrange("a p n -> (a p) n"),
                                 cst[:, :, :].rearrange("p a n -> p (a n)")).then_inc(ctx_out, 16)
                if e.kind == "ff2" and st.i == 6:
                    sp.wait_ge(x_ready, 8 * e.a + e.batch[0] + 1)
                    b = e.batch[0]
                    sp.dma_start(out[:, b, :], x[:, b, :]).then_inc(out_done, 16)
                if e.kind == "bo":
                    sp.wait_ge(x_ready, 8 * (e.a - 1))
                    sp.dma_start(bo_b[:, e.a % 2, :], bo[e.a:e.a + 1, :].broadcast_to([T, C])).then_inc(bo_in, 16)
            walk(sp, emit, "sp")
            sp.wait_ge(out_done, 16 * B)

        @block.tensor
        def _(pe):
            def mm(o, l, r, first, last):
                return nc.tensor.matmul(o, l, r, start=first, stop=last)

            def accumulate(o, passes):
                for i, (l, r) in enumerate(passes):
                    ins = mm(o, l, r, i == 0, i == len(passes) - 1)
                return ins

            done = {"q_lo": q_lo, "k_lo": k_lo, "v_ready": v_ready, "x_ready": x_ready, "hT_ready": hT_ready,
                    "gelu_ready": gelu_ready, "hid_ready": hid_ready}

            def piece_start(e, p):
                for name, n in e.prev or ():
                    if n != affine(0):
                        wait(pe, done[name], at(n, p))

            seen = set()

            def weights_ready(item):
                if item not in seen:
                    seen.add(item)
                    pe.wait_ge(w_lo, item_done[item])

            pe.wait_ge(const_ready, 1)

            def emit(e, p):
                st = e.st
                sh = shapes[st.i]
                if e.kind in ("q", "qk"):
                    weights_ready(ITEM_OF[st.i]["q"])
                    if e.kind == "qk":
                        weights_ready(ITEM_OF[st.i]["k"])
                    tok = of_batch(e, p, PAIR)
                    wait(pe, hT_ready, 8 * st.ln + of_batch(e, p, 2) + 2)
                    piece_start(e, p)
                    for n, (slot, col, ks) in enumerate((st.q, st.k)[:len(e.kind)]):
                        passes = []
                        for k in range(2):
                            hi = w_view(slot, 0, col + k * ks + e.a * 128, 128)
                            lo = w_view(slot, 1, col + k * ks + e.a * 128, 128)
                            ah, al = hT_hi[:, k, bass.ds(tok, PAIR)], hT_lo[:, k, bass.ds(tok, PAIR)]
                            passes += [(hi, ah), (hi, al), (lo, ah)]
                        ins = accumulate(pG[bank_of(e)][:, n * PAIR:(n + 1) * PAIR], passes)
                    ins.then_inc(pieces, 1)
                elif e.kind == "k":
                    weights_ready(ITEM_OF[st.i]["k"])
                    pe.wait_ge(src_in, 32 * 8 * st.i + of_batch(e, p, 32) + 32)
                    piece_start(e, p)
                    slot, col, ks = st.k
                    wv = [[w_view(slot, hl, col + k * ks + e.a * 128, 128) for hl in range(2)] for k in range(2)]
                    s = [src[:, i * SP:(i + 1) * SP] for i in range(3)]
                    accumulate(pG[bank_of(e)][:, 0:SP],
                               [(wv[0][0], s[0]), (wv[0][0], s[1]), (wv[0][1], s[0]), (wv[1][0], s[2]), (wv[1][1], s[2])]
                               ).then_inc(pieces, 1)
                elif e.kind == "v":
                    weights_ready(ITEM_OF[st.i]["v"])
                    pe.wait_ge(src_in, 32 * 8 * st.i + of_batch(e, p, 32) + 32)
                    piece_start(e, p)
                    slot, col, ks = st.v
                    wv = [[w_view(slot, hl, col + k * ks + e.a * 512, 512) for hl in range(2)] for k in range(2)]
                    if st.self_:
                        a = [[src[:, (hl * 2 + k) * T:(hl * 2 + k + 1) * T] for hl in range(2)] for k in range(2)]
                        passes = []
                        for k in range(2):
                            passes += [(a[k][0], wv[k][0]), (a[k][0], wv[k][1]), (a[k][1], wv[k][0])]
                    else:
                        s = [src[:, i * SP + e.b * KM:i * SP + (e.b + 1) * KM] for i in range(3)]
                        passes = [(s[0], wv[0][0]), (s[0], wv[0][1]), (s[1], wv[0][0]), (s[2], wv[1][0]), (s[2], wv[1][1])]
                    accumulate(pG[bank_of(e)][0:sh.krows, :], passes).then_inc(pieces, 1)
                elif e.kind == "scores":
                    U = unit(e, p)
                    tile = (e.a * sh.G + sh.G - 1) // sh.HPT
                    if (e.a * sh.G) % sh.HPT == 0:
                        wait(pe, q_lo, at(affine(base["q"][st.i] + tile + 1, sh.NT), p))
                        wait(pe, k_lo, k_tiles_before(e, p) + tile + 1)
                    wait(pe, exped, U - 1)
                    for g in range(sh.G):
                        h = e.a * sh.G + g
                        t = h // sh.HPT
                        qc = slice(e.par * T, (e.par + 1) * T)
                        kc = slice(e.par * T, (e.par + 1) * T) if st.self_ else slice(0, SP)
                        n = T if st.self_ else SP
                        o = pS[e.a % 2][0:T, g * T:g * T + n]
                        if st.small:
                            passes = [(QH[:, h, qc], KS[:, t, kc]), (QL[:, h, qc], KS[:, t, kc])]
                        else:
                            passes = [(QH[:, h, qc], KS[:, h, kc]), (QL[:, h, qc], KS[:, h, kc])]
                        ins = accumulate(o, passes)
                    ins.then_inc(scored, 1)
                elif e.kind == "trans":
                    U = unit(e, p)
                    wait(pe, normed, U + 1)
                    wait(pe, pt_ready, U - 1)
                    for i in range(sh.G * sh.KT):
                        lhsT = P[0:T, unit_ring(e), i * sh.krows:(i + 1) * sh.krows]
                        ins = nc.tensor.transpose(pT[e.a % 2][0:sh.krows, i * T:(i + 1) * T], lhsT, ident[0:T, 0:T])
                    ins.then_inc(transposed, 1)
                elif e.kind == "av":
                    U = unit(e, p)
                    pe.wait_ge(pt_ready, U + 1)
                    per = sh.NU // sh.NO
                    o = e.a // per
                    if e.a % per == 0:
                        A = at(affine(base["a"][st.i] + e.par * sh.NO + o, 2 * sh.NO), p)
                        wait(pe, ao_lo, A - 1)
                        pe.wait_ge(v_ready, at(affine(base["v"][st.i] + e.par * sh.NV + (o + 1) * sh.KT * sh.VH // sh.NO, 2 * sh.NV), p))
                    ob = pO[o if sh.NO == 2 else side(e)]
                    for g in range(sh.G):
                        h = e.a * sh.G + g
                        t = (h // sh.HPT) % 4
                        row = sh.M * (h % sh.HPT)
                        passes = []
                        vc = v_column(e, side(e))
                        for m in range(sh.KT):
                            vs = side(e) if st.self_ else m
                            pt = PT[0:sh.krows, e.a % 2, (g + m) * T:(g + m + 1) * T]
                            passes.append((V[0:sh.krows, vs, vc + h * sh.M:vc + (h + 1) * sh.M], pt))
                        ins = accumulate(ob[row:row + sh.M, t * T:(t + 1) * T], passes)
                    ins.then_inc(attended, 1)
                elif e.kind == "wo":
                    weights_ready(ITEM_OF[st.i]["o"])
                    pe.wait_ge(ao_lo, at(affine(base["a"][st.i] + (e.par + 1) * sh.NO, 2 * sh.NO), p))
                    piece_start(e, p)
                    slot, col, ks = st.o
                    passes = []
                    for t in range(sh.NT):
                        hi, lo = w_view(slot, 0, col + t * C, C), w_view(slot, 1, col + t * C, C)
                        passes += [(AOT_hi[:, t, :], hi), (AOT_hi[:, t, :], lo), (AOT_lo[:, t, :], hi)]
                    accumulate(pG[bank_of(e)][0:T, 0:C], passes).then_inc(pieces, 1)
                elif e.kind == "lnt":
                    wait(pe, ln_h, 8 * e.a + of_batch(e, p, 1) + 1)
                    piece_start(e, p)
                    for k in range(2):
                        ins = nc.tensor.transpose(pG[bank_of(e)][:, k * T:(k + 1) * T],
                                                  hn[:, side(e), k * 128:(k + 1) * 128], ident[0:T, 0:T])
                    ins.then_inc(pieces, 1)
                elif e.kind in ("ffg", "ffa"):
                    ff = FFS[st.i]
                    slot = ff.gate if e.kind == "ffg" else ff.value
                    weights_ready(FF_ITEMS[st.i][1 if e.kind == "ffg" else 0])
                    pe.wait_ge(hT_ready, 8 * ff.ln + 4 * (e.b + 1))
                    piece_start(e, p)
                    passes = []
                    for k in range(2):
                        hi, lo = w_view(slot, 0, k * 1024 + e.a * 128, 128), w_view(slot, 1, k * 1024 + e.a * 128, 128)
                        ah, al = hT_hi[:, k, e.b * CHUNK:(e.b + 1) * CHUNK], hT_lo[:, k, e.b * CHUNK:(e.b + 1) * CHUNK]
                        passes += [(hi, ah), (hi, al), (lo, ah)]
                    accumulate(pG[bank_of(e)][:, 0:CHUNK], passes).then_inc(pieces, 1)
                elif e.kind == "ff2":
                    ff = FFS[st.i]
                    weights_ready(FF_ITEMS[st.i][2])
                    k = sorted(FFS).index(st.i)
                    pe.wait_ge(hid_lo, 16 * k + 8 * (e.batch[0] // 4 + 1))
                    piece_start(e, p)
                    gh, gl = hidden(KS), hidden(QH)
                    passes = []
                    for t in range(8):
                        a = slice(e.b * T, (e.b + 1) * T)
                        hi, lo = w_view(ff.out, 0, t * C, C), w_view(ff.out, 1, t * C, C)
                        passes += [(gh[:, t, a], hi), (gh[:, t, a], lo), (gl[:, t, a], hi)]
                    accumulate(pG[bank_of(e)][0:T, 0:C], passes).then_inc(pieces, 1)
            walk(pe, emit, "pe")

        @block.scalar
        def _(act):
            act.wait_ge(consts_in, 64)

            def q_hi_of(st, e, g):
                if st.small:
                    act.wait_ge(q_zero, 3)
                    for i in range(4):
                        r = slice(32 * i, 32 * i + 32)
                        ins = act.activation(QH[r, 4 * e.a + i, :], g[r, 0:PAIR], ACT.Identity,
                                             bias=bsm_sb[r, 0 if st.self_ else 3, e.a:e.a + 1])
                    ins.then_inc(q_hi, 1)
                else:
                    act.activation(QH[0:64, 2 * e.a, :], g[0:64, 0:PAIR], ACT.Copy, scale=st.qscale)
                    act.activation(QH[64:128, 2 * e.a + 1, :], g[64:128, 0:PAIR], ACT.Copy, scale=st.qscale).then_inc(q_hi, 1)
                    act.activation(QH[0:64, 2 * e.a + 1, :], g[64:128, 0:PAIR], ACT.Copy, scale=st.qscale).then_inc(q_dup, 1)

            def k_hi_of(st, e, g):
                n = PAIR if st.self_ else SP
                if st.small:
                    act.activation(KS[:, 4 + e.a, 0:n], g[:, 0:n], ACT.Identity,
                                   bias=bsm_sb[:, 1 if st.self_ else 4, e.a:e.a + 1]).then_inc(k_all, 1)
                else:
                    act.activation(KS[0:64, 2 * e.a, 0:n], g[0:64, 0:n], ACT.Copy)
                    act.activation(KS[64:128, 2 * e.a + 1, 0:n], g[64:128, 0:n], ACT.Copy).then_inc(k_hi, 1)

            def emit(e, p):
                st = e.st
                sh = shapes[st.i]
                g = pG[bank_of(e)] if e.n is not None and e.kind != "w" else None
                if e.kind == "w":
                    buf, view = raw(e)
                    act.wait_ge(wraw_in[buf], at(raw_count(e), p))
                    wait(act, pieces, at(e.seg, p))
                    col = at(affine(e.batch[0] * WQ, e.batch[1] * WQ), p)
                    act.activation(W[:, e.b, 0, bass.ds(col, WQ)], view, ACT.Copy).then_inc(w_hi, 1)
                elif e.kind in ("q", "k", "qk"):
                    act.wait_ge(pieces, at(e.n, p, 1))
                    wait(act, scored, k_rewritable(e, p))
                    if e.batch[1] == 0:
                        wait(act, x_ready, ff_before(st))
                    if "q" in e.kind:
                        q_hi_of(st, e, g)
                    if "k" in e.kind:
                        k_hi_of(st, e, g[:, PAIR:2 * PAIR] if e.kind == "qk" else g)
                elif e.kind == "v":
                    act.wait_ge(pieces, at(e.n, p, 1))
                    if e.batch[1] == 0:
                        wait(act, attended, base["u"][st.i])
                        if st.i == 1:
                            act.wait_ge(ctx_lo2, B)
                            act.wait_ge(ctx_lo, B)
                    else:
                        per = sh.NU // sh.VH
                        back = 2 if st.self_ or st.small else 1
                        c = affine(base["u"][st.i] + (e.batch[0] - back) * sh.NU + (e.a + 1) * per, 2 * sh.NU)
                        wait(act, attended, at(c, p))
                    slot = (e.batch[0] % 2) if st.self_ else e.b
                    col = e.a * 512 + v_column(e, e.batch[0] % 2)
                    act.activation(V[0:sh.krows, slot, col:col + 512], g[0:sh.krows, :], ACT.Copy).then_inc(v_ready, 1)
                elif e.kind == "scores":
                    U = unit(e, p)
                    act.wait_ge(maxed, U + 1)
                    if type(U) is int and U == 0:
                        act.wait_ge(w_lo, FIRST_CHUNKS)
                    if not st.small:
                        wait(act, transposed, U - NP_ + 1)
                    for i in range(sh.G):
                        n = sh.keys
                        o = P[0:T, unit_ring(e), i * n:(i + 1) * n]
                        s = o if st.small else pS[e.a % 2][0:T, i * n:(i + 1) * n]
                        ins = act.activation(o, s, ACT.Exp, bias=nmax[:, unit_ring(e), i:i + 1], scale=st.escale,
                                             accum_out=rsum[:, unit_ring(e), i:i + 1])
                    ins.then_inc(exped, 1)
                elif e.kind == "trans":
                    U = unit(e, p)
                    act.wait_ge(transposed, U + 1)
                    wait(act, attended, U - 1)
                    n = sh.G * sh.KT * T
                    act.activation(PT[0:sh.krows, e.a % 2, 0:n], pT[e.a % 2][0:sh.krows, 0:n], ACT.Copy).then_inc(pt_ready, 1)
                elif e.kind == "ao":
                    per = sh.NU // sh.NO
                    act.wait_ge(attended, unit(e, p, (e.a + 1) * per - 1) + 1)
                    wait(act, x_ready, 8 * st.res + of_batch(e, p, 1))
                    ob = pO[e.a if sh.NO == 2 else side(e)]
                    if st.small:
                        for t in range(4):
                            ins = act.activation(AOT_hi[:, t, :], ob[:, t * T:(t + 1) * T], ACT.Identity,
                                                 bias=bsm_sb[:, 2 if st.self_ else 5, t:t + 1])
                    else:
                        ins = act.activation(AOT_hi[:, 4 * e.a:4 * e.a + 4, :],
                                             ob[:, 0:4 * T].rearrange("p (t n) -> p t n", t=4), ACT.Copy)
                    ins.then_inc(ao_hi, 1)
                elif e.kind == "lnt":
                    act.wait_ge(pieces, at(e.n, p, 1))
                    for k in range(2):
                        ins = act.activation(hT_hi[:, k, bass.ds(of_batch(e, p, T), T)], g[:, k * T:(k + 1) * T], ACT.Identity,
                                             bias=lnp_sb[:, e.a, 1, k:k + 1], scale=lnp_sb[:, e.a, 0, k:k + 1])
                    ins.then_inc(hT_hi_ready, 1)
                elif e.kind == "ffg":
                    ff = FFS[st.i]
                    N = 16 * sorted(FFS).index(st.i) + 8 * e.b + e.a
                    act.wait_ge(pieces, at(e.n, p, 1))
                    col = ff.bias + e.a + (8 if ff.value is not None else 0)
                    if ff.value is not None:
                        wait(act, hid_ready, N - 1 if N % 16 > 1 else N - N % 16)
                        o = gelu_buf(N % 2)
                        if N % 16 < 2:
                            act.wait_ge(transposed, base["u"][st.i + 1])
                    else:
                        wait(act, hid_lo, N - 1)
                        o = PT[:, N % 2, :]
                        if N % 16 < 2:
                            act.wait_ge(attended, base["u"][st.i + 1])
                    fn = ACT.Gelu if ff.act == "erf" else ACT.Gelu_apprx_tanh
                    act.activation(o, g[:, 0:CHUNK], fn, bias=bff_sb[:, col:col + 1]).then_inc(gelu_ready, 1)
            walk(act, emit, "act")

        @block.vector
        def _(dve):
            dve.wait_ge(consts_in, 64)
            dve.wait_ge(const_ready, 1)

            def split_w(e, p):
                view = raw(e)[1]
                col = at(affine(e.batch[0] * WQ, e.batch[1] * WQ), p)
                dve.wait_ge(w_hi, at(e.n, p, 1))
                dve.tensor_tensor(W[:, e.b, 1, bass.ds(col, WQ)], view, W[:, e.b, 0, bass.ds(col, WQ)].bitcast(F32),
                                  ALU.subtract).then_inc(w_lo, 1)

            def layer_norm(e, p, group):
                n = 8 * group + of_batch(e, p, 1)
                xb = x[:, bass.ds(of_batch(e, p, 1), 1), :].rearrange("p a n -> p (a n)")
                wait_apart(dve, ln_mv, n)
                if group:
                    wait_apart(dve, x_ready, n - 7)
                dve.bn_stats(bn6[:, :], xb).then_inc(ln_stats, 1)
                wait_apart(dve, ln_stats, n + 1)
                dve.bn_aggr(mv[:, side(e), :], bn6[:, :]).then_inc(ln_mv, 1)

            def q_lo_of(st, e, p, g):
                Q = at(affine(base["q"][st.i] + shapes[st.i].NT * e.batch[0] + e.a, shapes[st.i].NT * e.batch[1]), p)
                dve.wait_ge(q_hi, Q + 1)
                if st.small:
                    for i in range(4):
                        r = slice(32 * i, 32 * i + 32)
                        ins = dve.scalar_tensor_tensor(QL[r, 4 * e.a + i, :], g[r, 0:PAIR],
                                                       bsm_sb[r, 0 if st.self_ else 3, e.a:e.a + 1],
                                                       QH[r, 4 * e.a + i, :].bitcast(F32), ALU.add, ALU.subtract)
                    ins.then_inc(q_lo, 1)
                else:
                    dve.wait_ge(q_dup, Q + 1)
                    if st.i == 0 and e.batch[1] == 0:
                        dve.wait_ge(q_zero, 1)
                    dve.scalar_tensor_tensor(QL[0:64, 2 * e.a, :], g[0:64, 0:PAIR], st.qscale,
                                             QH[0:64, 2 * e.a, :].bitcast(F32), ALU.mult, ALU.subtract)
                    dve.scalar_tensor_tensor(QL[64:128, 2 * e.a + 1, :], g[64:128, 0:PAIR], st.qscale,
                                             QH[64:128, 2 * e.a + 1, :].bitcast(F32), ALU.mult, ALU.subtract)
                    dve.tensor_copy(QH[64:128, 2 * e.a, :], QH[0:64, 2 * e.a, :].bitcast(F32)).then_inc(q_lo, 1)

            def k_lo_of(st, e, p, g):
                n = PAIR if st.self_ else SP
                K = at(affine(base["k"][st.i] + shapes[st.i].NT * e.batch[0] + e.a, shapes[st.i].NT * e.batch[1]), p)
                dve.wait_ge(k_hi, K + 1)
                if st.small:
                    dve.scalar_tensor_tensor(KS[:, e.a, 0:n], g[:, 0:n], bsm_sb[:, 1 if st.self_ else 4, e.a:e.a + 1],
                                             KS[:, 8 + e.a, 0:n].bitcast(F32), ALU.add, ALU.subtract).then_inc(k_lo, 1)
                else:
                    dve.tensor_tensor(KS[64:128, 2 * e.a, 0:n], g[0:64, 0:n], KS[0:64, 2 * e.a, 0:n].bitcast(F32), ALU.subtract)
                    dve.tensor_tensor(KS[0:64, 2 * e.a + 1, 0:n], g[64:128, 0:n], KS[64:128, 2 * e.a + 1, 0:n].bitcast(F32),
                                      ALU.subtract).then_inc(k_lo, 1)

            def residual(e, p, ps):
                r = 8 * e.a + of_batch(e, p, 1)
                xb = x[:, bass.ds(of_batch(e, p, 1), 1), :].rearrange("p a n -> p (a n)")
                dve.wait_ge(bo_in, 16 * (e.a + 1) if e.a else 32)
                wait(dve, x_ready, r)
                dve.tensor_tensor(tmp[0:T, :], ps, bo_b[:, e.a % 2, :], ALU.add).then_inc(res_tmp, 1)
                dve.wait_ge(res_tmp, r + 1)
                dve.tensor_tensor(xb, xb, tmp[0:T, :], ALU.add).then_inc(x_ready, 1)

            def emit(e, p):
                st = e.st
                sh = shapes[st.i]
                isp = e.n is not None and e.kind != "w"
                g = pG[bank_of(e)] if isp else None
                if e.kind == "w":
                    split_w(e, p)
                elif e.kind == "zero":
                    dve.wait_ge(scored, base["u"][st.i])
                    dve.memset(QH[:, :, :].bitcast(F32), 0.0).then_inc(q_zero, 1)
                elif e.kind == "ln0":
                    if e.batch[0] == 0:
                        dve.wait_ge(x_in_sem, 16)
                    layer_norm(e, p, 0)
                elif e.kind in ("q", "k", "qk"):
                    if e.kind == "qk":
                        dve.wait_ge(k_hi, at(affine(base["k"][st.i] + sh.NT * e.batch[0] + e.a + 1, sh.NT * e.batch[1]), p))
                    if "q" in e.kind:
                        q_lo_of(st, e, p, g)
                    if "k" in e.kind:
                        k_lo_of(st, e, p, g[:, PAIR:2 * PAIR] if e.kind == "qk" else g)
                elif e.kind == "scores":
                    U = unit(e, p)
                    r = unit_ring(e)
                    (wait_apart if st.small else wait)(dve, scored, U + 1)
                    ps = pS[e.a % 2][0:T, 0:sh.G * sh.keys]
                    if not st.small:
                        if sh.G > 1:
                            ps = ps.rearrange("p (g n) -> p g n", g=sh.G)
                        dve.tensor_reduce(nmax[:, r, 0:sh.G], ps, AX.X, ALU.max, negate=True).then_inc(maxed, 1)
                    else:
                        i = U - base["u"][5]
                        if e.a == 0:
                            wait_apart(dve, mask_ready, at(affine(base["m"][st.i] + e.par + 1, 2), p))
                        wait_apart(dve, transposed, U - NP_ + 1)
                        wait_apart(dve, maxed, U)
                        po = P[0:T, r, 0:sh.G * sh.keys]
                        if st.self_:
                            po = po.rearrange("p (g n) -> p g n", g=4)
                            mk = maskf[:, side(e):side(e) + 1, 0:T].broadcast_to([T, 4, T])
                            dve.tensor_tensor(po, ps.rearrange("p (g n) -> p g n", g=4), mk, ALU.add).then_inc(masked, 1)
                            dve.wait_ge(masked, i + 1)
                            dve.tensor_reduce(rawmax[:, 0:4], po, AX.X, ALU.max).then_inc(rawmaxed, 1)
                        else:
                            dve.tensor_tensor_reduce(out=po, in0=ps, in1=maskf[:, side(e), 0:S2], scale=1.0, scalar=-3e38,
                                                     op0=ALU.add, op1=ALU.max, accum_out=rawmax[:, 0:1]).then_inc(rawmaxed, 1)
                        dve.wait_ge(rawmaxed, i + 1)
                        dve.tensor_scalar(nmax[:, r, 0:sh.G], rawmax[:, 0:sh.G], -st.escale, None, ALU.mult).then_inc(maxed, 1)
                elif e.kind == "norm":
                    U = unit(e, p)
                    dve.wait_ge(exped, U + 1)
                    r = unit_ring(e)
                    dve.reciprocal(rinv[:, r, 0:sh.G], rsum[:, r, 0:sh.G]).then_inc(recip, 1)
                elif e.kind == "ao":
                    A = at(affine(base["a"][st.i] + e.par * sh.NO + e.a, 2 * sh.NO), p)
                    dve.wait_ge(ao_hi, A + 1)
                    ob = pO[e.a if sh.NO == 2 else side(e)]
                    if st.small:
                        for t in range(4):
                            ins = dve.scalar_tensor_tensor(AOT_lo[:, t, :], ob[:, t * T:(t + 1) * T], bsm_sb[:, 2 if st.self_ else 5, t:t + 1],
                                                           AOT_hi[:, t, :].bitcast(F32), ALU.add, ALU.subtract)
                    else:
                        ins = dve.tensor_tensor(AOT_lo[:, 4 * e.a:4 * e.a + 4, :], ob[:, 0:4 * T].rearrange("p (t n) -> p t n", t=4),
                                                AOT_hi[:, 4 * e.a:4 * e.a + 4, :].bitcast(F32), ALU.subtract)
                    ins.then_inc(ao_lo, 1)
                elif e.kind in ("wo", "ff2"):
                    dve.wait_ge(pieces, at(e.n, p, 1))
                    residual(e, p, g[0:T, 0:C])
                    if e.a < N_LN - 1:
                        layer_norm(e, p, e.a + 1)
                elif e.kind == "ctx":
                    b = of_batch(e, p, 1)
                    dve.wait_ge(ctx_hi, b + 1)
                    dve.tensor_tensor(cst[64:128, 2, :].bitcast(F32R), craw[64:128, 1, :], cst[64:128, 2, :],
                                      ALU.subtract).then_inc(ctx_lo2, 1)
                elif e.kind == "lnh":
                    n = 8 * e.a + of_batch(e, p, 1)
                    xb = x[:, bass.ds(of_batch(e, p, 1), 1), :].rearrange("p a n -> p (a n)")
                    dve.wait_ge(ln_rstd, n + 1)
                    dve.tensor_scalar(hn[:, side(e), :], xb, mv[:, side(e), 0:1], rstd[:, side(e):side(e) + 1],
                                      ALU.subtract, ALU.mult).then_inc(ln_h, 1)
                elif e.kind == "lnt":
                    n = 8 * e.a + of_batch(e, p, 1)
                    dve.wait_ge(hT_hi_ready, n + 1)
                    wait(dve, hT_ready, n)
                    for k in range(2):
                        ins = dve.tensor_scalar(full[:, k, :], g[:, k * T:(k + 1) * T], lnp_sb[:, e.a, 0, k:k + 1],
                                                lnp_sb[:, e.a, 1, k:k + 1], ALU.mult, ALU.add)
                    ins.then_inc(ln_full, 1)
                    dve.wait_ge(ln_full, n + 1)
                    tok = of_batch(e, p, T)
                    dve.tensor_tensor(hT_lo[:, :, bass.ds(tok, T)], full[:, :, :], hT_hi[:, :, bass.ds(tok, T)].bitcast(F32),
                                      ALU.subtract).then_inc(hT_ready, 1)
                elif e.kind in ("ffg", "ffa"):
                    ff = FFS[st.i]
                    if e.kind == "ffg" and ff.value is not None:
                        return
                    k = sorted(FFS).index(st.i)
                    N = 16 * k + 8 * e.b + e.a
                    dve.wait_ge(gelu_ready, N + 1)
                    if ff.value is not None:
                        dve.wait_ge(pieces, at(e.n, p, 1))
                        if e.b == 0 and e.a == 0:
                            dve.wait_ge(attended, base["u"][st.i + 1])
                        col = ff.bias + e.a
                        dve.scalar_tensor_tensor(PT[:, N % 2, :], g[:, 0:CHUNK], bff_sb[:, col:col + 1], gelu_buf(N % 2),
                                                 ALU.add, ALU.mult).then_inc(hid_ready, 1)
                        dve.wait_ge(hid_ready, N + 1)
                    if e.b == 0 and e.a == 0:
                        dve.wait_ge(scored, base["u"][st.i + 1])
                    if e.b == 1 and e.a == 0:
                        dve.wait_ge(x_ready, 8 * ff.res + 4)
                    hid = PT[:, N % 2, :]
                    dve.tensor_copy(hidden(KS)[:, e.a, :], hid).then_inc(hid_hi, 1)
                    dve.wait_ge(hid_hi, N + 1)
                    dve.tensor_tensor(hidden(QH)[:, e.a, :], hid, hidden(KS)[:, e.a, :].bitcast(F32), ALU.subtract).then_inc(hid_lo, 1)
            walk(dve, emit, "dve")

        @block.gpsimd
        def _(pool):
            pool.memset(ident[:, :], 0.0).then_inc(ident0, 1)
            pool.memset(causal[:, :], 0.0).then_inc(ident0, 1)
            pool.memset(mhalf[:, :], -0.5).then_inc(ident0, 1)
            pool.wait_ge(ident0, 3)
            pool.affine_select(out=causal[:, :], in_=causal[:, :], compare_op=ALU.is_ge, fill=MASKED,
                               base=0, pattern=[[-1, T]], channel_multiplier=1).then_inc(ident0, 1)
            pool.affine_select(out=ident[:, :], in_=ident[:, :], compare_op=ALU.not_equal, fill=1.0,
                               base=0, pattern=[[-1, 128]], channel_multiplier=1).then_inc(const_ready, 1)
            pool.wait_ge(ident0, 4)
            pool.memset(QL[:, :, :].bitcast(F32), 0.0).then_inc(q_zero, 1)

            pool.wait_ge(consts_in, 64)

            def rstd_of(e, p, group):
                n = 8 * group + of_batch(e, p, 1)
                wait_apart(pool, ln_mv, n + 1)
                pool.tensor_scalar(ve[:, side(e):side(e) + 1], mv[:, side(e), 1:2], EPS, None, ALU.add).then_inc(ln_ve, 1)
                pool.wait_ge(ln_ve, n + 1)
                pool.tensor_tensor(rstd[:, side(e):side(e) + 1], ve[:, side(e):side(e) + 1], mhalf[:, :], ALU.pow).then_inc(ln_rstd, 1)

            def emit(e, p):
                st = e.st
                sh = shapes[st.i]
                if e.kind == "zero":
                    pool.wait_ge(scored, base["u"][st.i])
                    pool.memset(QL[:, :, :].bitcast(F32), 0.0).then_inc(q_zero, 1)
                elif e.kind in ("k", "qk") and st.small:
                    n = PAIR if st.self_ else SP
                    K = at(affine(base["k"][st.i] - base["k"][5] + sh.NT * e.batch[0] + e.a, sh.NT * e.batch[1]), p)
                    wait_apart(pool, k_all, K + 1)
                    pool.tensor_scalar(KS[:, 8 + e.a, 0:n], KS[:, 4 + e.a, 0:n].bitcast(F32), lo_rows_sb[:, 0:1], 1.0,
                                       ALU.mult, ALU.mult).then_inc(k_hi, 1)
                elif e.kind == "norm":
                    U = unit(e, p)
                    r = unit_ring(e)
                    wait_apart(pool, recip, U + 1)
                    for i in range(sh.G):
                        n = sh.keys
                        o = P[0:T, r, i * n:(i + 1) * n]
                        ins = pool.tensor_scalar(o, o, rinv[:, r, i:i + 1], st.nscale, ALU.mult, ALU.mult)
                    ins.then_inc(normed, 1)
                elif e.kind == "ln0":
                    rstd_of(e, p, 0)
                elif e.kind in ("wo", "ff2") and e.a < N_LN - 1:
                    rstd_of(e, p, e.a + 1)
                elif e.kind == "ctx":
                    b = of_batch(e, p, 1)
                    wait_apart(pool, craw_in, 16 * b + 16)
                    wait_apart(pool, ctx_out, 16 * b)
                    for i in range(2):
                        ins = pool.tensor_scalar(cst[:, 2 * i, :].bitcast(F32R), craw[:, i, :], 1.0, 1.0, ALU.mult, ALU.mult)
                    ins.then_inc(ctx_hi, 1)
                    wait_apart(pool, ctx_hi, b + 1)
                    pool.tensor_tensor(cst[:, 1, :].bitcast(F32R), craw[:, 0, :], cst[:, 0, :], ALU.subtract).then_inc(ctx_lo, 1)
                elif e.kind == "mask":
                    m = at(affine(base["m"][st.i] + e.batch[0], e.batch[1]), p)
                    keys = sh.keys
                    wait_apart(pool, mask_in[side(e)], at(affine(8 * base["m"][st.i] + 16 * (e.par // 2 + 1), 16 * (e.batch[1] // 2)), p))
                    wait_apart(pool, maxed, base["u"][st.i] if e.batch[1] == 0 else unit(e, p, -sh.NU))
                    mf = maskf[:, side(e), 0:keys]
                    ins = pool.tensor_scalar(mf, mask_words[:, side(e), :].bitcast(U8)[:, 0:keys], MASKED, 1.0, ALU.mult, ALU.mult).then_inc(mask_f, 1)
                    wait_apart(pool, mask_f, m + 1)
                    if st.self_:
                        pool.tensor_tensor(mf, mf, causal[:, :], ALU.add).then_inc(mask_ready, 1)
                    else:
                        pool.tensor_scalar(mf, mf, 1.0, 1.0, ALU.mult, ALU.mult).then_inc(mask_ready, 1)
            walk(pool, emit, "pool")


def pack_weights(g):
    def k256(w):
        return w.reshape(2, 128, 1024).transpose(1, 0, 2).reshape(128, 2048)

    def k192(w):
        return np.concatenate([w[:128], np.concatenate([w[128:], w[128:]], 0)], 1)

    def o1024(w):
        return w.reshape(8, 128, 256).transpose(1, 0, 2).reshape(128, 2048)

    def pad_heads(w):
        k = w.shape[0]
        return np.concatenate([w.reshape(k, 16, 16), np.zeros((k, 16, 16), w.dtype)], 2).reshape(k, 512)

    def twice_heads(w):
        k = w.shape[0]
        return np.concatenate([w.reshape(k, 16, 16)] * 2, 2).reshape(k, 512)

    def pad_rows(w):
        return np.concatenate([w.reshape(16, 16, 256), np.zeros((16, 16, 256), w.dtype)], 1).reshape(4, 128, 256) \
            .transpose(1, 0, 2).reshape(128, 1024)

    def tiles(w):
        return w.reshape(2, 128, w.shape[1]).transpose(1, 0, 2).reshape(128, 2 * w.shape[1])

    L0, L1, L2, L3 = ("L%d_xattn_" % i for i in range(4))
    qkv = g[L3 + "qkv_w"]
    items = [k256(g[L0 + "Wq1"]), k256(g[L0 + "Wk1"]), k256(g[L0 + "Wv1"]), o1024(g[L0 + "Wo1"]),
             k256(g[L0 + "Wq2"]), k192(g[L0 + "Wk2"]), k192(g[L0 + "Wv2"]), o1024(g[L0 + "Wo2"]),
             k256(g[L0 + "Wp"][:, :1024]), k256(g[L0 + "Wp"][:, 1024:]), o1024(g[L0 + "Wf"]),
             k256(g[L1 + "wq1"]), k256(g[L1 + "wk1"]), k256(g[L1 + "wv1"]), o1024(g[L1 + "wo1"]),
             k256(g[L1 + "wq2"]), k192(g[L1 + "wk2"]), k192(g[L1 + "wv2"]), o1024(g[L1 + "wo2"]),
             k256(g[L1 + "w_ff1"][:, :1024]), k256(g[L1 + "w_ff1"][:, 1024:]), o1024(g[L1 + "w_ff2"]),
             k256(g[L2 + "Wq"]), k192(g[L2 + "Wk"]), k192(g[L2 + "Wv"]), o1024(g[L2 + "Wo"]),
             k256(np.concatenate([twice_heads(qkv[:, :256]), twice_heads(qkv[:, 256:512])], 1)),
             np.concatenate([tiles(pad_heads(qkv[:, 512:])), pad_rows(g[L3 + "proj_w"])], 1),
             np.concatenate([tiles(twice_heads(g[L3 + "q_w"])), pad_rows(g[L3 + "out_w"])], 1),
             np.concatenate([k192(twice_heads(g[L3 + "k_w"])), k192(pad_heads(g[L3 + "v_w"]))], 1),
             k256(g[L3 + "mlp1_w"]), o1024(g[L3 + "mlp2_w"])]
    return np.stack(items)


def kernel(**inputs):
    import concourse.bacc as bacc
    from concourse.bass_utils import run_bass_kernel_spmd

    g = {k: np.asarray(v) for k, v in inputs.items()}
    L0, L1, L2, L3 = ("L%d_xattn_" % i for i in range(4))

    def cols(v):
        return v.reshape(-1, 128).T

    def small2(v):
        return cols(np.concatenate([v.reshape(16, 16)] * 2, 1).reshape(512))

    def small(v):
        return cols(np.concatenate([v.reshape(16, 16), np.zeros((16, 16), v.dtype)], 1).reshape(512))

    def words(m):
        m = np.ascontiguousarray(m).view(np.uint8)
        return np.concatenate([m, np.zeros((B, -m.shape[1] % 4), np.uint8)], 1).view(np.int32)

    norms = [(L0 + "g1", L0 + "b1"), (L0 + "g2", L0 + "b2"), (L0 + "g3", L0 + "b3"),
             (L1 + "ln1_g", L1 + "ln1_b"), (L1 + "ln2_g", L1 + "ln2_b"), (L1 + "ln3_g", L1 + "ln3_b"),
             (L2 + "gamma", L2 + "beta"), (L3 + "ln1_w", L3 + "ln1_b"), (L3 + "ln2_w", L3 + "ln2_b"), (L3 + "ln3_w", L3 + "ln3_b")]
    lnp = np.stack([np.stack([cols(g[a]), cols(g[b])]) for a, b in norms]).transpose(2, 0, 1, 3)
    bo = np.stack([g[n] for n in (L0 + "bo1", L0 + "bo2", L0 + "bf", L1 + "bo1", L1 + "bo2", L1 + "b_ff2", L2 + "bo",
                                  L3 + "proj_b", L3 + "out_b", L3 + "mlp2_b")])
    bff = np.concatenate([cols(g[L0 + "bp"]), cols(g[L1 + "b_ff1"]), cols(g[L3 + "mlp1_b"])], 1)
    qkv_b = g[L3 + "qkv_b"]
    bsm = np.stack([small2(qkv_b[:256]), small2(qkv_b[256:512]), small(qkv_b[512:]),
                    small2(g[L3 + "q_b"]), small2(g[L3 + "k_b"]), small(g[L3 + "v_b"])], 1)
    lo_rows = (np.arange(128) % 32 >= 16).astype(np.float32).reshape(128, 1)
    c = g["ctx_768"]
    c = np.concatenate([c, np.zeros((B, SP - S2, E), c.dtype)], 1).transpose(2, 0, 1)
    ctxT = np.stack([c[:128], np.concatenate([c[128:], c[128:]], 0)], 2)
    arrays = {
        "x_in": g["x"].transpose(1, 0, 2), "ctxT": ctxT, "wts": pack_weights(g), "lnp": lnp, "bo": bo, "bff": bff,
        "bsm": bsm, "lo_rows": lo_rows, "mask_s": words(g["mask_BxS_bf0"]), "mask_x": words(g["mask_BxS2_bf0"]),
    }
    arrays = {k: np.ascontiguousarray(v) for k, v in arrays.items()}
    nc = bacc.Bacc("TRN2", target_bir_lowering=False, num_devices=1, dynamic_dma_scratch_size=1024)
    aps = [nc.dram_tensor(k, v.shape, mybir.dt.from_np(v.dtype), kind="ExternalInput").ap() for k, v in arrays.items()]
    out = nc.dram_tensor("out", (T, B, C), mybir.dt.float32, kind="ExternalOutput").ap()
    program(nc, *aps, out)
    r = run_bass_kernel_spmd(nc, [arrays], core_ids=[0])
    return np.ascontiguousarray(r.results[0]["out"].transpose(1, 0, 2))
```
